# Optimizing a Trainium2 kernel written in Bass

```python
import numpy as np
import jax
import jax.numpy as jnp

def _softmax(x, axis=-1):
    return jax.nn.softmax(x, axis=axis)

def _gelu(x):
    return jax.nn.gelu(x, approximate=True)

def _silu(x):
    return jax.nn.silu(x)

def _sigmoid(x):
    return jax.nn.sigmoid(x)

def _layernorm(x, axis=-1, eps=1e-05):
    m = jnp.mean(x, axis=axis, keepdims=True)
    v = jnp.var(x, axis=axis, keepdims=True)
    return (x - m) / jnp.sqrt(v + eps)

def _scatter_add(tgt, idx, src, axis=0):
    return tgt.at[idx].add(src)

def _segment_sum(src, seg, n):
    return jax.ops.segment_sum(src, seg, n)
kernel_name = 'mk_gnn_resnorm_d2_gnn_r64_d554af'

def setup_inputs(seed: int=0):
    np.random.seed(seed)
    _w = jnp.asarray

    def _rec_inputs():
        import jax
        import jax.numpy as jnp
        _gk = jax.random.key(seed)
        x = 0.0003989 + 1 * jax.random.normal(jax.random.fold_in(_gk, 1), (50000, 128), jnp.float32)
        src = jax.random.randint(jax.random.fold_in(_gk, 2), (12500,), 0, 50000, jnp.int32)
        dst = jnp.minimum((50000 * jax.random.uniform(jax.random.fold_in(_gk, 3), (12500,)) ** 2.0).astype(jnp.int32), 49999)
        _o = jnp.argsort(dst, stable=True)
        src = src[_o]
        dst = dst[_o]
        edge_attr_2 = -1.09012e-05 + 0.99985 * jax.random.normal(jax.random.fold_in(_gk, 12), (12500, 2), jnp.float32)
        return (x, src, dst, edge_attr_2)
    x, src, dst, edge_attr_2 = _rec_inputs()

    def _L0_gnn_setup():
        import jax, jax.numpy as jnp
        import numpy as np
        N_NODES = 50000

        def _cheb_layer(h, src, dst, dinv, W, b):
            hn = h * dinv[:, None]
            agg = jax.ops.segment_sum(hn[src], dst, num_segments=N_NODES)
            x1 = -(agg * dinv[:, None])
            return jnp.concatenate([h, x1], axis=-1) @ W + b
        key = jax.random.key(seed)
        ks = jax.random.split(key, 8)
        E = 12500
        src = jax.random.randint(ks[0], (E,), 0, N_NODES, dtype=jnp.int32)
        dst = jax.random.randint(ks[1], (E,), 0, N_NODES, dtype=jnp.int32)

        def w(k, shape):
            fan_in = shape[0]
            return jax.random.normal(k, shape, jnp.float32) * (1.0 / np.sqrt(fan_in))
        return {'x': jax.random.normal(ks[2], (N_NODES, 128), jnp.float32), 'src': src, 'dst': dst, 'W1': w(ks[3], (256, 256)), 'b1': jnp.zeros((256,), jnp.float32), 'W2': w(ks[4], (512, 256)), 'b2': jnp.zeros((256,), jnp.float32), 'W3': w(ks[5], (512, 128)), 'b3': jnp.zeros((128,), jnp.float32)}
    _L0_gnn_all = _L0_gnn_setup()
    _L0_gnn_in = {k: v for k, v in _L0_gnn_all.items() if k in ('W1', 'b1', 'W2', 'b2', 'W3', 'b3')}
    del _L0_gnn_all

    def _L1_gnn_setup():
        import jax, jax.numpy as jnp
        import numpy as np
        N_NODES = 50000
        N_EDGES = 9375
        HID = 128
        N_LAYERS = 3
        NEG_SLOPE = 0.01
        key = jax.random.key(seed)
        ks = jax.random.split(key, 7)
        x = jax.random.normal(ks[0], (N_NODES, HID), dtype=jnp.float32)
        edge_index = jax.random.randint(ks[1], (2, N_EDGES), 0, N_NODES, dtype=jnp.int64)
        edge_attr = jax.random.normal(ks[2], (N_EDGES, 2), dtype=jnp.float32)
        Wl = jax.random.normal(ks[3], (N_LAYERS, 2, HID), dtype=jnp.float32) * 0.1
        bl = jax.random.normal(ks[4], (N_LAYERS, HID), dtype=jnp.float32) * 0.1
        W = jax.random.normal(ks[5], (N_LAYERS, HID, HID), dtype=jnp.float32) * (1.0 / np.sqrt(HID))
        b = jax.random.normal(ks[6], (N_LAYERS, HID), dtype=jnp.float32) * 0.1
        return {'x': x, 'edge_index': edge_index, 'edge_attr': edge_attr, 'Wl': Wl, 'bl': bl, 'W': W, 'b': b}
    _L1_gnn_all = _L1_gnn_setup()
    _L1_gnn_in = {k: v for k, v in _L1_gnn_all.items() if k in ('Wl', 'bl', 'W', 'b')}
    del _L1_gnn_all
    return {'x': x, 'src': src, 'dst': dst, 'edge_attr_2': edge_attr_2, 'L0_gnn_W1': _L0_gnn_in['W1'], 'L0_gnn_b1': _L0_gnn_in['b1'], 'L0_gnn_W2': _L0_gnn_in['W2'], 'L0_gnn_b2': _L0_gnn_in['b2'], 'L0_gnn_W3': _L0_gnn_in['W3'], 'L0_gnn_b3': _L0_gnn_in['b3'], 'L1_gnn_Wl': _L1_gnn_in['Wl'], 'L1_gnn_bl': _L1_gnn_in['bl'], 'L1_gnn_W': _L1_gnn_in['W'], 'L1_gnn_b': _L1_gnn_in['b']}

def reference(x, src, dst, edge_attr_2, L0_gnn_W1, L0_gnn_b1, L0_gnn_W2, L0_gnn_b2, L0_gnn_W3, L0_gnn_b3, L1_gnn_Wl, L1_gnn_bl, L1_gnn_W, L1_gnn_b):
    import jax
    import jax.numpy as jnp

    def _L0_gnn_ref(x, src, dst, W1, b1, W2, b2, W3, b3):
        import jax, jax.numpy as jnp
        import numpy as np
        N_NODES = 50000

        def _cheb_layer(h, src, dst, dinv, W, b):
            hn = h * dinv[:, None]
            agg = jax.ops.segment_sum(hn[src], dst, num_segments=N_NODES)
            x1 = -(agg * dinv[:, None])
            return jnp.concatenate([h, x1], axis=-1) @ W + b
        deg = jax.ops.segment_sum(jnp.ones_like(dst, dtype=x.dtype), dst, num_segments=N_NODES)
        dinv = jnp.where(deg > 0, jax.lax.rsqrt(jnp.maximum(deg, 1.0)), 0.0)
        h = jnp.tanh(_cheb_layer(x, src, dst, dinv, W1, b1))
        for _ in range(3):
            h = jnp.tanh(_cheb_layer(h, src, dst, dinv, W2, b2))
        return _cheb_layer(h, src, dst, dinv, W3, b3)

    def _L1_gnn_ref(x, edge_index, edge_attr, Wl, bl, W, b):
        import jax, jax.numpy as jnp
        import numpy as np
        N_NODES = 50000
        N_EDGES = 9375
        HID = 128
        N_LAYERS = 3
        NEG_SLOPE = 0.01
        src, dst = (edge_index[0], edge_index[1])
        n = x.shape[0]
        h = x
        for i in range(N_LAYERS):
            e = edge_attr @ Wl[i] + bl[i]
            msg = jax.nn.relu(h[src] + e)
            agg = jax.ops.segment_sum(msg, dst, num_segments=n)
            h = ((1.0 + 0.0) * h + agg) @ W[i] + b[i]
            h = jnp.where(h >= 0, h, NEG_SLOPE * h)
        return h
    edge_index = jnp.stack([src, dst])
    x = _layernorm(x + _L0_gnn_ref(x, src, dst, L0_gnn_W1, L0_gnn_b1, L0_gnn_W2, L0_gnn_b2, L0_gnn_W3, L0_gnn_b3), axis=-1)
    x = _layernorm(x + _L1_gnn_ref(x, edge_index, edge_attr_2, L1_gnn_Wl, L1_gnn_bl, L1_gnn_W, L1_gnn_b), axis=-1)
    return x

_drawn_inputs = setup_inputs


def setup_inputs(seed=0):
    import zlib

    import numpy as np

    out = dict(_drawn_inputs(seed))
    spreads = {'L0_gnn_b1': (0.0, 0.494), 'L0_gnn_b2': (0.0, 0.1), 'L0_gnn_b3': (0.0, 0.1)}
    factors = {}
    for name, (base, spread) in spreads.items():
        noise = np.random.default_rng([zlib.crc32(name.encode()), seed]).standard_normal(out[name].shape)
        drawn = base * np.exp(spread * noise) if base else spread * noise
        out[name] = jnp.asarray(drawn.astype(out[name].dtype))
    for name, factor in factors.items():
        out[name] = (out[name] * factor).astype(out[name].dtype)
    return out
```

```python
import concourse.bass as bass
from concourse import mybir
from contextlib import ExitStack

N = 50000
E = 12500
D = 128
H = 256
P = 128

DT, DR = 4, 128
DB = DT * DR
PAIRS = (N // DB + 1) // 2
TAIL_T, TAIL_R = 3, 112
ST, SR = 4, 112
SB = ST * SR
EP = -(-E // SB) * SB
BLOCKS = EP // SB
COLS = EP // SR
assert COLS == SR and BLOCKS % 2 == 0
assert (2 * PAIRS - 1) * DB + TAIL_T * TAIL_R == N

PAD_NODE = N + EP
TAB_ROWS = N + EP + 2
ZERO_ROW = EP
CHUNK = EP // 8
INIT_COLS = -(-TAB_ROWS // P)
EPS = 1e-5
SLOPE = 0.01
MAGIC = float(0x5F3759DF)
NEWTON = 3
RSQRT_LINKS = 2 + 3 * NEWTON
LN_LINKS = 3 + RSQRT_LINKS

L1, L2, L3, L4, L5, G1, G2, G3 = range(8)
PHASES = 8
HIDDEN = (L1, L2, L3, L4)
GIN = (G1, G2, G3)

AHEAD = {"tables": 1, "coefficients": 11, L1: 8, L2: 8, L3: 8, L4: 7, L5: 6}
assert sum(AHEAD.values()) == PAIRS


def gnn_kernel(nc, x, src, dst, attr_t, w1, b1, w2, b2, w3, b3, wl, bl, wg, bg, out):
    f32, bf16, i32 = mybir.dt.float32, mybir.dt.bfloat16, mybir.dt.int32
    ALU = mybir.AluOpType
    ACT = mybir.ActivationFunctionType

    ctx = ExitStack()
    with ctx:
        def sb(name, shape, dt=f32):
            return ctx.enter_context(nc.sbuf_tensor(name, shape, dt))

        def sem(name):
            return ctx.enter_context(nc.semaphore(name))

        def sems(name):
            return [sem(f"{name}{q}") for q in range(2)]

        def dram(name, shape, dt=f32):
            return nc.dram_tensor(name, shape, dt, kind="Internal").ap()

        def wait(eng, s, count):
            if not (isinstance(count, int) and count <= 0):
                eng.wait_ge(s, count)

        dst_x = dram("dst_x", (EP + 2,), i32)
        src_x = dram("src_x", (EP,), i32)
        attr_x = dram("attr_x", (3, EP))
        rank_x = dram("rank_x", (EP,))
        node_tab = dram("node_tab", (P * INIT_COLS, 2))
        h_tab = [dram(f"h_tab{i}", (EP + P, H)) for i in range(2)]
        g_tab = [dram(f"g_tab{i}", (N + EP, D)) for i in range(3)]
        state_x = dram("state_x", (BLOCKS, P, 2, SB))
        res_x = dram("res_x", (2, BLOCKS, P, SB))

        ident = sb("ident", [P, P])
        w1_s = sb("w1_s", [P, 2, H])
        w2_s = sb("w2_s", [P, 4, H])
        w3_s = sb("w3_s", [P, 4, D])
        wg_s = sb("wg_s", [P, 3, D])
        wl_s = sb("wl_s", [3, 3, D])
        b1_s = sb("b1_s", [P, 2])
        b2_s = sb("b2_s", [P, 2])
        b3_s = sb("b3_s", [P, 1])
        bg_s = sb("bg_s", [P, 3])
        ones = sb("ones", [1, CHUNK])
        zero_rows = sb("zero_rows", [P, H])

        keep = sb("keep", [P, EP], bf16)
        dst_chunk = sb("dst_chunk", [P, CHUNK + 1], i32)
        rank_row = sb("rank_row", [1, 2, CHUNK])
        init_i = sb("init_i", [P, 1], i32)
        init_f = sb("init_f", [P, 1])
        node_init = sb("node_init", [P, INIT_COLS, 2])
        rows_i = sb("rows_i", [SR, 3, COLS], i32)
        rows_f = sb("rows_f", [SR, 4, COLS])
        cols_f = sb("cols_f", [SR, 4, COLS])
        slot_i = sb("slot_i", [SR, COLS], i32)
        slot_f = sb("slot_f", [SR, COLS])
        tmp = sb("tmp", [SR, 4, COLS])
        scatter_idx = sb("scatter_idx", [SR, COLS], i32)
        scatter_val = sb("scatter_val", [SR, COLS, 2])
        dst_idx = sb("dst_idx", [SR, COLS], i32)
        x_dst_idx = sb("x_dst_idx", [SR, COLS], i32)
        src_idx = sb("src_idx", [SR, COLS], i32)
        of_dst = sb("of_dst", [SR, COLS, 2])
        of_src = sb("of_src", [SR, COLS, 2])
        coef = sb("coef", [SR, COLS])
        h_idx = sb("h_idx", [SR, COLS], i32)
        g_idx = sb("g_idx", [SR, COLS], i32)
        idx_now = [sb(f"idx_now{q}", [SR, 2 * ST], i32) for q in range(2)]
        carrier = sb("carrier", [1, 1])
        out_idx = [sb(f"out_idx{q}", [SR, ST], i32) for q in range(2)]
        tab_now = [sb(f"tab_now{q}", [SR, 2 * ST, 2]) for q in range(2)]
        rs_a = sb("rs_a", [P, COLS])
        rs_b = sb("rs_b", [P, COLS])

        x_rows = [sb(f"x_rows{q}", [P, DT, D]) for q in range(2)]
        x_t = [sb(f"x_t{q}", [P, DB]) for q in range(2)]
        h_t = [[sb(f"h_t{q}{v}", [P, 2, DB]) for v in range(2)] for q in range(2)]
        z_t = [sb(f"z_t{q}", [P, DB]) for q in range(2)]
        y_rows = [sb(f"y_rows{q}", [P, DT, D]) for q in range(2)]
        y_t = [sb(f"y_t{q}", [P, DB]) for q in range(2)]
        u_t = [sb(f"u_t{q}", [P, DB]) for q in range(2)]
        g_t = [[sb(f"g_t{q}{v}", [P, DB]) for v in range(2)] for q in range(2)]
        g_rows = [[sb(f"g_rows{g}{q}", [P, DT, D]) for q in range(2)] for g in range(2)]
        z2_t = [sb(f"z2_t{q}", [P, DB]) for q in range(2)]
        out_rows = [sb(f"out_rows{q}", [P, DT, D]) for q in range(2)]
        stats = sb("stats", [P, 2 * DT, 6])
        mean_var = sb("mean_var", [P, 2 * DT, 2])
        rstd = sb("rstd", [P, 2 * DT])
        ln_a = sb("ln_a", [P, 2 * DT])
        ln_b = sb("ln_b", [P, 2 * DT])

        got = [sb(f"got{q}", [SR, ST, H]) for q in range(2)]
        scaled = [sb(f"scaled{q}", [SR, ST, H]) for q in range(2)]
        state = [sb(f"state{q}", [P, 2, SB]) for q in range(2)]
        res = [sb(f"res{q}", [P, SB]) for q in range(2)]
        agg = [sb(f"agg{q}", [P, 2, SB]) for q in range(2)]
        new = [sb(f"new{q}", [P, 2, SB]) for q in range(2)]
        lin = [sb(f"lin{q}", [P, SB]) for q in range(2)]
        msg = [sb(f"msg{q}", [P, SB]) for q in range(2)]
        attr = [sb(f"attr{q}", [3, SB]) for q in range(2)]
        new_rows = [sb(f"new_rows{q}", [SR, ST, H]) for q in range(2)]

        mm = [[ctx.enter_context(nc.psum_tensor(f"mm{q}{i}", [P, 512], f32)) for i in range(2)]
              for q in range(2)]
        ga = [ctx.enter_context(nc.psum_tensor(f"ga{i}", [P, 512], f32)) for i in range(2)]
        tr = [ctx.enter_context(nc.psum_tensor(f"tr{i}", [P, 512], f32)) for i in range(2)]

        weights_in = sem("weights_in")
        scratch_in = sem("scratch_in")
        pads_set = sem("pads_set")
        pads_in = sem("pads_in")
        ident_zero, ident_set = sem("ident_zero"), sem("ident_set")
        chunk_in, keep_done = sem("chunk_in"), sem("keep_done")
        rank_done, rank_out = sem("rank_done"), [sem(f"rank_out{q}") for q in range(2)]
        init_set, init_out = sem("init_set"), sem("init_out")
        rows_in, rows_cast = sem("rows_in"), sem("rows_cast")
        cols_t, cols_done = sem("cols_t"), sem("cols_done")
        dve_link = sem("dve_link")
        slot_made, index_made = sem("slot_made"), sem("index_made")
        scattered, tab_got = sems("scattered"), sems("tab_got")
        staged, out_staged = sem("staged"), sem("out_staged")
        stats_set = sem("stats_set")
        tab_read = sem("tab_read")
        coef_made = sem("coef_made")
        pe_left, act_left, dve_left = sem("pe_left"), sem("act_left"), sem("dve_left")

        x_loaded = sems("x_loaded")
        x_turned, x_t_ready = sem("x_turned"), sem("x_t_ready")
        layer_mm, h_ready = sem("layer_mm"), sem("h_ready")
        y_mm, z_ready, z_turned, ln1_done = sem("y_mm"), sem("z_ready"), sem("z_turned"), sem("ln1_done")
        y_turned, y_t_ready = sem("y_turned"), sem("y_t_ready")
        g_mm, u_ready, g_ready = sem("g_mm"), sem("u_ready"), sem("g_ready")
        g_turned, g_rows_ready = sem("g_turned"), sem("g_rows_ready")
        z2_ready, z2_turned, ln2_done = sem("z2_ready"), sem("z2_turned"), sem("ln2_done")
        ln1_link, ln2_link, ln_slot_link = sem("ln1_link"), sem("ln2_link"), sem("ln_slot_link")
        y_stored, out_stored = sems("y_stored"), sems("out_stored")
        g_stored = [sems(f"g_stored{g}") for g in range(2)]

        got_in, own_in, attr_in = sems("got_in"), sems("own_in"), sems("attr_in")
        state_in, res_in = sems("state_in"), sems("res_in")
        scale_done, turned, copied, scanned = sem("scale_done"), sem("turned"), sem("copied"), sem("scanned")
        summed = sem("summed")
        mm_done, lin_done, new_half, new_ready = sem("mm_done"), sem("lin_done"), sem("new_half"), sem("new_ready")
        back_turned, rows_ready = sem("back_turned"), sem("rows_ready")
        state_out, res_out, rows_out, out_scattered = (
            sems("state_out"), sems("res_out"), sems("rows_out"), sems("out_scattered"))

        block = ctx.enter_context(nc.Block())

        PADS = 4 + 2 + EP // CHUNK + 2

        def dense_blocks(k):
            if isinstance(k, int) and k == PAIRS - 1:
                return [(0, DT, DR), (1, TAIL_T, TAIL_R)]
            return [(0, DT, DR), (1, DT, DR)]

        def dense_view(table, k, q, tiles, rows):
            if tiles == DT:
                whole = table[0:(2 * PAIRS - 1) * DB, :]
                return whole.rearrange("(b p j) f -> b p j f", p=DR, j=DT)[2 * k + q]
            return table[N - tiles * rows:N, :].rearrange("(p j) f -> p j f", p=rows)

        def dense_run(eng, first, n, body):
            steps = list(range(first, first + n))
            while steps and steps[0] < 2:
                body(steps.pop(0))
            late = [k for k in steps if k >= PAIRS - 2]
            steps = [k for k in steps if k < PAIRS - 2]
            if steps:
                with eng.Fori(steps[0], steps[-1] + 1) as k:
                    body(k)
            for k in late:
                body(k)

        class Step:

            def __init__(self, i, par):
                self.i, self.par = i, par

            def block(self, lag):
                par, half = (self.par - lag) % 2, self.i + (self.par - lag) // 2
                b = 2 * half + par
                if isinstance(b, int) and not 0 <= b < BLOCKS:
                    return None
                return b, par, half

        def phase_run(eng, body):
            for s in (-1, 0, 1):
                body(Step(s // 2, s % 2))
            with eng.Fori(1, BLOCKS // 2 - 1) as i:
                body(Step(i, 0))
                body(Step(i, 1))
            for s in range(BLOCKS - 2, BLOCKS + 2):
                body(Step(s // 2, s % 2))

        def dma_count(per_block, phase, half):
            before = sum(per_block.get(p, 0) for p in range(phase)) * (BLOCKS // 2)
            return 16 * (before + per_block[phase] * (half + 1))

        GOT = {p: 4 for p in range(PHASES)} | {L1: 8}
        ONCE_L1_G1 = {L1: 1, G1: 1}
        STATE = {L2: 1, L3: 1, L4: 1, L5: 1, G2: 1, G3: 1}
        STATE_OUT = {L1: 1, L2: 1, L3: 1, L4: 1, G1: 1, G2: 1}
        RES = {L5: 1, G3: 1}
        ROWS_OUT = {p: 1 for p in range(G3)}
        GIN_ONCE = {G1: 1, G2: 1, G3: 1}

        def schedule(dense, phase, part):
            k = 0
            for what, n in AHEAD.items():
                if n:
                    dense(k, n)
                    k += n
                part(what) if isinstance(what, str) else phase(what)
            dense(k, 1)
            for p in GIN:
                phase(p)

        class Turnstile:

            def __init__(self, eng, mine):
                self.eng, self.mine, self.n = eng, mine, 0

            def __call__(self):
                self.n += 1
                self.eng.drain().then_inc(self.mine, 1)
                for s in (pe_left, act_left, dve_left):
                    self.eng.wait_ge(s, self.n)

        @block.sync
        def _(sp):
            for tile, view in (
                (w1_s[:, :, :], w1.rearrange("(k p) n -> p k n", p=P)),
                (w2_s[:, :, :], w2.rearrange("(k p) n -> p k n", p=P)),
                (w3_s[:, :, :], w3.rearrange("(k p) n -> p k n", p=P)),
                (wg_s[:, :, :], wg.rearrange("l p n -> p l n")),
                (wl_s[0:2, :, :], wl.rearrange("l p n -> p l n")),
                (wl_s[2:3, :, :], bl.rearrange("(a l) n -> a l n", a=1)),
                (b1_s[:, :], b1.rearrange("(k p) -> p k", p=P)),
                (b2_s[:, :], b2.rearrange("(k p) -> p k", p=P)),
                (b3_s[:, :], b3.rearrange("(k p) -> p k", p=P)),
                (bg_s[:, :], bg.rearrange("l p -> p l")),
            ):
                with nc.allow_non_contiguous_dma(reason="a few hundred words of biases"):
                    sp.dma_start(tile, view).then_inc(weights_in, 16)
            row = lambda a: a.rearrange("(a n) -> a n", a=1)
            sp.dma_start(row(dst_x[1:1 + E]), row(dst)).then_inc(scratch_in, 16)
            sp.dma_start(row(src_x[0:E]), row(src)).then_inc(scratch_in, 16)
            sp.dma_start(attr_x[0:2, 0:E], attr_t).then_inc(scratch_in, 16)
            sp.wait_ge(pads_set, 4)
            pad = EP - E
            pad_i = slot_i
            sp.dma_start(row(dst_x[0:1]), pad_i[0:1, 0:1]).then_inc(pads_in, 16)
            sp.dma_start(row(dst_x[1 + E:1 + EP]), dst_chunk[0:1, 0:pad]).then_inc(pads_in, 16)
            sp.dma_start(row(dst_x[1 + EP:2 + EP]), pad_i[0:1, 0:1]).then_inc(pads_in, 16)
            sp.dma_start(row(src_x[E:EP]), src_idx[0:1, 0:pad]).then_inc(pads_in, 16)
            for r in range(2):
                sp.dma_start(attr_x[r:r + 1, E:EP], ones[0:1, 0:pad]).then_inc(pads_in, 16)
            for c in range(EP // CHUNK):
                sp.dma_start(attr_x[2:3, c * CHUNK:(c + 1) * CHUNK], ones[:, :]).then_inc(pads_in, 16)
            for t in h_tab:
                sp.dma_start(t[EP:EP + P, :], zero_rows[:, :]).then_inc(pads_in, 16)
            sp.wait_ge(scratch_in, 48)
            sp.wait_ge(pads_in, 16 * PADS)
            for c in range(EP // CHUNK):
                wait(sp, keep_done, c)
                sp.dma_start(dst_chunk[:, :],
                             row(dst_x[c * CHUNK:(c + 1) * CHUNK + 1]).to_broadcast([P, CHUNK + 1])
                             ).then_inc(chunk_in, 16)
                if c:
                    sp.wait_ge(rank_done, c)
                    sp.dma_start(row(rank_x[(c - 1) * CHUNK:c * CHUNK]),
                                 rank_row[:, (c - 1) % 2, :]).then_inc(rank_out[(c - 1) % 2], 16)
            c = EP // CHUNK
            sp.wait_ge(rank_done, c)
            sp.dma_start(row(rank_x[(c - 1) * CHUNK:c * CHUNK]),
                         rank_row[:, (c - 1) % 2, :]).then_inc(rank_out[(c - 1) % 2], 16)
            sp.wait_ge(init_set, 1)
            sp.dma_start(node_tab[0:P * INIT_COLS, :].rearrange("(p c) w -> p c w", p=P),
                         node_init[:, :, :]).then_inc(init_out, 16)
            square = lambda a: a.rearrange("(t p) -> t p", p=SR)
            sp.dma_start(rows_i[:, 0, :], square(dst_x[1:1 + EP])).then_inc(rows_in, 16)
            sp.dma_start(rows_i[:, 1, :], square(dst_x[2:2 + EP])).then_inc(rows_in, 16)
            sp.dma_start(rows_i[:, 2, :], square(src_x[0:EP])).then_inc(rows_in, 16)
            for q in range(2):
                sp.wait_ge(rank_out[q], 16 * c // 2)
            sp.dma_start(rows_f[:, 3, :], square(rank_x[0:EP])).then_inc(rows_in, 16)

            def load_x(k):
                for q, tiles, rows in dense_blocks(k):
                    wait(sp, x_turned, 2 * k + q - 1)
                    sp.dma_start(x_rows[q][:rows, :tiles, :],
                                 dense_view(x, k, q, tiles, rows)).then_inc(x_loaded[q], 16)

            def dense(first, n):
                def body(k):
                    if isinstance(k, int) and k == 0:
                        load_x(0)
                        load_x(1)
                        return
                    if not isinstance(k, int) or k < PAIRS - 1:
                        load_x(k + 1)
                    p = k - 1
                    for q, tiles, rows in dense_blocks(p):
                        sp.wait_ge(ln1_done, 2 * p + q + 1)
                        sp.dma_start(dense_view(g_tab[0], p, q, tiles, rows),
                                     y_rows[q][:rows, :tiles, :]).then_inc(y_stored[q], 16)
                    for g in range(2):
                        for q, tiles, rows in dense_blocks(p):
                            sp.wait_ge(g_rows_ready, 4 * p + 2 * g + q + 1)
                            sp.dma_start(dense_view(g_tab[1 + g], p, q, tiles, rows),
                                         g_rows[g][q][:rows, :tiles, :]).then_inc(g_stored[g][q], 16)
                    for q, tiles, rows in dense_blocks(p):
                        sp.wait_ge(ln2_done, 2 * p + q + 1)
                        sp.dma_start(dense_view(out, p, q, tiles, rows),
                                     out_rows[q][:rows, :tiles, :]).then_inc(out_stored[q], 16)
                dense_run(sp, first, n, body)

            def phase(ph):
                n0 = ph * BLOCKS

                def rows_of(b, table, base, width):
                    whole = table[base:base + EP, :].rearrange("(b j p) f -> b p j f", j=ST, p=SR)
                    return whole[b]

                def body(s):
                    if at := s.block(-1):
                        b, q, half = at
                        n = n0 + b
                        if ph == G1 and isinstance(b, int) and b < 2:
                            for r in range(2):
                                sp.wait_ge(rows_out[r], dma_count(ROWS_OUT, L5, BLOCKS // 2 - 1))
                        if ph in GIN:
                            wait(sp, turned, n - 1)
                            sp.dma_start(attr[q][:, :], attr_x[:, :].rearrange(
                                "r (b c) -> b r c", c=SB)[b]).then_inc(attr_in[q], 16)
                        if ph == G1:
                            sp.dma_start(scaled[q][:, :, 0:D],
                                         rows_of(b, g_tab[0], N, D)).then_inc(own_in[q], 16)
                        if ph in STATE:
                            if isinstance(b, int) and b < 2:
                                prev = max(p for p in STATE_OUT if p < ph)
                                sp.wait_ge(state_out[q], dma_count(STATE_OUT, prev, BLOCKS // 2 - 1))
                            wait(sp, mm_done, n - 1)
                            parts = 1 if ph in GIN else 2
                            sp.dma_start(state[q][:, 0:parts, :],
                                         state_x[b, :, 0:parts, :]).then_inc(state_in[q], 16)
                        if ph in RES:
                            if isinstance(b, int) and b < 2:
                                sp.wait_ge(res_out[q], dma_count(ONCE_L1_G1, L1 if ph == L5 else G1,
                                                                 BLOCKS // 2 - 1))
                            wait(sp, new_ready, n - 1)
                            sp.dma_start(res[q][:, :], res_x[ph == G3, b]).then_inc(res_in[q], 16)
                    if at := s.block(1):
                        b, q, half = at
                        if ph in ONCE_L1_G1:
                            sp.wait_ge(copied, ((ph == G1) * BLOCKS) + b + 1)
                            sp.dma_start(res_x[ph == G1, b], res[q][:, :]).then_inc(res_out[q], 16)
                        if ph in STATE_OUT:
                            parts = 1 if ph in GIN else 2
                            sp.wait_ge(new_ready, n0 + b + 1)
                            sp.dma_start(state_x[b, :, 0:parts, :],
                                         new[q][:, 0:parts, :]).then_inc(state_out[q], 16)
                    if at := s.block(2):
                        b, q, half = at
                        if ph in ROWS_OUT:
                            sp.wait_ge(rows_ready, n0 + b + 1)
                            if ph in HIDDEN:
                                to = rows_of(b, h_tab[ph % 2], 0, H)
                                sp.dma_start(to, new_rows[q][:, :, :]).then_inc(rows_out[q], 16)
                            else:
                                to = rows_of(b, g_tab[ph - L5], N, D)
                                sp.dma_start(to, new_rows[q][:, :, 0:D]).then_inc(rows_out[q], 16)
                phase_run(sp, body)

            schedule(dense, phase, lambda what: None)
            for q in range(2):
                sp.wait_ge(out_scattered[q], 16 * 4 * BLOCKS // 2)
                sp.wait_ge(out_stored[q], 16 * PAIRS)

        @block.gpsimd
        def _(pool):
            pool.memset(ident[:, :], 0.0).then_inc(ident_zero, 1)
            pool.wait_ge(ident_zero, 1)
            pool.affine_select(out=ident[:, :], in_=ident[:, :], compare_op=ALU.not_equal, fill=1.0,
                               base=0, pattern=[[-1, P]], channel_multiplier=1).then_inc(ident_set, 1)
            pool.memset(slot_i[:, :], -1).then_inc(pads_set, 1)
            pool.memset(dst_chunk[:, :], PAD_NODE).then_inc(pads_set, 1)
            pool.memset(src_idx[:, :], 0).then_inc(pads_set, 1)
            pool.memset(zero_rows[:, :], 0.0)
            pool.memset(carrier[:, :], 0.0)
            pool.memset(ones[:, :], 1.0).then_inc(pads_set, 1)
            pool.iota(init_i[:, :], pattern=[[0, 1]], base=ZERO_ROW, channel_multiplier=1
                      ).then_inc(slot_made, 1)
            pool.wait_ge(pads_in, 16 * PADS)
            pool.iota(slot_i[:, :], pattern=[[SR, COLS]], base=0, channel_multiplier=1
                      ).then_inc(slot_made, 1)

            def gather(to, table, index, done):
                pool.indirect_dma_start(out=to, out_offset=None, in_=table,
                                        in_offset=bass.IndirectOffsetOnAxis(ap=index, axis=0)
                                        ).then_inc(done, 16)

            def scatter(table, index, of, done):
                pool.indirect_dma_start(out=table, in_=of, in_offset=None,
                                        out_offset=bass.IndirectOffsetOnAxis(ap=index, axis=0)
                                        ).then_inc(done, 16)

            def settled(done, count):
                pool.wait_ge(done, count)
                if not isinstance(count, int):
                    pool.tensor_tensor(out=carrier[:, :], in0=carrier[:, :], in1=carrier[:, :], op=ALU.add)

            def part(what):
                if what == "tables":
                    pool.wait_ge(index_made, 1)
                    pool.wait_ge(init_out, 16)
                    def put(i):
                        for q in range(2):
                            b = 2 * i + q
                            wait(pool, scattered[q], 16 * ST * i)
                            pool.tensor_copy(idx_now[q][:, 0:ST], scatter_idx[:, bass.ds(ST * b, ST)])
                            pool.tensor_copy(tab_now[q][:, 0:ST, :], scatter_val[:, bass.ds(ST * b, ST), :]
                                             ).then_inc(staged, 1)
                            pool.wait_ge(init_out, 16)
                            settled(staged, b + 1)
                            for j in range(ST):
                                scatter(node_tab, idx_now[q][:, j:j + 1], tab_now[q][:, j, :], scattered[q])
                    put(0)
                    with pool.Fori(1, BLOCKS // 2) as i:
                        put(i)
                    for q in range(2):
                        pool.wait_ge(scattered[q], 16 * ST * BLOCKS // 2)

                    def read(q, b):
                        pool.tensor_copy(of_dst[:, bass.ds(ST * b, ST), :], tab_now[q][:, 0:ST, :])
                        return pool.tensor_copy(of_src[:, bass.ds(ST * b, ST), :], tab_now[q][:, ST:2 * ST, :])

                    def get(i):
                        for q in range(2):
                            b = 2 * i + q
                            if not isinstance(i, int):
                                pool.wait_ge(tab_got[q], 16 * 2 * ST * i)
                                read(q, b - 2)
                            pool.tensor_copy(idx_now[q][:, 0:ST], dst_idx[:, bass.ds(ST * b, ST)])
                            pool.tensor_copy(idx_now[q][:, ST:2 * ST], src_idx[:, bass.ds(ST * b, ST)]
                                             ).then_inc(staged, 1)
                            pool.wait_ge(scattered[q], 16 * ST * BLOCKS // 2)
                            settled(staged, BLOCKS + b + 1)
                            for j in range(2 * ST):
                                gather(tab_now[q][:, j, :], node_tab, idx_now[q][:, j:j + 1], tab_got[q])
                    get(0)
                    with pool.Fori(1, BLOCKS // 2) as i:
                        get(i)
                    for q in range(2):
                        pool.wait_ge(tab_got[q], 16 * 2 * ST * BLOCKS // 2)
                        read(q, BLOCKS - 2 + q).then_inc(tab_read, 1)

            def phase(ph):
                n0 = ph * BLOCKS
                table = x if ph == L1 else h_tab[(ph - 1) % 2] if ph <= L5 else g_tab[ph - G1]
                index = src_idx if ph == L1 else h_idx if ph <= L5 else g_idx
                width = D if ph == L1 or ph in GIN else H
                if ph == L2:
                    pool.wait_ge(coef_made, 1)
                if ph > L1:
                    for q in range(2):
                        pool.wait_ge(rows_out[q], dma_count(ROWS_OUT, ph - 1, BLOCKS // 2 - 1))
                if ph in GIN:
                    for q in range(2):
                        pool.wait_ge((y_stored, g_stored[0], g_stored[1])[ph - G1][q], 16 * PAIRS)
                if ph == G3:
                    for q in range(2):
                        pool.wait_ge(out_stored[q], 16 * PAIRS)

                def body(s):
                    if at := s.block(-1):
                        b, q, half = at
                        if ph in GIN:
                            wait(pool, turned, n0 + b - 1)
                            if ph == G1 and isinstance(b, int) and b < 2:
                                pool.wait_ge(scale_done, G1 * BLOCKS)
                        else:
                            wait(pool, scale_done, n0 + b - 1)
                        if ph == L1:
                            pool.tensor_copy(idx_now[q][:, ST:2 * ST], x_dst_idx[:, bass.ds(ST * b, ST)])
                        pool.tensor_copy(idx_now[q][:, 0:ST], index[:, bass.ds(ST * b, ST)]).then_inc(staged, 1)
                        settled(staged, 2 * BLOCKS + n0 + b + 1)
                        for j in range(ST):
                            gather(got[q][:, j, 0:width], table, idx_now[q][:, j:j + 1], got_in[q])
                        if ph == L1:
                            for j in range(ST):
                                gather(got[q][:, j, D:2 * D], x, idx_now[q][:, ST + j:ST + j + 1], got_in[q])
                    if ph == G3 and (at := s.block(2)):
                        b, q, half = at
                        pool.wait_ge(rows_ready, n0 + b + 1)
                        wait(pool, out_scattered[q], 16 * ST * half)
                        pool.tensor_copy(out_idx[q][:, :], scatter_idx[:, bass.ds(ST * b, ST)]).then_inc(out_staged, 1)
                        pool.wait_ge(out_stored[q], 16 * PAIRS)
                        settled(out_staged, b + 1)
                        for j in range(ST):
                            scatter(out, out_idx[q][:, j:j + 1], new_rows[q][:, j, 0:D], out_scattered[q])
                phase_run(pool, body)

            schedule(lambda k, n: None, phase, part)

        @block.tensor
        def _(pe):
            leave = Turnstile(pe, pe_left)
            pe.wait_ge(ident_set, 1)
            pe.wait_ge(weights_in, 160)
            pe.wait_ge(rows_cast, 1)
            for i in range(4):
                last = pe.transpose(tr[0][:SR, i * COLS:(i + 1) * COLS], rows_f[:, i, :], ident[:SR, :SR])
            last.then_inc(cols_t, 1)

            def turn(to, of, tiles, rows):
                for j in range(tiles):
                    last = pe.transpose(to[:, j * rows:(j + 1) * rows], of[:rows, j, :], ident[:rows, :rows])
                return last

            def turn_back(to, of, tiles, rows):
                for j in range(tiles):
                    last = pe.transpose(to[:rows, j * D:(j + 1) * D], of[:, j * rows:(j + 1) * rows], ident[:, :])
                return last

            def product(to, weights, moving, cols):
                for i, (w, m) in enumerate(zip(weights, moving)):
                    last = pe.matmul(to[:, 0:cols], w, m, start=i == 0, stop=i == len(weights) - 1)
                return last

            def dense(first, n):
                def body(k):
                    run = not isinstance(k, int) or k < PAIRS
                    fol = not isinstance(k, int) or k > 0
                    mine = dense_blocks(k) if run else []
                    p = k - 1
                    prev = dense_blocks(p) if fol else []

                    def layer(l):
                        for q, tiles, rows in mine:
                            c = tiles * rows
                            if l == 0:
                                pe.wait_ge(x_t_ready, 2 * k + q + 1)
                                weights, moving = lambda f: [w1_s[:, 0, f]], [x_t[q][:, 0:c]]
                            else:
                                pe.wait_ge(h_ready, 8 * k + 2 * (l - 1) + q + 1)
                                of = h_t[q][(l - 1) % 2]
                                moving = [of[:, i, 0:c] for i in range(2)]
                                weights = (lambda f: [w2_s[:, i, f] for i in range(2)]) if l < 4 else (
                                    lambda f: [w3_s[:, i, f] for i in range(2)])
                            for i in range(2 if l < 4 else 1):
                                last = product(mm[q][i], weights(slice(i * P, (i + 1) * P)), moving, c)
                            last.then_inc(layer_mm if l < 4 else y_mm, 1)

                    for q, tiles, rows in mine:
                        pe.wait_ge(x_loaded[q], 16 * (k + 1))
                        wait(pe, h_ready, 8 * k - 1 + q)
                        turn(mm[q][1], x_rows[q], tiles, rows).then_inc(x_turned, 1)
                    layer(0)
                    for q, tiles, rows in prev:
                        pe.wait_ge(ln1_done, 2 * p + q + 1)
                        turn(ga[q], y_rows[q], tiles, rows).then_inc(y_turned, 1)
                    layer(1)

                    def gin(g):
                        for q, tiles, rows in prev:
                            c = tiles * rows
                            if g == 0:
                                pe.wait_ge(y_t_ready, 2 * p + q + 1)
                                moving = y_t[q][:, 0:c]
                            else:
                                pe.wait_ge(g_ready, 6 * p + 2 * (g - 1) + q + 1)
                                moving = g_t[q][(g - 1) % 2][:, 0:c]
                            product(ga[q], [wg_s[:, g, :]], [moving], c).then_inc(g_mm, 1)

                    def gin_rows(g):
                        for q, tiles, rows in prev:
                            pe.wait_ge(g_ready, 6 * p + 2 * g + q + 1)
                            if g == 0:
                                wait(pe, ln2_done, 2 * p - 1 + q)
                            else:
                                pe.wait_ge(g_rows_ready, 4 * p + 2 * (g - 1) + q + 1)
                            turn_back(tr[q], g_t[q][g % 2], tiles, rows).then_inc(g_turned, 1)

                    gin(0)
                    layer(2)
                    gin(1)
                    gin_rows(0)
                    layer(3)
                    gin(2)
                    gin_rows(1)
                    layer(4)
                    for q, tiles, rows in prev:
                        pe.wait_ge(z2_ready, 2 * p + q + 1)
                        pe.wait_ge(g_rows_ready, 4 * p + 2 + q + 1)
                        turn_back(tr[q], z2_t[q], tiles, rows).then_inc(z2_turned, 1)
                    for q, tiles, rows in mine:
                        pe.wait_ge(z_ready, 2 * k + q + 1)
                        wait(pe, u_ready, 6 * k - 1 + q)
                        turn_back(ga[q], z_t[q], tiles, rows).then_inc(z_turned, 1)
                leave()
                dense_run(pe, first, n, body)

            def phase(ph):
                n0 = ph * BLOCKS

                def body(s):
                    if at := s.block(0):
                        b, q, half = at
                        n = n0 + b
                        wait(pe, scanned, n)
                        if ph in GIN:
                            pe.wait_ge(attr_in[q], dma_count(GIN_ONCE, ph, half))
                            pe.wait_ge(got_in[q], dma_count(GOT, ph, half))
                            if ph == G1:
                                pe.wait_ge(own_in[q], 16 * (half + 1))
                                wait(pe, copied, BLOCKS + b)
                                turn(ga[1], scaled[q][:, :, 0:D], ST, SR)
                            pe.matmul(ga[0][:, 0:SB], wl_s[:, ph - G1, :], attr[q][:, :], start=True, stop=False)
                            for j in range(ST):
                                last = pe.matmul(ga[0][:, j * SR:(j + 1) * SR], got[q][:, j, 0:D],
                                                 ident[:SR, :SR], start=False, stop=j == ST - 1)
                        else:
                            pe.wait_ge(scale_done, n + 1)
                            if ph == L1:
                                wait(pe, copied, b)
                            for i in range(2):
                                last = turn(ga[i], scaled[q][:, :, i * D:(i + 1) * D], ST, SR)
                        last.then_inc(turned, 1)
                    if at := s.block(1):
                        b, q, half = at
                        n = n0 + b
                        wait(pe, new_ready, n - 1)
                        if ph in GIN:
                            pe.wait_ge(summed, n - G1 * BLOCKS + 1)
                            last = product(mm[q][0], [wg_s[:, ph - G1, :]], [agg[q][:, 1, :]], SB)
                        else:
                            pe.wait_ge(scanned, n + 1)
                            if ph == L1:
                                pe.wait_ge(copied, b + 1)
                                moving, w, k = [res[q][:, :], agg[q][:, 0, :]], w1_s, 2
                            else:
                                pe.wait_ge(state_in[q], dma_count(STATE, ph, half))
                                moving = [state[q][:, 0, :], state[q][:, 1, :], agg[q][:, 0, :], agg[q][:, 1, :]]
                                w, k = (w3_s if ph == L5 else w2_s), 4
                            for i in range(1 if ph == L5 else 2):
                                last = product(mm[q][i], [w[:, r, i * P:(i + 1) * P] for r in range(k)], moving, SB)
                        last.then_inc(mm_done, 1)
                    if at := s.block(2):
                        b, q, half = at
                        n = n0 + b
                        pe.wait_ge(new_ready, n + 1)
                        wait(pe, rows_ready, n)
                        if ph in HIDDEN:
                            turn_back(tr[0], new[q][:, 0, :], ST, SR)
                            last = turn_back(tr[1], new[q][:, 1, :], ST, SR)
                        else:
                            last = turn_back(tr[0], new[q][:, ph == G3, :], ST, SR)
                        last.then_inc(back_turned, 1)
                leave()
                phase_run(pe, body)

            schedule(dense, phase, lambda what: leave())

        @block.scalar
        def _(act):
            leave = Turnstile(act, act_left)
            act.wait_ge(weights_in, 160)

            def dense(first, n):
                def body(k):
                    run = not isinstance(k, int) or k < PAIRS
                    fol = not isinstance(k, int) or k > 0
                    mine = dense_blocks(k) if run else []
                    p = k - 1
                    prev = dense_blocks(p) if fol else []

                    def tanh(l):
                        for q, tiles, rows in mine:
                            c = tiles * rows
                            act.wait_ge(layer_mm, 8 * k + 2 * l + q + 1)
                            for i in range(2):
                                last = act.activation(h_t[q][l % 2][:, i, 0:c], mm[q][i][:, 0:c], ACT.Tanh,
                                                      bias=(b2_s if l else b1_s)[:, i:i + 1])
                            last.then_inc(h_ready, 1)

                    def linear(g):
                        for q, tiles, rows in prev:
                            c = tiles * rows
                            act.wait_ge(g_mm, 6 * p + 2 * g + q + 1)
                            act.activation(u_t[q][:, 0:c], ga[q][:, 0:c], ACT.Identity,
                                           bias=bg_s[:, g:g + 1]).then_inc(u_ready, 1)

                    def rows_copy(g):
                        for q, tiles, rows in prev:
                            act.wait_ge(g_turned, 4 * p + 2 * g + q + 1)
                            wait(act, g_stored[g][q], 16 * p)
                            act.activation(g_rows[g][q][:rows, :tiles, :].rearrange("p j f -> p (j f)"),
                                           tr[q][:rows, 0:tiles * D], ACT.Copy).then_inc(g_rows_ready, 1)

                    for q, tiles, rows in mine:
                        act.wait_ge(x_turned, 2 * k + q + 1)
                        wait(act, z_ready, 2 * k - 1 + q)
                        act.activation(x_t[q][:, 0:tiles * rows], mm[q][1][:, 0:tiles * rows],
                                       ACT.Copy).then_inc(x_t_ready, 1)
                    tanh(0)
                    for q, tiles, rows in prev:
                        act.wait_ge(y_turned, 2 * p + q + 1)
                        act.activation(y_t[q][:, 0:tiles * rows], ga[q][:, 0:tiles * rows],
                                       ACT.Copy).then_inc(y_t_ready, 1)
                    tanh(1)
                    linear(0)
                    tanh(2)
                    linear(1)
                    rows_copy(0)
                    tanh(3)
                    linear(2)
                    rows_copy(1)
                leave()
                dense_run(act, first, n, body)

            def phase(ph):
                n0 = ph * BLOCKS

                def body(s):
                    if ph in (L1, G1) and (at := s.block(0)):
                        b, q, half = at
                        act.wait_ge(turned, n0 + b + 1)
                        wait(act, res_out[q], dma_count(ONCE_L1_G1, ph, half - 1))
                        wait(act, mm_done, n0 + b - 1)
                        if ph == G1:
                            wait(act, summed, b - 1)
                        act.activation(res[q][:, :], ga[1][:, 0:SB], ACT.Copy).then_inc(copied, 1)
                    if ph not in GIN and (at := s.block(-1)):
                        b, q, half = at
                        n = n0 + b
                        act.wait_ge(got_in[q], dma_count(GOT, ph, half))
                        wait(act, turned, n - 1)
                        for j in range(ST):
                            w = D if ph == L1 else H
                            last = act.activation(scaled[q][:, j, 0:w], got[q][:, j, 0:w], ACT.Copy,
                                                  scale=coef[:, bass.ds(ST * b + j, 1)])
                        if ph == L1:
                            last = act.activation(scaled[q][:, :, D:2 * D], got[q][:, :, D:2 * D], ACT.Copy)
                        last.then_inc(scale_done, 1)
                    if ph in GIN and (at := s.block(0)):
                        b, q, half = at
                        act.wait_ge(turned, n0 + b + 1)
                        wait(act, scanned, n0 + b - 1)
                        act.activation(msg[q][:, :], ga[0][:, 0:SB], ACT.Relu).then_inc(scale_done, 1)
                    if at := s.block(1):
                        b, q, half = at
                        n = n0 + b
                        if ph in HIDDEN:
                            act.wait_ge(mm_done, n + 1)
                            wait(act, back_turned, n - 1)
                            if not (ph == L1 and isinstance(b, int) and b < 2):
                                count = (dma_count(STATE_OUT, ph, half - 1))
                                act.wait_ge(state_out[q], count)
                            for i in range(2):
                                last = act.activation(new[q][:, i, :], mm[q][i][:, 0:SB], ACT.Tanh,
                                                      bias=(b1_s if ph == L1 else b2_s)[:, i:i + 1])
                            last.then_inc(new_ready, 1)
                        elif ph in GIN:
                            act.wait_ge(mm_done, n + 1)
                            wait(act, new_ready, n - 1)
                            act.activation(lin[q][:, :], mm[q][0][:, 0:SB], ACT.Identity,
                                           bias=bg_s[:, ph - G1:ph - G1 + 1]).then_inc(lin_done, 1)
                if ph == L1:
                    act.wait_ge(coef_made, 1)
                leave()
                phase_run(act, body)

            schedule(dense, phase, lambda what: leave())

        @block.vector
        def _(dve):
            leave = Turnstile(dve, dve_left)
            links = [0]

            def link(instruction):
                links[0] += 1
                instruction.then_inc(dve_link, 1)
                dve.wait_ge(dve_link, links[0])

            def rsqrt(y, v, a, b, done):
                done(dve.tensor_scalar(a.bitcast(i32), v.bitcast(i32), 1, None, ALU.logical_shift_right))
                done(dve.tensor_scalar(y.bitcast(i32), a.bitcast(i32), -1.0, MAGIC, ALU.mult, ALU.add))
                for _ in range(NEWTON):
                    done(dve.scalar_tensor_tensor(out=a, in0=y, scalar=-0.5, in1=y, op0=ALU.mult, op1=ALU.mult))
                    done(dve.tensor_tensor(out=b, in0=a, in1=v, op=ALU.mult))
                    done(dve.scalar_tensor_tensor(out=y, in0=b, scalar=1.5, in1=y, op0=ALU.add, op1=ALU.mult))

            def layer_norm(blocks, link_sem, index, done_sem, arrived, free):
                count = [index * LN_LINKS]

                def done(instruction):
                    count[0] = count[0] + 1
                    instruction.then_inc(link_sem, 1)
                    dve.wait_ge(link_sem, count[0])

                for q, tiles, rows, bank, to in blocks:
                    arrived(q)
                    for j in range(tiles):
                        last = dve.bn_stats(stats[:rows, q * DT + j, :], bank[:rows, j * D:(j + 1) * D])
                done(last)
                dve.memset(ln_b[:, :], 0.0)
                for q, tiles, rows, bank, to in blocks:
                    for j in range(tiles):
                        last = dve.bn_aggr(mean_var[:rows, q * DT + j, :], stats[:rows, q * DT + j, :])
                done(last)
                w = max(q * DT + tiles for q, tiles, *_ in blocks)
                r = max(rows for _, _, rows, *_ in blocks)
                done(dve.tensor_scalar(rs_a[:r, 0:w], mean_var[:r, 0:w, 1], EPS, None, ALU.add))
                rsqrt(rstd[:r, 0:w], rs_a[:r, 0:w], ln_a[:r, 0:w], ln_b[:r, 0:w], done)
                for q, tiles, rows, bank, to in blocks:
                    free(q)
                    for j in range(tiles):
                        c = q * DT + j
                        last = dve.tensor_scalar(to[:rows, j, 0:D], bank[:rows, j * D:(j + 1) * D],
                                                 mean_var[:rows, c, 0:1], rstd[:rows, c:c + 1],
                                                 ALU.subtract, ALU.mult)
                    last.then_inc(done_sem, 1)

            for t in agg:
                dve.memset(t[:, :, :], 0.0)
            dve.memset(stats[:, :, :], 1.0)
            dve.memset(mean_var[:, :, :], 1.0).then_inc(stats_set, 1)
            dve.wait_ge(pads_set, 4)
            for c in range(EP // CHUNK):
                dve.wait_ge(chunk_in, 16 * (c + 1))
                at = slice(c * CHUNK, (c + 1) * CHUNK)
                dve.tensor_tensor(out=keep[:, at], in0=dst_chunk[:, 1:CHUNK + 1], in1=dst_chunk[:, 0:CHUNK],
                                  op=ALU.is_equal).then_inc(keep_done, 1)
                dve.wait_ge(keep_done, c + 1)
                if c >= 2:
                    dve.wait_ge(rank_out[c % 2], 16 * (c // 2))
                if c:
                    dve.wait_ge(rank_done, c)
                before = rank_row[:, (c - 1) % 2, CHUNK - 1:CHUNK] if c else 0.0
                dve.tensor_tensor_scan(rank_row[:, c % 2, :], keep[0:1, at], ones[:, :], before,
                                       ALU.mult, ALU.add).then_inc(rank_done, 1)
            dve.wait_ge(slot_made, 2)
            dve.tensor_copy(init_f[:, :], init_i[:, :]).then_inc(dve_link, 1)
            links[0] += 1
            dve.memset(node_init[:, :, 1], 0.0)
            dve.wait_ge(dve_link, links[0])
            dve.tensor_copy(node_init[:, :, 0], init_f[:, 0:1].to_broadcast([P, INIT_COLS])).then_inc(init_set, 1)
            dve.wait_ge(rows_in, 64)
            dve.tensor_copy(rows_f[:, 0:3, :], rows_i[:, :, :]).then_inc(rows_cast, 1)
            dve.wait_ge(cols_t, 1)
            link(dve.tensor_copy(cols_f[:, :, :].rearrange("p a b -> p (a b)"), tr[0][:SR, 0:4 * COLS]))
            dst_c, next_c, src_c, rank_c = (cols_f[:, i, :] for i in range(4))
            link(dve.tensor_copy(slot_f[:, :], slot_i[:, :]))
            dve.tensor_scalar(tmp[:, 0, :], slot_f[:, :], float(N), None, ALU.add)
            link(dve.tensor_tensor(out=tmp[:, 1, :], in0=next_c, in1=dst_c, op=ALU.not_equal))
            link(dve.tensor_tensor(out=tmp[:, 2, :], in0=dst_c, in1=tmp[:, 0, :], op=ALU.subtract))
            link(dve.tensor_tensor(out=tmp[:, 2, :], in0=tmp[:, 2, :], in1=tmp[:, 1, :], op=ALU.mult))
            dve.tensor_tensor(out=scatter_idx[:, :], in0=tmp[:, 2, :], in1=tmp[:, 0, :], op=ALU.add)
            dve.tensor_copy(scatter_val[:, :, 0], slot_f[:, :])
            dve.tensor_copy(scatter_val[:, :, 1], rank_c)
            dve.tensor_copy(dst_idx[:, :], dst_c)
            dve.tensor_scalar(x_dst_idx[:, :], dst_c, float(N - 1), None, ALU.min)
            dve.wait_ge(pads_in, 16 * PADS)
            dve.tensor_copy(src_idx[:, :], src_c).then_inc(index_made, 1)

            def part(what):
                if what == "coefficients":
                    dve.wait_ge(tab_read, 2)
                    slot_s, deg_s, deg_d = of_src[:, :, 0], of_src[:, :, 1], of_dst[:, :, 1]
                    dve.tensor_copy(h_idx[:, :], slot_s)
                    dve.tensor_scalar(tmp[:, 1, :], deg_s, 0.0, None, ALU.is_gt)
                    link(dve.tensor_scalar(tmp[:, 0, :], deg_s, 1.0, None, ALU.max))
                    link(dve.scalar_tensor_tensor(out=tmp[:, 0, :], in0=deg_d, scalar=1.0, in1=tmp[:, 0, :],
                                                  op0=ALU.max, op1=ALU.mult))
                    rsqrt(tmp[:, 2, :], tmp[:, 0, :], rs_a[:SR, :], rs_b[:SR, :], link)
                    dve.scalar_tensor_tensor(out=coef[:, :], in0=tmp[:, 2, :], scalar=-1.0, in1=tmp[:, 1, :],
                                             op0=ALU.mult, op1=ALU.mult)
                    link(dve.scalar_tensor_tensor(out=tmp[:, 3, :], in0=slot_s, scalar=float(N), in1=src_c,
                                                  op0=ALU.add, op1=ALU.subtract))
                    link(dve.tensor_tensor(out=tmp[:, 3, :], in0=tmp[:, 3, :], in1=tmp[:, 1, :], op=ALU.mult))
                    dve.tensor_tensor(out=g_idx[:, :], in0=tmp[:, 3, :], in1=src_c, op=ALU.add).then_inc(coef_made, 1)
                leave()

            def dense(first, n):
                def body(k):
                    run = not isinstance(k, int) or k < PAIRS
                    fol = not isinstance(k, int) or k > 0
                    mine = dense_blocks(k) if run else []
                    p = k - 1
                    prev = dense_blocks(p) if fol else []
                    for g in range(3):
                        for q, tiles, rows in prev:
                            c = tiles * rows
                            dve.wait_ge(u_ready, 6 * p + 2 * g + q + 1)
                            dve.scalar_tensor_tensor(out=g_t[q][g % 2][:, 0:c], in0=u_t[q][:, 0:c], scalar=SLOPE,
                                                     in1=u_t[q][:, 0:c], op0=ALU.mult, op1=ALU.max).then_inc(g_ready, 1)
                            if g == 2:
                                dve.wait_ge(g_ready, 6 * p + 2 * g + q + 1)
                                dve.tensor_tensor(out=z2_t[q][:, 0:c], in0=g_t[q][0][:, 0:c], in1=y_t[q][:, 0:c],
                                                  op=ALU.add).then_inc(z2_ready, 1)
                    for q, tiles, rows in mine:
                        c = tiles * rows
                        dve.wait_ge(y_mm, 2 * k + q + 1)
                        dve.scalar_tensor_tensor(out=z_t[q][:, 0:c], in0=mm[q][0][:, 0:c], scalar=b3_s[:, 0:1],
                                                 in1=x_t[q][:, 0:c], op0=ALU.add, op1=ALU.add).then_inc(z_ready, 1)
                    if mine:
                        layer_norm([(q, t, r, ga[q], y_rows[q]) for q, t, r in mine], ln1_link, k, ln1_done,
                                   lambda q: dve.wait_ge(z_turned, 2 * k + q + 1),
                                   lambda q: wait(dve, y_stored[q], 16 * k))
                    if prev:
                        layer_norm([(q, t, r, tr[q], out_rows[q]) for q, t, r in prev], ln2_link, p, ln2_done,
                                   lambda q: dve.wait_ge(z2_turned, 2 * p + q + 1),
                                   lambda q: wait(dve, out_stored[q], 16 * p))
                leave()
                dense_run(dve, first, n, body)

            def phase(ph):
                n0 = ph * BLOCKS

                def body(s):
                    if at := s.block(0):
                        b, q, half = at
                        n = n0 + b
                        if ph in GIN:
                            dve.wait_ge(scale_done, n + 1)
                        else:
                            dve.wait_ge(turned, n + 1)
                        wait(dve, mm_done, n - 1)
                        wait(dve, scanned, n)
                        for i in range(2 if L1 < ph <= L5 else 1):
                            last = dve.tensor_tensor_scan(
                                agg[q][:, i, :], keep[:, bass.ds(SB * b, SB)],
                                msg[q][:, :] if ph in GIN else ga[i][:, 0:SB],
                                agg[1 - q][:, i, SB - 1:SB], ALU.mult, ALU.add)
                        last.then_inc(scanned, 1)
                        if ph in GIN:
                            dve.wait_ge(scanned, n + 1)
                            if ph == G1:
                                dve.wait_ge(copied, BLOCKS + b + 1)
                            else:
                                dve.wait_ge(state_in[q], dma_count(STATE, ph, half))
                            own = res[q][:, :] if ph == G1 else state[q][:, 0, :]
                            dve.tensor_tensor(out=agg[q][:, 1, :], in0=agg[q][:, 0, :], in1=own,
                                              op=ALU.add).then_inc(summed, 1)
                    if at := s.block(1):
                        b, q, half = at
                        n = n0 + b
                        if ph == L5:
                            dve.wait_ge(mm_done, n + 1)
                            dve.wait_ge(res_in[q], dma_count(RES, ph, half))
                            wait(dve, back_turned, n - 1)
                            if isinstance(b, int) and b < 2:
                                dve.wait_ge(state_out[q], dma_count(STATE_OUT, L4, BLOCKS // 2 - 1))
                            dve.scalar_tensor_tensor(out=new[q][:, 0, :], in0=mm[q][0][:, 0:SB], scalar=b3_s[:, 0:1],
                                                     in1=res[q][:, :], op0=ALU.add, op1=ALU.add).then_inc(new_ready, 1)
                        elif ph in GIN:
                            dve.wait_ge(lin_done, n - G1 * BLOCKS + 1)
                            wait(dve, back_turned, n - 1)
                            if ph in STATE_OUT:
                                count = dma_count(STATE_OUT, ph, half - 1)
                            else:
                                count = dma_count(STATE_OUT, G2, BLOCKS // 2 - 1)
                            if ph in STATE_OUT or (isinstance(b, int) and b < 2):
                                dve.wait_ge(state_out[q], count)
                            last = dve.scalar_tensor_tensor(out=new[q][:, 0, :], in0=lin[q][:, :], scalar=SLOPE,
                                                            in1=lin[q][:, :], op0=ALU.mult, op1=ALU.max)
                            if ph == G3:
                                last.then_inc(new_half, 1)
                                dve.wait_ge(new_half, b + 1)
                                dve.wait_ge(res_in[q], dma_count(RES, ph, half))
                                last = dve.tensor_tensor(out=new[q][:, 1, :], in0=new[q][:, 0, :],
                                                         in1=res[q][:, :], op=ALU.add)
                            last.then_inc(new_ready, 1)
                    if at := s.block(2):
                        b, q, half = at
                        n = n0 + b
                        def free(_):
                            if ph == G3:
                                if isinstance(b, int) and b < 2:
                                    dve.wait_ge(rows_out[q], dma_count(ROWS_OUT, G2, BLOCKS // 2 - 1))
                                else:
                                    dve.wait_ge(out_scattered[q], 16 * ST * half)
                            else:
                                wait(dve, rows_out[q], dma_count(ROWS_OUT, ph, half - 1))
                        if ph in (L5, G3):
                            layer_norm([(0, ST, SR, tr[0], new_rows[q])], ln_slot_link,
                                       b + (ph == G3) * BLOCKS, rows_ready,
                                       lambda _: dve.wait_ge(back_turned, n + 1), free)
                        else:
                            dve.wait_ge(back_turned, n + 1)
                            free(q)
                            for i in range(2 if ph in HIDDEN else 1):
                                last = dve.tensor_copy(
                                    new_rows[q][:, :, i * D:(i + 1) * D],
                                    tr[i][:SR, 0:ST * D].rearrange("p (j f) -> p j f", f=D))
                            last.then_inc(rows_ready, 1)
                leave()
                phase_run(dve, body)

            schedule(dense, phase, part)


def kernel(x, src, dst, edge_attr_2, L0_gnn_W1, L0_gnn_b1, L0_gnn_W2, L0_gnn_b2, L0_gnn_W3, L0_gnn_b3,
           L1_gnn_Wl, L1_gnn_bl, L1_gnn_W, L1_gnn_b):
    import numpy as np
    import concourse.bacc as bacc
    from concourse import mybir as mb
    from concourse.bass_utils import run_bass_kernel_spmd

    nc = bacc.Bacc("TRN2", target_bir_lowering=False, num_devices=1)
    given = {
        "x": x, "src": src, "dst": dst, "attr_t": np.asarray(edge_attr_2).T,
        "w1": L0_gnn_W1, "b1": L0_gnn_b1, "w2": L0_gnn_W2, "b2": L0_gnn_b2, "w3": L0_gnn_W3, "b3": L0_gnn_b3,
        "wl": L1_gnn_Wl, "bl": L1_gnn_bl, "wg": L1_gnn_W, "bg": L1_gnn_b,
    }
    arrays, args = {}, []
    for name, a in given.items():
        a = np.ascontiguousarray(a)
        arrays[f"in_{name}"] = a
        args.append(nc.dram_tensor(f"in_{name}", a.shape, mb.dt.from_np(a.dtype), kind="ExternalInput").ap())
    args.append(nc.dram_tensor("out_x", (TAB_ROWS, D), mb.dt.float32, kind="ExternalOutput").ap())
    gnn_kernel(nc, *args)
    r = run_bass_kernel_spmd(nc, [arrays], core_ids=[0])
    return r.results[0]["out_x"][:N]
```

```python
import concourse.bass as bass
from concourse import mybir
from contextlib import ExitStack

N = 50000
E = 12500
D = 128
H = 256
P = 128

DT, DR = 4, 128
DB = DT * DR
PAIRS = (N // DB + 1) // 2
TAIL_T, TAIL_R = 3, 112
ST, SR = 4, 112
SB = ST * SR
EP = -(-E // SB) * SB
BLOCKS = EP // SB
COLS = EP // SR
assert COLS == SR and BLOCKS % 2 == 0
assert (2 * PAIRS - 1) * DB + TAIL_T * TAIL_R == N

PAD_NODE = N + EP
TAB_ROWS = N + EP + 2
ZERO_ROW = EP
CHUNK = EP // 8
INIT_COLS = -(-TAB_ROWS // P)
EPS = 1e-5
SLOPE = 0.01
MAGIC = float(0x5F3759DF)
NEWTON = 3
RSQRT_LINKS = 2 + 3 * NEWTON
LN_LINKS = 3 + RSQRT_LINKS

L1, L2, L3, L4, L5, G1, G2, G3 = range(8)
PHASES = 8
HIDDEN = (L1, L2, L3, L4)
GIN = (G1, G2, G3)
SPLIT = (L2, L3, L4)

PARTS = {"check": 1, "flag": 2, "sort": 3, "runs0": 4, "runs1": 5, "rows": 6, "columns": 7,
         "coefficients": 28}
CHUNKS = 8

SORT_CHUNK = 8 * SR
SORT_CHUNKS = EP // SORT_CHUNK
assert EP % SORT_CHUNK == 0
PLACE = 2.0 ** -14
assert EP < 1 / PLACE


def gnn_kernel(nc, x, x_turned, src, dst, attr_t, w1, b1, w2, b2, w3, b3, wl, bl, wg, bg, out):
    f32, f32r, bf16, i32 = mybir.dt.float32, mybir.dt.float32r, mybir.dt.bfloat16, mybir.dt.int32
    ALU = mybir.AluOpType
    ACT = mybir.ActivationFunctionType

    ctx = ExitStack()
    with ctx:
        def sb(name, shape, dt=f32):
            return ctx.enter_context(nc.sbuf_tensor(name, shape, dt))

        def sem(name):
            return ctx.enter_context(nc.semaphore(name))

        def sems(name):
            return [sem(f"{name}{q}") for q in range(2)]

        def dram(name, shape, dt=f32):
            return nc.dram_tensor(name, shape, dt, kind="Internal").ap()

        def wait(eng, s, count):
            if not (isinstance(count, int) and count <= 0):
                eng.wait_ge(s, count)

        dst_x = dram("dst_x", (EP + 2,), i32)
        src_x = dram("src_x", (EP,), i32)
        attr_x = dram("attr_x", (3, EP))
        rank_x = dram("rank_x", (EP,))
        node_tab = dram("node_tab", (P * INIT_COLS, 2))
        own_x = dram("own_x", (EP, 2 * D))
        sorted_x = dram("sorted_x", (EP, 4))
        h_tab = [dram(f"h_tab{i}", (EP + P, H)) for i in range(2)]
        g_tab = [dram(f"g_tab{i}", (N + EP, D)) for i in range(3)]
        state_x = dram("state_x", (BLOCKS, P, 2, SB))
        res_x = dram("res_x", (2, BLOCKS, P, SB))

        ident = sb("ident", [P, P])
        w1_s = sb("w1_s", [P, 2, H])
        w2_s = sb("w2_s", [P, 4, H])
        w3_s = sb("w3_s", [P, 4, D])
        wg_s = sb("wg_s", [P, 3, D])
        wl_s = sb("wl_s", [3, 3, D])
        b1_s = sb("b1_s", [P, 2])
        b2_s = sb("b2_s", [P, 2])
        b3_s = sb("b3_s", [P, 1])
        bg_s = sb("bg_s", [P, 3])
        ones = sb("ones", [1, CHUNK])
        w2_hi = sb("w2_hi", [P, 4, H], f32r)
        w2_lo = sb("w2_lo", [P, 4, H], f32r)
        zero_rows = sb("zero_rows", [P, H])

        keep = sb("keep", [P, EP], bf16)
        dst_chunk = sb("dst_chunk", [P, CHUNK + 1], i32)
        rank_row = sb("rank_row", [1, 2, CHUNK])
        init_i = sb("init_i", [P, 1], i32)
        init_f = sb("init_f", [P, 1])
        node_init = sb("node_init", [P, INIT_COLS, 2])
        rows_i = sb("rows_i", [SR, 3, COLS], i32)
        rows_f = sb("rows_f", [SR, 4, COLS])
        cols_f = sb("cols_f", [SR, 4, COLS])
        slot_i = sb("slot_i", [SR, COLS], i32)
        slot_f = sb("slot_f", [SR, COLS])
        tmp = sb("tmp", [SR, 4, COLS])
        scatter_idx = sb("scatter_idx", [SR, COLS], i32)
        scatter_val = sb("scatter_val", [SR, COLS, 2])
        dst_idx = sb("dst_idx", [SR, COLS], i32)
        x_dst_idx = sb("x_dst_idx", [SR, COLS], i32)
        src_idx = sb("src_idx", [SR, COLS], i32)
        of_dst = sb("of_dst", [SR, COLS, 2])
        of_src = sb("of_src", [SR, COLS, 2])
        coef = sb("coef", [SR, COLS])
        h_idx = sb("h_idx", [SR, COLS], i32)
        g_idx = sb("g_idx", [SR, COLS], i32)
        idx_now = [sb(f"idx_now{q}", [SR, 2 * ST], i32) for q in range(2)]
        carrier = sb("carrier", [1, 1])
        out_idx = [sb(f"out_idx{q}", [SR, ST], i32) for q in range(2)]
        tab_now = [sb(f"tab_now{q}", [SR, 2 * ST, 2]) for q in range(2)]
        violations = sb("violations", [SR, COLS])
        column_of_ones = sb("column_of_ones", [P, 1])
        flag_row = sb("flag_row", [1, COLS])
        flag_f = sb("flag_f", [1, 1])
        flag_i = sb("flag_i", [1, 1], i32)
        rs_a = sb("rs_a", [P, COLS])
        rs_b = sb("rs_b", [P, COLS])

        x_t = [[sb(f"x_t{q}{v}", [P, DB]) for v in range(2)] for q in range(2)]
        h_t = [[sb(f"h_t{q}{v}", [P, 2, DB]) for v in range(2)] for q in range(2)]
        z_t = [sb(f"z_t{q}", [P, DB]) for q in range(2)]
        y_rows = [sb(f"y_rows{q}", [P, DT, D]) for q in range(2)]
        y_t = [sb(f"y_t{q}", [P, DB]) for q in range(2)]
        u_t = [sb(f"u_t{q}", [P, DB]) for q in range(2)]
        g_t = [[sb(f"g_t{q}{v}", [P, DB]) for v in range(2)] for q in range(2)]
        g_rows_pair = [sb(f"g_rows_pair{q}", [P, 2 * DT, D]) for q in range(2)]
        g_rows = [[g_rows_pair[q][:, g * DT:(g + 1) * DT, :] for q in range(2)] for g in range(2)]
        z2_t = [sb(f"z2_t{q}", [P, DB]) for q in range(2)]
        out_rows = [sb(f"out_rows{q}", [P, DT, D]) for q in range(2)]
        stats = sb("stats", [P, 2 * DT, 6])
        mean_var = sb("mean_var", [P, 2 * DT, 2])
        rstd = sb("rstd", [P, 2 * DT])
        ln_a = sb("ln_a", [P, 2 * DT])
        ln_b = sb("ln_b", [P, 2 * DT])

        got = [sb(f"got{q}", [SR, ST, H]) for q in range(2)]
        scaled = [sb(f"scaled{q}", [SR, ST, H]) for q in range(2)]
        state = [sb(f"state{q}", [P, 2, SB]) for q in range(2)]
        res = [u_t[q][:, 0:SB] for q in range(2)]
        agg = [h_t[q][0][:, :, 0:SB] for q in range(2)]
        new = [h_t[q][1][:, :, 0:SB] for q in range(2)]
        state_hi, state_lo, agg_hi, agg_lo = (
            [sb(f"{name}{q}", [P, 2, SB], f32r) for q in range(2)]
            for name in ("state_hi", "state_lo", "agg_hi", "agg_lo"))
        lin = [z_t[q][:, 0:SB] for q in range(2)]
        msg = [y_t[q][:, 0:SB] for q in range(2)]
        attr = [sb(f"attr{q}", [3, SB]) for q in range(2)]
        new_rows = [g_rows_pair[q][:SR, :, :].rearrange("p (j a) f -> p j (a f)", a=2) for q in range(2)]

        mm = [[ctx.enter_context(nc.psum_tensor(f"mm{q}{i}", [P, 512], f32)) for i in range(2)]
              for q in range(2)]
        ga = [ctx.enter_context(nc.psum_tensor(f"ga{i}", [P, 512], f32)) for i in range(2)]
        tr = [ctx.enter_context(nc.psum_tensor(f"tr{i}", [P, 512], f32)) for i in range(2)]

        weights_in = sem("weights_in")
        scratch_in = sem("scratch_in")
        pads_set = sem("pads_set")
        pads_in = sem("pads_in")
        ident_zero, ident_set = sem("ident_zero"), sem("ident_set")
        chunk_in, keep_done = sem("chunk_in"), sem("keep_done")
        rank_done, rank_out = sem("rank_done"), [sem(f"rank_out{q}") for q in range(2)]
        init_set, init_out = sem("init_set"), sem("init_out")
        rows_in, rows_cast = sem("rows_in"), sem("rows_cast")
        cols_t, cols_done = sem("cols_t"), sem("cols_done")
        dve_link = sem("dve_link")
        slot_made, index_made = sem("slot_made"), sem("index_made")
        scattered, tab_got = sems("scattered"), sems("tab_got")
        staged, out_staged = sem("staged"), sem("out_staged")
        tab_read = sem("tab_read")
        coef_made = sem("coef_made")
        pe_left, act_left, dve_left = sem("pe_left"), sem("act_left"), sem("dve_left")

        x_loaded = [sems(f"x_loaded{q}") for q in range(2)]
        violations_made, violations_summed, flag_made = sem("violations_made"), sem("violations_summed"), sem("flag_made")
        flag_summed = sem("flag_summed")
        pre_in, pre_out = sems("pre_in"), sems("pre_out")
        sort_cols_in, sort_chunk_in, sort_chunk_read = sem("sort_cols_in"), sem("sort_chunk_in"), sem("sort_chunk_read")
        sort_iota, sort_link, sort_differences, sort_counted = (
            sem("sort_iota"), sem("sort_link"), sem("sort_differences"), sem("sort_counted"))
        sort_placed, sort_staged, sort_scattered = sem("sort_placed"), sem("sort_staged"), sem("sort_scattered")
        sort_rows_in, sort_cast, sort_stored = sem("sort_rows_in"), sem("sort_cast"), sem("sort_stored")
        layer_mm, h_ready = sem("layer_mm"), sem("h_ready")
        y_mm, z_ready, z_turned, ln1_done = sem("y_mm"), sem("z_ready"), sem("z_turned"), sem("ln1_done")
        y_turned, y_t_ready = sem("y_turned"), sem("y_t_ready")
        g_mm, u_ready, g_ready = sem("g_mm"), sem("u_ready"), sem("g_ready")
        g_turned, g_rows_ready = sem("g_turned"), sem("g_rows_ready")
        z2_ready, z2_turned, ln2_done = sem("z2_ready"), sem("z2_turned"), sem("ln2_done")
        ln1_link, ln2_link, ln_slot_link = sem("ln1_link"), sem("ln2_link"), sem("ln_slot_link")
        y_stored, out_stored = sems("y_stored"), sems("out_stored")
        g_stored = [sems(f"g_stored{g}") for g in range(2)]

        got_in, own_in, attr_in = sems("got_in"), sems("own_in"), sems("attr_in")
        state_in, res_in = sems("state_in"), sems("res_in")
        scale_done, turned, copied, scanned = sem("scale_done"), sem("turned"), sem("copied"), sem("scanned")
        summed = sem("summed")
        agg_zero = sem("agg_zero")
        w2_high_made, w2_split = sem("w2_high_made"), sem("w2_split")
        state_high, agg_high, low_made = sem("state_high"), sem("agg_high"), sem("low_made")
        mm_done, lin_done, new_half, new_ready = sem("mm_done"), sem("lin_done"), sem("new_half"), sem("new_ready")
        back_turned, rows_ready = sem("back_turned"), sem("rows_ready")
        state_out, res_out, rows_out, out_scattered = (
            sems("state_out"), sems("res_out"), sems("rows_out"), sems("out_scattered"))

        block = ctx.enter_context(nc.Block())

        PADS = 4 + 2 + EP // CHUNK + 2

        flat = lambda t: t[:, :, :].rearrange("p j f -> p (j f)")[:, 0:SORT_CHUNK]
        sort_dst, sort_place, sort_diff, sort_less = flat(got[0]), flat(got[1]), flat(scaled[0]), flat(scaled[1])
        sort_iota_i = keep[:SR, 0:2 * SORT_CHUNK].bitcast(i32)
        edge_cols = state[0][:SR, 0, :].rearrange("p (t w) -> p t w", w=4)
        edge_rows = state[1][:SR, 0, :].rearrange("t (p w) -> t p w", w=4)

        def if_unsorted(eng):
            eng.wait_ge(flag_made, 1)
            return eng.If(eng.value_load(flag_i[0:1, 0:1]) > 0)

        def dense_blocks(k):
            if isinstance(k, int) and k == PAIRS - 1:
                return [(0, DT, DR), (1, TAIL_T, TAIL_R)]
            return [(0, DT, DR), (1, DT, DR)]

        def dense_view(table, k, q, tiles, rows):
            if tiles == DT:
                whole = table[0:(2 * PAIRS - 1) * DB, :]
                return whole.rearrange("(b j p) f -> b p j f", p=DR, j=DT)[2 * k + q]
            return table[N - tiles * rows:N, :].rearrange("(j p) f -> p j f", p=rows)

        def dense_run(eng, first, n, body):
            steps = list(range(first, first + n))

            def alone():
                k = steps.pop(0)
                body(k, k % 2, k // 2)

            while steps and (steps[0] < 2 or steps[0] % 2):
                alone()
            twos = max(0, (min(first + n, PAIRS - 2) - first - n + len(steps)) // 2)
            if twos:
                half = steps[0] // 2
                with eng.Fori(half, half + twos) as i:
                    body(2 * i, 0, i)
                    body(2 * i + 1, 1, i)
                del steps[:2 * twos]
            while steps:
                alone()

        class Step:

            def __init__(self, i, par):
                self.i, self.par = i, par

            def block(self, lag):
                par, half = (self.par - lag) % 2, self.i + (self.par - lag) // 2
                b = 2 * half + par
                if isinstance(b, int) and not 0 <= b < BLOCKS:
                    return None
                return b, par, half

        def phase_run(eng, body, more=0):
            peeled = 2 + more
            for s in range(-1, 2 * peeled):
                body(Step(s // 2, s % 2))
            with eng.Fori(peeled, BLOCKS // 2 - 1) as i:
                body(Step(i, 0))
                body(Step(i, 1))
            for s in range(BLOCKS - 2, BLOCKS + 2 + more):
                body(Step(s // 2, s % 2))

        def dma_count(per_block, phase, half):
            before = sum(per_block.get(p, 0) for p in range(phase)) * (BLOCKS // 2)
            return 16 * (before + per_block[phase] * (half + 1))

        GOT = {p: 4 for p in range(PHASES)} | {L1: 1}
        ONCE_L1_G1 = {L1: 1, G1: 1}
        STATE = {L2: 1, L3: 1, L4: 1, L5: 1, G2: 1, G3: 1}
        STATE_OUT = {L1: 1, L2: 1, L3: 1, L4: 1, G1: 1, G2: 1}
        RES = {L5: 1, G3: 1}
        ROWS_OUT = {p: 1 for p in range(G3)}
        GIN_ONCE = {G1: 1, G2: 1, G3: 1}

        def schedule(dense, phase, part):
            k = 0
            for what, upto in PARTS.items():
                dense(k, upto - k)
                k = upto
                part(what)
            dense(k, PAIRS + 1 - k)
            for p in range(PHASES):
                phase(p)

        class Turnstile:

            def __init__(self, eng, mine):
                self.eng, self.mine, self.n = eng, mine, 0

            def __call__(self):
                self.n += 1
                self.eng.drain().then_inc(self.mine, 1)
                for s in (pe_left, act_left, dve_left):
                    self.eng.wait_ge(s, self.n)

        @block.sync
        def _(sp):
            for tile, view in (
                (w1_s[:, :, :], w1.rearrange("(k p) n -> p k n", p=P)),
                (w2_s[:, :, :], w2.rearrange("(k p) n -> p k n", p=P)),
                (w3_s[:, :, :], w3.rearrange("(k p) n -> p k n", p=P)),
                (wg_s[:, :, :], wg.rearrange("l p n -> p l n")),
                (wl_s[0:2, :, :], wl.rearrange("l p n -> p l n")),
                (wl_s[2:3, :, :], bl.rearrange("(a l) n -> a l n", a=1)),
                (b1_s[:, :], b1.rearrange("(k p) -> p k", p=P)),
                (b2_s[:, :], b2.rearrange("(k p) -> p k", p=P)),
                (b3_s[:, :], b3.rearrange("(k p) -> p k", p=P)),
                (bg_s[:, :], bg.rearrange("l p -> p l")),
            ):
                with nc.allow_non_contiguous_dma(reason="a few hundred words of biases"):
                    sp.dma_start(tile, view).then_inc(weights_in, 16)
            row = lambda a: a.rearrange("(a n) -> a n", a=1)
            square = lambda a: a.rearrange("(t p) -> t p", p=SR)
            pad = EP - E

            def edges():
                sp.dma_start(row(dst_x[1:1 + E]), row(dst)).then_inc(scratch_in, 16)
                sp.dma_start(row(src_x[0:E]), row(src)).then_inc(scratch_in, 16)
                sp.dma_start(attr_x[0:2, 0:E], attr_t).then_inc(scratch_in, 16)
                sp.wait_ge(pads_set, 5)
                sp.dma_start(row(dst_x[0:1]), slot_i[0:1, 0:1]).then_inc(pads_in, 16)
                sp.dma_start(row(dst_x[1 + E:1 + EP]), dst_chunk[0:1, 0:pad]).then_inc(pads_in, 16)
                sp.dma_start(row(dst_x[1 + EP:2 + EP]), x_dst_idx[0:1, 0:1]).then_inc(pads_in, 16)
                sp.dma_start(row(src_x[E:EP]), src_idx[0:1, 0:pad]).then_inc(pads_in, 16)
                for r in range(2):
                    sp.dma_start(attr_x[r:r + 1, E:EP], ones[0:1, 0:pad]).then_inc(pads_in, 16)
                for c in range(CHUNKS):
                    sp.dma_start(attr_x[2:3, c * CHUNK:(c + 1) * CHUNK], ones[:, :]).then_inc(pads_in, 16)
                for t in h_tab:
                    sp.dma_start(t[EP:EP + P, :], zero_rows[:, :]).then_inc(pads_in, 16)
                sp.wait_ge(scratch_in, 48)
                sp.wait_ge(pads_in, 16 * PADS)
                dst_rows()
                sp.wait_ge(init_set, 1)
                sp.dma_start(node_tab.rearrange("(p c) w -> p c w", p=P),
                             node_init[:, :, :]).then_inc(init_out, 16)

            def dst_rows():
                sp.dma_start(rows_i[:, 0, :], square(dst_x[1:1 + EP])).then_inc(rows_in, 16)
                sp.dma_start(rows_i[:, 1, :], square(dst_x[2:2 + EP])).then_inc(rows_in, 16)

            def put_ranks(c):
                sp.wait_ge(rank_done, c + 1)
                sp.dma_start(row(rank_x[c * CHUNK:(c + 1) * CHUNK]),
                             rank_row[:, c % 2, :]).then_inc(rank_out[c % 2], 16)

            def sort():
                column = lambda a: a.rearrange("(t p) -> p t", p=SR)
                with nc.allow_non_contiguous_dma(reason="the edges' tables by column, once"):
                    for to, of in ((rows_i[:, 0, :], dst_x[1:1 + EP]), (rows_i[:, 1, :], src_x[0:EP]),
                                   (cols_f[:, 0, :], attr_x[0]), (cols_f[:, 1, :], attr_x[1])):
                        sp.dma_start(to, column(of)).then_inc(sort_cols_in, 16)
                for c in range(SORT_CHUNKS):
                    wait(sp, sort_chunk_read, c)
                    at = 1 + c * SORT_CHUNK
                    sp.dma_start(dst_chunk[:, 0:SORT_CHUNK],
                                 row(dst_x[at:at + SORT_CHUNK]).to_broadcast([P, SORT_CHUNK])
                                 ).then_inc(sort_chunk_in, 16)
                sp.wait_ge(sort_scattered, 16 * COLS)
                sp.dma_start(edge_rows, sorted_x.rearrange("(t p) w -> t p w", p=SR)).then_inc(sort_rows_in, 16)
                sp.wait_ge(sort_cast, 1)
                for to, of in ((dst_x[1:1 + EP], rows_i[:, 0, :]), (src_x[0:EP], rows_i[:, 1, :]),
                               (attr_x[0], cols_f[:, 0, :]), (attr_x[1], cols_f[:, 1, :])):
                    sp.dma_start(square(to), of).then_inc(sort_stored, 16)
                sp.wait_ge(sort_stored, 64)

            def part(what):
                if what == "check":
                    edges()
                if what == "sort":
                    with if_unsorted(sp):
                        sort()
                if what.startswith("runs"):
                    at = int(what[-1]) * CHUNKS // 2
                    for c in range(at, at + CHUNKS // 2):
                        wait(sp, keep_done, c)
                        sp.dma_start(dst_chunk[:, :],
                                     row(dst_x[c * CHUNK:(c + 1) * CHUNK + 1]).to_broadcast([P, CHUNK + 1])
                                     ).then_inc(chunk_in, 16)
                        if c > at:
                            put_ranks(c - 1)
                    put_ranks(at + CHUNKS // 2 - 1)
                if what == "rows":
                    dst_rows()
                    sp.dma_start(rows_i[:, 2, :], square(src_x[0:EP])).then_inc(rows_in, 16)
                    for q in range(2):
                        sp.wait_ge(rank_out[q], 16 * CHUNKS // 2)
                    sp.dma_start(rows_f[:, 3, :], square(rank_x[0:EP])).then_inc(rows_in, 16)

            def load_x(k, v):
                for q, tiles, rows in dense_blocks(k):
                    wait(sp, z_ready, 2 * k + q - 3)
                    if tiles == DT:
                        of = x_turned[:, 0:(2 * PAIRS - 1) * DB].rearrange("f (b c) -> b f c", c=DB)[2 * k + q]
                    else:
                        of = x_turned[:, N - tiles * rows:N]
                    sp.dma_start(x_t[q][v][:, 0:tiles * rows], of).then_inc(x_loaded[q][v], 16)

            def dense(first, n):
                def body(k, v, half):
                    if isinstance(k, int) and k == 0:
                        load_x(0, 0)
                        load_x(1, 1)
                        return
                    if not isinstance(k, int) or k < PAIRS - 1:
                        load_x(k + 1, 1 - v)
                    p = k - 1
                    for q, tiles, rows in dense_blocks(p):
                        sp.wait_ge(ln1_done, 2 * p + q + 1)
                        sp.dma_start(dense_view(g_tab[0], p, q, tiles, rows),
                                     y_rows[q][:rows, :tiles, :]).then_inc(y_stored[q], 16)
                    for g in range(2):
                        for q, tiles, rows in dense_blocks(p):
                            sp.wait_ge(g_rows_ready, 4 * p + 2 * g + q + 1)
                            sp.dma_start(dense_view(g_tab[1 + g], p, q, tiles, rows),
                                         g_rows[g][q][:rows, :tiles, :]).then_inc(g_stored[g][q], 16)
                    for q, tiles, rows in dense_blocks(p):
                        sp.wait_ge(ln2_done, 2 * p + q + 1)
                        sp.dma_start(dense_view(out, p, q, tiles, rows),
                                     out_rows[q][:rows, :tiles, :]).then_inc(out_stored[q], 16)
                dense_run(sp, first, n, body)

            def phase(ph):
                n0 = ph * BLOCKS

                def rows_of(b, table, base, width):
                    whole = table[base:base + EP, :].rearrange("(b j p) f -> b p j f", j=ST, p=SR)
                    return whole[b]

                def body(s):
                    if at := s.block(-1):
                        b, q, half = at
                        n = n0 + b
                        if ph == G1 and isinstance(b, int) and b < 2:
                            for r in range(2):
                                sp.wait_ge(rows_out[r], dma_count(ROWS_OUT, L5, BLOCKS // 2 - 1))
                        if ph in GIN:
                            wait(sp, turned, n - 1)
                            sp.dma_start(attr[q][:, :], attr_x[:, :].rearrange(
                                "r (b c) -> b r c", c=SB)[b]).then_inc(attr_in[q], 16)
                        if ph == G1:
                            sp.dma_start(scaled[q][:, :, 0:D],
                                         rows_of(b, g_tab[0], N, D)).then_inc(own_in[q], 16)
                        if ph in STATE:
                            if isinstance(b, int) and b < 2:
                                prev = max(p for p in STATE_OUT if p < ph)
                                sp.wait_ge(state_out[q], dma_count(STATE_OUT, prev, BLOCKS // 2 - 1))
                            wait(sp, mm_done, n - 1)
                            parts = 1 if ph in GIN else 2
                            sp.dma_start(state[q][:, 0:parts, :],
                                         state_x[b, :, 0:parts, :]).then_inc(state_in[q], 16)
                        if ph in RES:
                            if isinstance(b, int) and b < 2:
                                sp.wait_ge(res_out[q], dma_count(ONCE_L1_G1, L1 if ph == L5 else G1,
                                                                 BLOCKS // 2 - 1))
                            wait(sp, new_ready, n - 1)
                            sp.dma_start(res[q][:, :], res_x[ph == G3, b]).then_inc(res_in[q], 16)
                    if at := s.block(1):
                        b, q, half = at
                        if ph in ONCE_L1_G1:
                            sp.wait_ge(copied, ((ph == G1) * BLOCKS) + b + 1)
                            sp.dma_start(res_x[ph == G1, b], res[q][:, :]).then_inc(res_out[q], 16)
                        if ph in STATE_OUT:
                            parts = 1 if ph in GIN else 2
                            sp.wait_ge(new_ready, n0 + b + 1)
                            sp.dma_start(state_x[b, :, 0:parts, :],
                                         new[q][:, 0:parts, :]).then_inc(state_out[q], 16)
                    if at := s.block(2):
                        b, q, half = at
                        if ph in ROWS_OUT:
                            sp.wait_ge(rows_ready, n0 + b + 1)
                            if ph in HIDDEN:
                                to = rows_of(b, h_tab[ph % 2], 0, H)
                                sp.dma_start(to, new_rows[q][:, :, :]).then_inc(rows_out[q], 16)
                            else:
                                to = rows_of(b, g_tab[ph - L5], N, D)
                                sp.dma_start(to, new_rows[q][:, :, 0:D]).then_inc(rows_out[q], 16)
                phase_run(sp, body)

            schedule(dense, phase, part)
            for q in range(2):
                sp.wait_ge(out_scattered[q], 16 * 4 * BLOCKS // 2)
                sp.wait_ge(out_stored[q], 16 * PAIRS)

        @block.gpsimd
        def _(pool):
            pool.memset(ident[:, :], 0.0).then_inc(ident_zero, 1)
            pool.wait_ge(ident_zero, 1)
            pool.affine_select(out=ident[:, :], in_=ident[:, :], compare_op=ALU.not_equal, fill=1.0,
                               base=0, pattern=[[-1, P]], channel_multiplier=1).then_inc(ident_set, 1)
            pool.memset(slot_i[:, :], -1).then_inc(pads_set, 1)
            pool.memset(dst_chunk[:, :], PAD_NODE).then_inc(pads_set, 1)
            pool.memset(src_idx[:, :], 0).then_inc(pads_set, 1)
            pool.memset(x_dst_idx[:, :], PAD_NODE + 1).then_inc(pads_set, 1)
            pool.memset(zero_rows[:, :], 0.0)
            pool.memset(carrier[:, :], 0.0)
            pool.memset(ones[:, :], 1.0).then_inc(pads_set, 1)
            pool.iota(init_i[:, :], pattern=[[0, 1]], base=ZERO_ROW, channel_multiplier=1
                      ).then_inc(slot_made, 1)
            pool.wait_ge(pads_in, 16 * PADS)
            pool.iota(slot_i[:, :], pattern=[[SR, COLS]], base=0, channel_multiplier=1
                      ).then_inc(slot_made, 1)

            def gather(to, table, index, done):
                pool.indirect_dma_start(out=to, out_offset=None, in_=table,
                                        in_offset=bass.IndirectOffsetOnAxis(ap=index, axis=0)
                                        ).then_inc(done, 16)

            def scatter(table, index, of, done):
                pool.indirect_dma_start(out=table, in_=of, in_offset=None,
                                        out_offset=bass.IndirectOffsetOnAxis(ap=index, axis=0)
                                        ).then_inc(done, 16)

            def settled(done, count):
                pool.wait_ge(done, count)
                if not isinstance(count, int):
                    pool.tensor_tensor(out=carrier[:, :], in0=carrier[:, :], in1=carrier[:, :], op=ALU.add)

            def sort():
                pool.iota(sort_iota_i, pattern=[[1, SORT_CHUNK]], base=0, channel_multiplier=0
                          ).then_inc(sort_iota, 1)
                pool.wait_ge(sort_placed, 1)
                rows = tab_now[0][:, :, :].rearrange("p (j a) w -> p j (a w)", a=2)

                def put(b):
                    wait(pool, sort_scattered, 16 * ST * b)
                    pool.tensor_copy(idx_now[0][:, 0:ST], dst_idx[:, bass.ds(ST * b, ST)])
                    pool.tensor_copy(rows, edge_cols[:, bass.ds(ST * b, ST), :]).then_inc(sort_staged, 1)
                    settled(sort_staged, b + 1)
                    for j in range(ST):
                        scatter(sorted_x, idx_now[0][:, j:j + 1], rows[:, j, :], sort_scattered)
                put(0)
                with pool.Fori(1, BLOCKS) as b:
                    put(b)
                pool.wait_ge(sort_scattered, 16 * COLS)

            def part(what):
                if what == "sort":
                    with if_unsorted(pool):
                        sort()
                if what == "columns":
                    pool.wait_ge(index_made, 1)
                    pool.wait_ge(init_out, 16)
                    def put(i):
                        for q in range(2):
                            b = 2 * i + q
                            wait(pool, scattered[q], 16 * ST * i)
                            pool.tensor_copy(idx_now[q][:, 0:ST], scatter_idx[:, bass.ds(ST * b, ST)])
                            pool.tensor_copy(tab_now[q][:, 0:ST, :], scatter_val[:, bass.ds(ST * b, ST), :]
                                             ).then_inc(staged, 1)
                            pool.wait_ge(init_out, 16)
                            settled(staged, b + 1)
                            for j in range(ST):
                                scatter(node_tab, idx_now[q][:, j:j + 1], tab_now[q][:, j, :], scattered[q])
                    put(0)
                    with pool.Fori(1, BLOCKS // 2) as i:
                        put(i)
                    for q in range(2):
                        pool.wait_ge(scattered[q], 16 * ST * BLOCKS // 2)

                    def read(q, b):
                        pool.tensor_copy(of_dst[:, bass.ds(ST * b, ST), :], tab_now[q][:, 0:ST, :])
                        return pool.tensor_copy(of_src[:, bass.ds(ST * b, ST), :], tab_now[q][:, ST:2 * ST, :])

                    def get(i):
                        for q in range(2):
                            b = 2 * i + q
                            if not isinstance(i, int):
                                pool.wait_ge(tab_got[q], 16 * 2 * ST * i)
                                read(q, b - 2)
                            pool.tensor_copy(idx_now[q][:, 0:ST], dst_idx[:, bass.ds(ST * b, ST)])
                            pool.tensor_copy(idx_now[q][:, ST:2 * ST], src_idx[:, bass.ds(ST * b, ST)]
                                             ).then_inc(staged, 1)
                            pool.wait_ge(scattered[q], 16 * ST * BLOCKS // 2)
                            settled(staged, BLOCKS + b + 1)
                            for j in range(2 * ST):
                                gather(tab_now[q][:, j, :], node_tab, idx_now[q][:, j:j + 1], tab_got[q])
                    get(0)
                    with pool.Fori(1, BLOCKS // 2) as i:
                        get(i)
                    for q in range(2):
                        pool.wait_ge(tab_got[q], 16 * 2 * ST * BLOCKS // 2)
                        read(q, BLOCKS - 2 + q).then_inc(tab_read, 1)

                    def ends(i):
                        for q in range(2):
                            b = 2 * i + q
                            wait(pool, pre_out[q], 16 * i)
                            pool.tensor_copy(idx_now[q][:, 0:ST], src_idx[:, bass.ds(ST * b, ST)])
                            pool.tensor_copy(idx_now[q][:, ST:2 * ST], x_dst_idx[:, bass.ds(ST * b, ST)]
                                             ).then_inc(staged, 1)
                            settled(staged, 2 * BLOCKS + b + 1)
                            for j in range(2 * ST):
                                gather(got[q][:, j % ST, j // ST * D:(j // ST + 1) * D], x,
                                       idx_now[q][:, j:j + 1], pre_in[q])
                        for q in range(2):
                            b = 2 * i + q
                            pool.wait_ge(pre_in[q], 16 * 2 * ST * (i + 1))
                            pool.dma_start(own_x.rearrange("(b j p) f -> b p j f", j=ST, p=SR)[b],
                                           got[q][:, :, :]).then_inc(pre_out[q], 16)
                    ends(0)
                    with pool.Fori(1, BLOCKS // 2) as i:
                        ends(i)

            def phase(ph):
                n0 = ph * BLOCKS
                if ph == L1:
                    def load(s):
                        if at := s.block(-1):
                            b, q, half = at
                            if isinstance(b, int) and b < 2:
                                for r in range(2):
                                    pool.wait_ge(pre_out[r], 16 * BLOCKS // 2)
                            wait(pool, scale_done, b - 1)
                            pool.dma_start(got[q][:, :, :],
                                           own_x.rearrange("(b j p) f -> b p j f", j=ST, p=SR)[b]
                                           ).then_inc(got_in[q], 16)
                    phase_run(pool, load)
                    return
                table = h_tab[(ph - 1) % 2] if ph <= L5 else g_tab[ph - G1]
                index = h_idx if ph <= L5 else g_idx
                width = D if ph in GIN else H
                if ph == L2:
                    pool.wait_ge(coef_made, 1)
                for q in range(2):
                    pool.wait_ge(rows_out[q], dma_count(ROWS_OUT, ph - 1, BLOCKS // 2 - 1))
                if ph in GIN:
                    for q in range(2):
                        pool.wait_ge((y_stored, g_stored[0], g_stored[1])[ph - G1][q], 16 * PAIRS)
                if ph == G3:
                    for q in range(2):
                        pool.wait_ge(out_stored[q], 16 * PAIRS)

                def body(s):
                    if at := s.block(-1):
                        b, q, half = at
                        if ph in GIN:
                            wait(pool, turned, n0 + b - 1)
                            if ph == G1 and isinstance(b, int) and b < 2:
                                pool.wait_ge(scale_done, G1 * BLOCKS)
                        else:
                            wait(pool, scale_done, n0 + b - 1)
                        pool.tensor_copy(idx_now[q][:, 0:ST], index[:, bass.ds(ST * b, ST)]).then_inc(staged, 1)
                        settled(staged, 2 * BLOCKS + n0 + b + 1)
                        for j in range(ST):
                            gather(got[q][:, j, 0:width], table, idx_now[q][:, j:j + 1], got_in[q])
                    if ph == G3 and (at := s.block(3)):
                        b, q, half = at
                        pool.wait_ge(rows_ready, n0 + b + 1)
                        wait(pool, out_scattered[q], 16 * ST * half)
                        pool.tensor_copy(out_idx[q][:, :], scatter_idx[:, bass.ds(ST * b, ST)]).then_inc(out_staged, 1)
                        pool.wait_ge(out_stored[q], 16 * PAIRS)
                        settled(out_staged, b + 1)
                        for j in range(ST):
                            scatter(out, out_idx[q][:, j:j + 1], new_rows[q][:, j, 0:D], out_scattered[q])
                phase_run(pool, body, more=ph == G3)

            schedule(lambda k, n: None, phase, part)

        @block.tensor
        def _(pe):
            leave = Turnstile(pe, pe_left)
            pe.wait_ge(ident_set, 1)
            pe.wait_ge(weights_in, 160)

            def part(what):
                k = PARTS.get(what) - 1
                if what == "flag":
                    pe.wait_ge(violations_made, 1)
                    pe.wait_ge(h_ready, 8 * k + 7)
                    pe.matmul(mm[0][1][0:1, 0:COLS], column_of_ones[:SR, :], violations[:, :],
                              start=True, stop=True).then_inc(violations_summed, 1)
                    pe.wait_ge(flag_made, 1)
                if what == "columns":
                    pe.wait_ge(rows_cast, 1)
                    pe.wait_ge(h_ready, 8 * k + 7)
                    for i in range(4):
                        last = pe.transpose(mm[0][1][:SR, i * COLS:(i + 1) * COLS], rows_f[:, i, :],
                                            ident[:SR, :SR])
                    last.then_inc(cols_t, 1)
                    pe.wait_ge(cols_done, 1)

            def turn(to, of, tiles, rows):
                for j in range(tiles):
                    last = pe.transpose(to[:, j * rows:(j + 1) * rows], of[:rows, j, :], ident[:rows, :rows])
                return last

            def turn_back(to, of, tiles, rows):
                for j in range(tiles):
                    last = pe.transpose(to[:rows, j * D:(j + 1) * D], of[:, j * rows:(j + 1) * rows], ident[:, :])
                return last

            def product(to, weights, moving, cols):
                for i, (w, m) in enumerate(zip(weights, moving)):
                    last = pe.matmul(to[:, 0:cols], w, m, start=i == 0, stop=i == len(weights) - 1)
                return last

            def dense(first, n):
                def body(k, v, half):
                    run = not isinstance(k, int) or k < PAIRS
                    fol = not isinstance(k, int) or k > 0
                    mine = dense_blocks(k) if run else []
                    p = k - 1
                    prev = dense_blocks(p) if fol else []

                    def layer(l, only=(0, 1)):
                        for q, tiles, rows in mine:
                            if q not in only:
                                continue
                            c = tiles * rows
                            if l == 0:
                                pe.wait_ge(x_loaded[q][v], 16 * (half + 1))
                                weights, moving = lambda f: [w1_s[:, 0, f]], [x_t[q][v][:, 0:c]]
                            else:
                                pe.wait_ge(h_ready, 8 * k + 2 * (l - 1) + q + 1)
                                of = h_t[q][(l - 1) % 2]
                                moving = [of[:, i, 0:c] for i in range(2)]
                                weights = (lambda f: [w2_s[:, i, f] for i in range(2)]) if l < 4 else (
                                    lambda f: [w3_s[:, i, f] for i in range(2)])
                            for i in range(2 if l < 4 else 1):
                                last = product(mm[q][i], weights(slice(i * P, (i + 1) * P)), moving, c)
                            last.then_inc(layer_mm if l < 4 else y_mm, 1)

                    layer(0)
                    layer(1, (0,))
                    for q, tiles, rows in prev:
                        pe.wait_ge(ln1_done, 2 * p + q + 1)
                        turn(ga[q], y_rows[q], tiles, rows).then_inc(y_turned, 1)
                    layer(1, (1,))

                    def gin(g):
                        for q, tiles, rows in prev:
                            c = tiles * rows
                            if g == 0:
                                pe.wait_ge(y_t_ready, 2 * p + q + 1)
                                moving = y_t[q][:, 0:c]
                            else:
                                pe.wait_ge(g_ready, 6 * p + 2 * (g - 1) + q + 1)
                                moving = g_t[q][(g - 1) % 2][:, 0:c]
                            product(ga[q], [wg_s[:, g, :]], [moving], c).then_inc(g_mm, 1)

                    def gin_rows(g):
                        for q, tiles, rows in prev:
                            pe.wait_ge(g_ready, 6 * p + 2 * g + q + 1)
                            if g == 0:
                                wait(pe, ln2_done, 2 * p - 1 + q)
                            else:
                                pe.wait_ge(g_rows_ready, 4 * p + 2 * (g - 1) + q + 1)
                            turn_back(tr[q], g_t[q][g % 2], tiles, rows).then_inc(g_turned, 1)

                    gin(0)
                    layer(2)
                    gin(1)
                    gin_rows(0)
                    layer(3)
                    gin(2)
                    gin_rows(1)
                    layer(4)
                    for q, tiles, rows in prev:
                        pe.wait_ge(z2_ready, 2 * p + q + 1)
                        pe.wait_ge(g_rows_ready, 4 * p + 2 + q + 1)
                        turn_back(tr[q], z2_t[q], tiles, rows).then_inc(z2_turned, 1)
                    for q, tiles, rows in mine:
                        pe.wait_ge(z_ready, 2 * k + q + 1)
                        wait(pe, u_ready, 6 * k - 1 + q)
                        turn_back(ga[q], z_t[q], tiles, rows).then_inc(z_turned, 1)
                dense_run(pe, first, n, body)

            def phase(ph):
                n0 = ph * BLOCKS

                def body(s):
                    if at := s.block(0):
                        b, q, half = at
                        n = n0 + b
                        wait(pe, scanned, n)
                        if ph in GIN:
                            pe.wait_ge(attr_in[q], dma_count(GIN_ONCE, ph, half))
                            pe.wait_ge(got_in[q], dma_count(GOT, ph, half))
                            if ph == G1:
                                pe.wait_ge(own_in[q], 16 * (half + 1))
                                wait(pe, copied, BLOCKS + b)
                                turn(ga[1], scaled[q][:, :, 0:D], ST, SR)
                            pe.matmul(ga[0][:, 0:SB], wl_s[:, ph - G1, :], attr[q][:, :], start=True, stop=False)
                            for j in range(ST):
                                last = pe.matmul(ga[0][:, j * SR:(j + 1) * SR], got[q][:, j, 0:D],
                                                 ident[:SR, :SR], start=False, stop=j == ST - 1)
                        else:
                            pe.wait_ge(scale_done, n + 1)
                            if ph == L1:
                                wait(pe, copied, b)
                            for i in range(2):
                                last = turn(ga[i], scaled[q][:, :, i * D:(i + 1) * D], ST, SR)
                        last.then_inc(turned, 1)
                    if at := s.block(1):
                        b, q, half = at
                        n = n0 + b
                        wait(pe, new_ready, n - 1)
                        if ph in GIN:
                            pe.wait_ge(summed, n - G1 * BLOCKS + 1)
                            last = product(mm[q][0], [wg_s[:, ph - G1, :]], [agg[q][:, 1, :]], SB)
                        elif ph in SPLIT:
                            pe.wait_ge(w2_split, 1)
                            pe.wait_ge(low_made, 2 * (n - L2 * BLOCKS + 1))
                            for i in range(2):
                                weights, moving = [], []
                                for high, low, at in ((state_hi[q], state_lo[q], 0), (agg_hi[q], agg_lo[q], 2)):
                                    for r in range(2):
                                        w_high, w_low = (w[:, at + r, i * P:(i + 1) * P] for w in (w2_hi, w2_lo))
                                        weights += [w_high, w_low, w_high]
                                        moving += [high[:, r, :], high[:, r, :], low[:, r, :]]
                                last = product(mm[q][i], weights, moving, SB)
                        else:
                            pe.wait_ge(scanned, n + 1)
                            if ph == L1:
                                pe.wait_ge(copied, b + 1)
                                moving, w, k = [res[q][:, :], agg[q][:, 0, :]], w1_s, 2
                            else:
                                pe.wait_ge(state_in[q], dma_count(STATE, ph, half))
                                moving = [state[q][:, 0, :], state[q][:, 1, :], agg[q][:, 0, :], agg[q][:, 1, :]]
                                w, k = (w3_s if ph == L5 else w2_s), 4
                            for i in range(1 if ph == L5 else 2):
                                last = product(mm[q][i], [w[:, r, i * P:(i + 1) * P] for r in range(k)], moving, SB)
                        last.then_inc(mm_done, 1)
                    if at := s.block(2):
                        b, q, half = at
                        n = n0 + b
                        pe.wait_ge(new_ready, n + 1)
                        wait(pe, rows_ready, n)
                        if ph in HIDDEN:
                            turn_back(tr[0], new[q][:, 0, :], ST, SR)
                            last = turn_back(tr[1], new[q][:, 1, :], ST, SR)
                        else:
                            last = turn_back(tr[0], new[q][:, ph == G3, :], ST, SR)
                        last.then_inc(back_turned, 1)
                leave()
                phase_run(pe, body)

            schedule(dense, phase, part)

        @block.scalar
        def _(act):
            leave = Turnstile(act, act_left)
            act.wait_ge(weights_in, 160)

            def part(what):
                if what == "flag":
                    act.wait_ge(violations_summed, 1)
                    act.activation(flag_row[:, :], mm[0][1][0:1, 0:COLS], ACT.Copy,
                                   accum_out=flag_f[:, :]).then_inc(flag_summed, 1)
                    act.wait_ge(flag_summed, 1)
                    act.activation(flag_i[:, :], flag_f[:, :], ACT.Copy).then_inc(flag_made, 1)
                if what == "columns":
                    act.wait_ge(cols_t, 1)
                    act.activation(cols_f[:, :, :].rearrange("p a b -> p (a b)"), mm[0][1][:SR, 0:4 * COLS],
                                   ACT.Copy).then_inc(cols_done, 1)

            def dense(first, n):
                def body(k, v, half):
                    run = not isinstance(k, int) or k < PAIRS
                    fol = not isinstance(k, int) or k > 0
                    mine = dense_blocks(k) if run else []
                    p = k - 1
                    prev = dense_blocks(p) if fol else []

                    def tanh(l, only=(0, 1)):
                        for q, tiles, rows in mine:
                            if q not in only:
                                continue
                            c = tiles * rows
                            act.wait_ge(layer_mm, 8 * k + 2 * l + q + 1)
                            for i in range(2):
                                last = act.activation(h_t[q][l % 2][:, i, 0:c], mm[q][i][:, 0:c], ACT.Tanh,
                                                      bias=(b2_s if l else b1_s)[:, i:i + 1])
                            last.then_inc(h_ready, 1)

                    def linear(g):
                        for q, tiles, rows in prev:
                            c = tiles * rows
                            act.wait_ge(g_mm, 6 * p + 2 * g + q + 1)
                            act.activation(u_t[q][:, 0:c], ga[q][:, 0:c], ACT.Identity,
                                           bias=bg_s[:, g:g + 1]).then_inc(u_ready, 1)

                    def rows_copy(g):
                        for q, tiles, rows in prev:
                            act.wait_ge(g_turned, 4 * p + 2 * g + q + 1)
                            wait(act, g_stored[g][q], 16 * p)
                            act.activation(g_rows[g][q][:rows, :tiles, :].rearrange("p j f -> p (j f)"),
                                           tr[q][:rows, 0:tiles * D], ACT.Copy).then_inc(g_rows_ready, 1)

                    tanh(0)
                    tanh(1, (0,))
                    for q, tiles, rows in prev:
                        act.wait_ge(y_turned, 2 * p + q + 1)
                        act.activation(y_t[q][:, 0:tiles * rows], ga[q][:, 0:tiles * rows],
                                       ACT.Copy).then_inc(y_t_ready, 1)
                    tanh(1, (1,))
                    linear(0)
                    tanh(2)
                    linear(1)
                    rows_copy(0)
                    tanh(3)
                    linear(2)
                    rows_copy(1)
                dense_run(act, first, n, body)

            def phase(ph):
                n0 = ph * BLOCKS

                def body(s):
                    if ph in (L1, G1) and (at := s.block(0)):
                        b, q, half = at
                        act.wait_ge(turned, n0 + b + 1)
                        wait(act, res_out[q], dma_count(ONCE_L1_G1, ph, half - 1))
                        wait(act, mm_done, n0 + b - 1)
                        if ph == G1:
                            wait(act, summed, b - 1)
                        act.activation(res[q][:, :], ga[1][:, 0:SB], ACT.Copy).then_inc(copied, 1)
                    if ph in SPLIT and (at := s.block(0)):
                        b, q, half = at
                        n = n0 + b
                        act.wait_ge(state_in[q], dma_count(STATE, ph, half))
                        wait(act, mm_done, n - 1)
                        act.activation(state_hi[q][:, :, :], state[q][:, :, :], ACT.Copy).then_inc(state_high, 1)
                        act.wait_ge(scanned, n + 1)
                        act.activation(agg_hi[q][:, :, :], agg[q][:, :, :], ACT.Copy).then_inc(agg_high, 1)
                    if ph not in GIN and (at := s.block(-1)):
                        b, q, half = at
                        n = n0 + b
                        act.wait_ge(got_in[q], dma_count(GOT, ph, half))
                        wait(act, turned, n - 1)
                        for j in range(ST):
                            w = D if ph == L1 else H
                            last = act.activation(scaled[q][:, j, 0:w], got[q][:, j, 0:w], ACT.Copy,
                                                  scale=coef[:, bass.ds(ST * b + j, 1)])
                        if ph == L1:
                            last = act.activation(scaled[q][:, :, D:2 * D], got[q][:, :, D:2 * D], ACT.Copy)
                        last.then_inc(scale_done, 1)
                    if ph in GIN and (at := s.block(0)):
                        b, q, half = at
                        act.wait_ge(turned, n0 + b + 1)
                        wait(act, scanned, n0 + b - 1)
                        act.activation(msg[q][:, :], ga[0][:, 0:SB], ACT.Relu).then_inc(scale_done, 1)
                    if at := s.block(1):
                        b, q, half = at
                        n = n0 + b
                        if ph in HIDDEN:
                            act.wait_ge(mm_done, n + 1)
                            wait(act, back_turned, n - 1)
                            if not (ph == L1 and isinstance(b, int) and b < 2):
                                count = (dma_count(STATE_OUT, ph, half - 1))
                                act.wait_ge(state_out[q], count)
                            for i in range(2):
                                last = act.activation(new[q][:, i, :], mm[q][i][:, 0:SB], ACT.Tanh,
                                                      bias=(b1_s if ph == L1 else b2_s)[:, i:i + 1])
                            last.then_inc(new_ready, 1)
                        elif ph in GIN:
                            act.wait_ge(mm_done, n + 1)
                            wait(act, new_ready, n - 1)
                            act.activation(lin[q][:, :], mm[q][0][:, 0:SB], ACT.Identity,
                                           bias=bg_s[:, ph - G1:ph - G1 + 1]).then_inc(lin_done, 1)
                if ph == L1:
                    act.wait_ge(coef_made, 1)
                leave()
                phase_run(act, body)

            schedule(dense, phase, part)

        @block.vector
        def _(dve):
            leave = Turnstile(dve, dve_left)
            links = [0]

            def link(instruction):
                links[0] += 1
                instruction.then_inc(dve_link, 1)
                dve.wait_ge(dve_link, links[0])

            def rsqrt(y, v, a, b, done):
                done(dve.tensor_scalar(a.bitcast(i32), v.bitcast(i32), 1, None, ALU.logical_shift_right))
                done(dve.tensor_scalar(y.bitcast(i32), a.bitcast(i32), -1.0, MAGIC, ALU.mult, ALU.add))
                for _ in range(NEWTON):
                    done(dve.scalar_tensor_tensor(out=a, in0=y, scalar=-0.5, in1=y, op0=ALU.mult, op1=ALU.mult))
                    done(dve.tensor_tensor(out=b, in0=a, in1=v, op=ALU.mult))
                    done(dve.scalar_tensor_tensor(out=y, in0=b, scalar=1.5, in1=y, op0=ALU.add, op1=ALU.mult))

            def layer_norm(blocks, link_sem, index, done_sem, arrived, free):
                count = [index * LN_LINKS]

                def done(instruction):
                    count[0] = count[0] + 1
                    instruction.then_inc(link_sem, 1)
                    dve.wait_ge(link_sem, count[0])

                for q, tiles, rows, bank, to in blocks:
                    arrived(q)
                    for j in range(tiles):
                        last = dve.bn_stats(stats[:rows, q * DT + j, :], bank[:rows, j * D:(j + 1) * D])
                done(last)
                dve.memset(ln_b[:, :], 0.0)
                for q, tiles, rows, bank, to in blocks:
                    for j in range(tiles):
                        last = dve.bn_aggr(mean_var[:rows, q * DT + j, :], stats[:rows, q * DT + j, :])
                done(last)
                w = max(q * DT + tiles for q, tiles, *_ in blocks)
                r = max(rows for _, _, rows, *_ in blocks)
                done(dve.tensor_scalar(rs_a[:r, 0:w], mean_var[:r, 0:w, 1], EPS, None, ALU.add))
                rsqrt(rstd[:r, 0:w], rs_a[:r, 0:w], ln_a[:r, 0:w], ln_b[:r, 0:w], done)
                for q, tiles, rows, bank, to in blocks:
                    free(q)
                    for j in range(tiles):
                        c = q * DT + j
                        last = dve.tensor_scalar(to[:rows, j, 0:D], bank[:rows, j * D:(j + 1) * D],
                                                 mean_var[:rows, c, 0:1], rstd[:rows, c:c + 1],
                                                 ALU.subtract, ALU.mult)
                    last.then_inc(done_sem, 1)

            dve.memset(stats[:, :, :], 1.0)
            dve.memset(mean_var[:, :, :], 1.0)
            dve.memset(column_of_ones[:, :], 1.0)
            dve.wait_ge(weights_in, 160)
            dve.tensor_copy(w2_hi[:, :, :], w2_s[:, :, :]).then_inc(w2_high_made, 1)
            dve.wait_ge(w2_high_made, 1)
            dve.tensor_tensor(out=w2_lo[:, :, :], in0=w2_s[:, :, :], in1=w2_hi[:, :, :].bitcast(f32),
                              op=ALU.subtract).then_inc(w2_split, 1)

            def runs(c):
                dve.wait_ge(chunk_in, 16 * (c + 1))
                at = slice(c * CHUNK, (c + 1) * CHUNK)
                dve.tensor_tensor(out=keep[:, at], in0=dst_chunk[:, 1:CHUNK + 1], in1=dst_chunk[:, 0:CHUNK],
                                  op=ALU.is_equal).then_inc(keep_done, 1)
                dve.wait_ge(keep_done, c + 1)
                if c >= 2:
                    dve.wait_ge(rank_out[c % 2], 16 * (c // 2))
                if c:
                    dve.wait_ge(rank_done, c)
                before = rank_row[:, (c - 1) % 2, CHUNK - 1:CHUNK] if c else 0.0
                dve.tensor_tensor_scan(rank_row[:, c % 2, :], keep[0:1, at], ones[:, :], before,
                                       ALU.mult, ALU.add).then_inc(rank_done, 1)

            def sort():
                links = [0]

                def link(instruction):
                    links[0] += 1
                    instruction.then_inc(sort_link, 1)
                    dve.wait_ge(sort_link, links[0])

                own_dst, own_place, bound, less = (tmp[:, i, :] for i in range(4))
                places = rs_a[:SR, :]
                dve.wait_ge(sort_cols_in, 64)
                dve.tensor_copy(own_dst, rows_i[:, 0, :])
                for i, of in enumerate((rows_i[:, 0, :], rows_i[:, 1, :], cols_f[:, 0, :], cols_f[:, 1, :])):
                    dve.tensor_copy(edge_cols[:, :, i], of)
                link(dve.tensor_copy(slot_f[:, :], slot_i[:, :]))
                dve.tensor_scalar(own_place, slot_f[:, :], PLACE, None, ALU.mult)
                dve.wait_ge(sort_iota, 1)
                link(dve.tensor_copy(sort_diff, sort_iota_i))
                link(dve.tensor_scalar(sort_place, sort_diff, PLACE, None, ALU.mult))
                for c in range(SORT_CHUNKS):
                    dve.wait_ge(sort_chunk_in, 16 * (c + 1))
                    dve.tensor_copy(sort_dst, dst_chunk[:SR, 0:SORT_CHUNK]).then_inc(sort_chunk_read, 1)
                    link(dve.tensor_scalar(bound, own_place, -PLACE * SORT_CHUNK * c, None, ALU.add))
                    dve.wait_ge(sort_chunk_read, c + 1)

                    def count(t):
                        wait(dve, sort_counted, t + c * COLS)
                        dve.scalar_tensor_tensor(out=sort_diff, in0=sort_dst, scalar=own_dst[:, bass.ds(t, 1)],
                                                 in1=sort_place, op0=ALU.subtract, op1=ALU.add
                                                 ).then_inc(sort_differences, 1)
                        dve.wait_ge(sort_differences, t + (c * COLS + 1))
                        dve.tensor_scalar(sort_less, sort_diff, bound[:, bass.ds(t, 1)], None, ALU.is_lt, ALU.add,
                                          accum_out=less[:, bass.ds(t, 1)]).then_inc(sort_counted, 1)
                    count(0)
                    with dve.Fori(1, COLS) as t:
                        count(t)
                    dve.wait_ge(sort_counted, (c + 1) * COLS)
                    if c:
                        link(dve.tensor_tensor(out=places, in0=places, in1=less, op=ALU.add))
                    else:
                        link(dve.tensor_copy(places, less))
                dve.tensor_copy(dst_idx[:, :], places).then_inc(sort_placed, 1)
                dve.wait_ge(sort_rows_in, 16)
                for i, to in enumerate((rows_i[:, 0, :], rows_i[:, 1, :], cols_f[:, 0, :], cols_f[:, 1, :])):
                    last = dve.tensor_copy(to, edge_rows[:, :, i])
                last.then_inc(sort_cast, 1)

            dst_c, next_c, src_c, rank_c = (cols_f[:, i, :] for i in range(4))

            def part(what):
                if what == "check":
                    dve.wait_ge(slot_made, 2)
                    link(dve.tensor_copy(init_f[:, :], init_i[:, :]))
                    dve.memset(node_init[:, :, 1], 0.0)
                    dve.tensor_copy(node_init[:, :, 0], init_f[:, 0:1].to_broadcast([P, INIT_COLS])).then_inc(init_set, 1)
                    dve.wait_ge(rows_in, 32)
                    link(dve.tensor_copy(rows_f[:, 0:2, :], rows_i[:, 0:2, :]))
                    dve.tensor_tensor(out=violations[:, :], in0=rows_f[:, 0, :], in1=rows_f[:, 1, :],
                                      op=ALU.is_gt).then_inc(violations_made, 1)
                if what == "sort":
                    with if_unsorted(dve):
                        sort()
                if what.startswith("runs"):
                    at = int(what[-1]) * CHUNKS // 2
                    for c in range(at, at + CHUNKS // 2):
                        runs(c)
                if what == "rows":
                    dve.wait_ge(rows_in, 96)
                    dve.tensor_copy(rows_f[:, 0:3, :], rows_i[:, :, :]).then_inc(rows_cast, 1)
                if what == "columns":
                    dve.wait_ge(cols_done, 1)
                    link(dve.tensor_copy(slot_f[:, :], slot_i[:, :]))
                    dve.tensor_scalar(tmp[:, 0, :], slot_f[:, :], float(N), None, ALU.add)
                    link(dve.tensor_tensor(out=tmp[:, 1, :], in0=next_c, in1=dst_c, op=ALU.not_equal))
                    link(dve.tensor_tensor(out=tmp[:, 2, :], in0=dst_c, in1=tmp[:, 0, :], op=ALU.subtract))
                    link(dve.tensor_tensor(out=tmp[:, 2, :], in0=tmp[:, 2, :], in1=tmp[:, 1, :], op=ALU.mult))
                    dve.tensor_tensor(out=scatter_idx[:, :], in0=tmp[:, 2, :], in1=tmp[:, 0, :], op=ALU.add)
                    dve.tensor_copy(scatter_val[:, :, 0], slot_f[:, :])
                    dve.tensor_copy(scatter_val[:, :, 1], rank_c)
                    dve.tensor_copy(dst_idx[:, :], dst_c)
                    dve.tensor_scalar(x_dst_idx[:, :], dst_c, float(N - 1), None, ALU.min)
                    dve.tensor_copy(src_idx[:, :], src_c).then_inc(index_made, 1)
                if what == "coefficients":
                    dve.wait_ge(tab_read, 2)
                    slot_s, deg_s, deg_d = of_src[:, :, 0], of_src[:, :, 1], of_dst[:, :, 1]
                    dve.tensor_copy(h_idx[:, :], slot_s)
                    dve.tensor_scalar(tmp[:, 1, :], deg_s, 0.0, None, ALU.is_gt)
                    link(dve.tensor_scalar(tmp[:, 0, :], deg_s, 1.0, None, ALU.max))
                    link(dve.scalar_tensor_tensor(out=tmp[:, 0, :], in0=deg_d, scalar=1.0, in1=tmp[:, 0, :],
                                                  op0=ALU.max, op1=ALU.mult))
                    rsqrt(tmp[:, 2, :], tmp[:, 0, :], rs_a[:SR, :], rs_b[:SR, :], link)
                    dve.scalar_tensor_tensor(out=coef[:, :], in0=tmp[:, 2, :], scalar=-1.0, in1=tmp[:, 1, :],
                                             op0=ALU.mult, op1=ALU.mult)
                    link(dve.scalar_tensor_tensor(out=tmp[:, 3, :], in0=slot_s, scalar=float(N), in1=src_c,
                                                  op0=ALU.add, op1=ALU.subtract))
                    link(dve.tensor_tensor(out=tmp[:, 3, :], in0=tmp[:, 3, :], in1=tmp[:, 1, :], op=ALU.mult))
                    dve.tensor_tensor(out=g_idx[:, :], in0=tmp[:, 3, :], in1=src_c, op=ALU.add).then_inc(coef_made, 1)

            def dense(first, n):
                def body(k, v, half):
                    run = not isinstance(k, int) or k < PAIRS
                    fol = not isinstance(k, int) or k > 0
                    mine = dense_blocks(k) if run else []
                    p = k - 1
                    prev = dense_blocks(p) if fol else []
                    for g in range(3):
                        for q, tiles, rows in prev:
                            c = tiles * rows
                            dve.wait_ge(u_ready, 6 * p + 2 * g + q + 1)
                            dve.scalar_tensor_tensor(out=g_t[q][g % 2][:, 0:c], in0=u_t[q][:, 0:c], scalar=SLOPE,
                                                     in1=u_t[q][:, 0:c], op0=ALU.mult, op1=ALU.max).then_inc(g_ready, 1)
                            if g == 2:
                                dve.wait_ge(g_ready, 6 * p + 2 * g + q + 1)
                                dve.tensor_tensor(out=z2_t[q][:, 0:c], in0=g_t[q][0][:, 0:c], in1=y_t[q][:, 0:c],
                                                  op=ALU.add).then_inc(z2_ready, 1)
                    for q, tiles, rows in mine:
                        c = tiles * rows
                        dve.wait_ge(y_mm, 2 * k + q + 1)
                        dve.scalar_tensor_tensor(out=z_t[q][:, 0:c], in0=mm[q][0][:, 0:c], scalar=b3_s[:, 0:1],
                                                 in1=x_t[q][v][:, 0:c], op0=ALU.add, op1=ALU.add).then_inc(z_ready, 1)
                    if mine:
                        layer_norm([(q, t, r, ga[q], y_rows[q]) for q, t, r in mine], ln1_link, k, ln1_done,
                                   lambda q: dve.wait_ge(z_turned, 2 * k + q + 1),
                                   lambda q: wait(dve, y_stored[q], 16 * k))
                    if prev:
                        layer_norm([(q, t, r, tr[q], out_rows[q]) for q, t, r in prev], ln2_link, p, ln2_done,
                                   lambda q: dve.wait_ge(z2_turned, 2 * p + q + 1),
                                   lambda q: wait(dve, out_stored[q], 16 * p))
                dense_run(dve, first, n, body)

            def phase(ph):
                n0 = ph * BLOCKS

                def body(s):
                    if at := s.block(0):
                        b, q, half = at
                        n = n0 + b
                        if ph in GIN:
                            dve.wait_ge(scale_done, n + 1)
                        else:
                            dve.wait_ge(turned, n + 1)
                        wait(dve, mm_done, n - 1)
                        wait(dve, scanned, n)
                        for i in range(2 if L1 < ph <= L5 else 1):
                            last = dve.tensor_tensor_scan(
                                agg[q][:, i, :], keep[:, bass.ds(SB * b, SB)],
                                msg[q][:, :] if ph in GIN else ga[i][:, 0:SB],
                                agg[1 - q][:, i, SB - 1:SB], ALU.mult, ALU.add)
                        last.then_inc(scanned, 1)
                        if ph in SPLIT:
                            m = n - L2 * BLOCKS
                            dve.wait_ge(state_high, m + 1)
                            dve.tensor_tensor(out=state_lo[q][:, :, :], in0=state[q][:, :, :], in1=state_hi[q][:, :, :].bitcast(f32),
                                              op=ALU.subtract).then_inc(low_made, 1)
                            dve.wait_ge(agg_high, m + 1)
                            dve.tensor_tensor(out=agg_lo[q][:, :, :], in0=agg[q][:, :, :],
                                              in1=agg_hi[q][:, :, :].bitcast(f32), op=ALU.subtract
                                              ).then_inc(low_made, 1)
                        if ph in GIN:
                            dve.wait_ge(scanned, n + 1)
                            if ph == G1:
                                dve.wait_ge(copied, BLOCKS + b + 1)
                            else:
                                dve.wait_ge(state_in[q], dma_count(STATE, ph, half))
                            own = res[q][:, :] if ph == G1 else state[q][:, 0, :]
                            dve.tensor_tensor(out=agg[q][:, 1, :], in0=agg[q][:, 0, :], in1=own,
                                              op=ALU.add).then_inc(summed, 1)
                    if at := s.block(1):
                        b, q, half = at
                        n = n0 + b
                        if ph == L5:
                            dve.wait_ge(mm_done, n + 1)
                            dve.wait_ge(res_in[q], dma_count(RES, ph, half))
                            wait(dve, back_turned, n - 1)
                            if isinstance(b, int) and b < 2:
                                dve.wait_ge(state_out[q], dma_count(STATE_OUT, L4, BLOCKS // 2 - 1))
                            dve.scalar_tensor_tensor(out=new[q][:, 0, :], in0=mm[q][0][:, 0:SB], scalar=b3_s[:, 0:1],
                                                     in1=res[q][:, :], op0=ALU.add, op1=ALU.add).then_inc(new_ready, 1)
                        elif ph in GIN:
                            dve.wait_ge(lin_done, n - G1 * BLOCKS + 1)
                            wait(dve, back_turned, n - 1)
                            if ph in STATE_OUT:
                                count = dma_count(STATE_OUT, ph, half - 1)
                            else:
                                count = dma_count(STATE_OUT, G2, BLOCKS // 2 - 1)
                            if ph in STATE_OUT or (isinstance(b, int) and b < 2):
                                dve.wait_ge(state_out[q], count)
                            last = dve.scalar_tensor_tensor(out=new[q][:, 0, :], in0=lin[q][:, :], scalar=SLOPE,
                                                            in1=lin[q][:, :], op0=ALU.mult, op1=ALU.max)
                            if ph == G3:
                                last.then_inc(new_half, 1)
                                dve.wait_ge(new_half, b + 1)
                                dve.wait_ge(res_in[q], dma_count(RES, ph, half))
                                last = dve.tensor_tensor(out=new[q][:, 1, :], in0=new[q][:, 0, :],
                                                         in1=res[q][:, :], op=ALU.add)
                            last.then_inc(new_ready, 1)
                    if at := s.block(2):
                        b, q, half = at
                        n = n0 + b
                        def free(_):
                            if ph == G3:
                                if isinstance(b, int) and b < 2:
                                    dve.wait_ge(rows_out[q], dma_count(ROWS_OUT, G2, BLOCKS // 2 - 1))
                                else:
                                    dve.wait_ge(out_scattered[q], 16 * ST * half)
                            else:
                                wait(dve, rows_out[q], dma_count(ROWS_OUT, ph, half - 1))
                                if ph == L1 and isinstance(b, int) and b < 2:
                                    for g in range(2):
                                        dve.wait_ge(g_stored[g][q], 16 * PAIRS)
                        if ph in (L5, G3):
                            layer_norm([(0, ST, SR, tr[0], new_rows[q])], ln_slot_link,
                                       b + (ph == G3) * BLOCKS, rows_ready,
                                       lambda _: dve.wait_ge(back_turned, n + 1), free)
                        else:
                            dve.wait_ge(back_turned, n + 1)
                            free(q)
                            for i in range(2 if ph in HIDDEN else 1):
                                last = dve.tensor_copy(
                                    new_rows[q][:, :, i * D:(i + 1) * D],
                                    tr[i][:SR, 0:ST * D].rearrange("p (j f) -> p j f", f=D))
                            last.then_inc(rows_ready, 1)
                leave()
                if ph == L1:
                    for t in agg:
                        last = dve.memset(t[:, :, :], 0.0)
                    last.then_inc(agg_zero, 1)
                    dve.wait_ge(agg_zero, 1)
                phase_run(dve, body)

            schedule(dense, phase, part)


def kernel(x, src, dst, edge_attr_2, L0_gnn_W1, L0_gnn_b1, L0_gnn_W2, L0_gnn_b2, L0_gnn_W3, L0_gnn_b3,
           L1_gnn_Wl, L1_gnn_bl, L1_gnn_W, L1_gnn_b):
    import numpy as np
    import concourse.bacc as bacc
    from concourse import mybir as mb
    from concourse.bass_utils import run_bass_kernel_spmd

    nc = bacc.Bacc("TRN2", target_bir_lowering=False, num_devices=1)
    given = {
        "x": x, "x_turned": np.asarray(x).T, "src": src, "dst": dst, "attr_t": np.asarray(edge_attr_2).T,
        "w1": L0_gnn_W1, "b1": L0_gnn_b1, "w2": L0_gnn_W2, "b2": L0_gnn_b2, "w3": L0_gnn_W3, "b3": L0_gnn_b3,
        "wl": L1_gnn_Wl, "bl": L1_gnn_bl, "wg": L1_gnn_W, "bg": L1_gnn_b,
    }
    arrays, args = {}, []
    for name, a in given.items():
        a = np.ascontiguousarray(a)
        arrays[f"in_{name}"] = a
        args.append(nc.dram_tensor(f"in_{name}", a.shape, mb.dt.from_np(a.dtype), kind="ExternalInput").ap())
    args.append(nc.dram_tensor("out_x", (TAB_ROWS, D), mb.dt.float32, kind="ExternalOutput").ap())
    gnn_kernel(nc, *args)
    r = run_bass_kernel_spmd(nc, [arrays], core_ids=[0])
    return r.results[0]["out_x"][:N]
```

```python
import concourse.bass as bass
from concourse import mybir
from contextlib import ExitStack

N = 50000
E = 12500
D = 128
H = 256
P = 128

DT, DR = 4, 128
DB = DT * DR
PAIRS = (N // DB + 1) // 2
TAIL_T, TAIL_R = 3, 112
ST, SR = 4, 112
SB = ST * SR
EP = -(-E // SB) * SB
BLOCKS = EP // SB
COLS = EP // SR
assert COLS == SR and BLOCKS % 2 == 0
assert (2 * PAIRS - 1) * DB + TAIL_T * TAIL_R == N

PAD_NODE = N + EP
TAB_ROWS = N + EP + 2
ZERO_ROW = EP
CHUNK = 8 * SR
CHUNKS = EP // CHUNK
assert EP % CHUNK == 0
INIT_COLS = -(-TAB_ROWS // P)
EPS = 1e-5
SLOPE = 0.01
MAGIC = float(0x5F3759DF)
NEWTON = 3
RSQRT_LINKS = 2 + 3 * NEWTON
LN_LINKS = 3 + RSQRT_LINKS

L1, L2, L3, L4, L5, G1, G2, G3 = range(8)
PHASES = 8
HIDDEN = (L1, L2, L3, L4)
GIN = (G1, G2, G3)
SPLIT = (L2, L3, L4)

PARTS = ({"check": 1, "flag": 2, "sort": 3} | {f"runs{i}": 4 + i for i in range(CHUNKS)}
         | {"rows": 4 + CHUNKS, "columns": 5 + CHUNKS, "coefficients": 35})

PLACE = 2.0 ** -14
assert EP < 1 / PLACE


def gnn_kernel(nc, x, x_turned, src, dst, attr_t, w1, b1, w2, b2, w3, b3, wl, bl, wg, bg, out):
    f32, f32r, bf16, i32 = mybir.dt.float32, mybir.dt.float32r, mybir.dt.bfloat16, mybir.dt.int32
    ALU = mybir.AluOpType
    ACT = mybir.ActivationFunctionType

    ctx = ExitStack()
    with ctx:
        def sb(name, shape, dt=f32):
            return ctx.enter_context(nc.sbuf_tensor(name, shape, dt))

        def sem(name):
            return ctx.enter_context(nc.semaphore(name))

        def sems(name):
            return [sem(f"{name}{q}") for q in range(2)]

        def dram(name, shape, dt=f32):
            return nc.dram_tensor(name, shape, dt, kind="Internal").ap()

        def wait(eng, s, count):
            if not (isinstance(count, int) and count <= 0):
                eng.wait_ge(s, count)

        dst_x = dram("dst_x", (EP + 2,), i32)
        src_x = dram("src_x", (EP,), i32)
        attr_x = dram("attr_x", (3, EP))
        rank_x = dram("rank_x", (EP,))
        node_tab = dram("node_tab", (P * INIT_COLS, 2))
        own_x = dram("own_x", (EP, 2 * D))
        sorted_x = dram("sorted_x", (EP, 4))
        h_tab = [dram(f"h_tab{i}", (EP + P, H)) for i in range(2)]
        g_tab = [dram(f"g_tab{i}", (N + EP, D)) for i in range(3)]
        state_x = dram("state_x", (BLOCKS, P, 2, SB))
        res_x = dram("res_x", (2, BLOCKS, P, SB))

        ident = sb("ident", [P, P])
        w1_s = sb("w1_s", [P, 2, H])
        w2_s = sb("w2_s", [P, 4, H])
        w3_s = sb("w3_s", [P, 4, D])
        wg_s = sb("wg_s", [P, 3, D])
        wl_s = sb("wl_s", [3, 3, D])
        b1_s = sb("b1_s", [P, 2])
        b2_s = sb("b2_s", [P, 2])
        b3_s = sb("b3_s", [P, 1])
        bg_s = sb("bg_s", [P, 3])
        ones = sb("ones", [1, CHUNK])
        w1_hi = sb("w1_hi", [P, H], f32r)
        w1_lo = sb("w1_lo", [P, H], f32r)
        w2_hi = sb("w2_hi", [P, 4, H], f32r)
        w2_lo = sb("w2_lo", [P, 4, H], f32r)
        zero_rows = sb("zero_rows", [P, H])

        keep = sb("keep", [P, EP], bf16)
        dst_chunk = sb("dst_chunk", [P, CHUNK + 1], i32)
        rank_row = sb("rank_row", [1, 2, CHUNK])
        init_i = sb("init_i", [P, 1], i32)
        init_f = sb("init_f", [P, 1])
        node_init = sb("node_init", [P, INIT_COLS, 2])
        rows_i = sb("rows_i", [SR, 3, COLS], i32)
        rows_f = sb("rows_f", [SR, 4, COLS])
        cols_f = sb("cols_f", [SR, 4, COLS])
        slot_i = sb("slot_i", [SR, COLS], i32)
        slot_f = sb("slot_f", [SR, COLS])
        tmp = sb("tmp", [SR, 4, COLS])
        scatter_idx = sb("scatter_idx", [SR, COLS], i32)
        scatter_val = sb("scatter_val", [SR, COLS, 2])
        dst_idx = sb("dst_idx", [SR, COLS], i32)
        x_dst_idx = sb("x_dst_idx", [SR, COLS], i32)
        src_idx = sb("src_idx", [SR, COLS], i32)
        of_dst = sb("of_dst", [SR, COLS, 2])
        of_src = sb("of_src", [SR, COLS, 2])
        coef = sb("coef", [SR, COLS])
        h_idx = sb("h_idx", [SR, COLS], i32)
        g_idx = sb("g_idx", [SR, COLS], i32)
        idx_now = [sb(f"idx_now{q}", [SR, 2 * ST], i32) for q in range(2)]
        carrier = sb("carrier", [1, 1])
        out_idx = [sb(f"out_idx{q}", [SR, ST], i32) for q in range(2)]
        tab_now = [sb(f"tab_now{q}", [SR, 2 * ST, 2]) for q in range(2)]
        violations = sb("violations", [SR, COLS])
        column_of_ones = sb("column_of_ones", [P, 1])
        flag_row = sb("flag_row", [1, COLS])
        flag_f = sb("flag_f", [1, 1])
        flag_i = sb("flag_i", [1, 1], i32)
        rs_a = sb("rs_a", [P, COLS])
        rs_b = sb("rs_b", [P, COLS])

        x_t = [[sb(f"x_t{q}{v}", [P, DB]) for v in range(2)] for q in range(2)]
        h_t = [sb(f"h_t{q}", [P, 2, DB]) for q in range(2)]
        x_hi = [sb(f"x_hi{q}", [P, DB], f32r) for q in range(2)]
        x_lo = [sb(f"x_lo{q}", [P, DB], f32r) for q in range(2)]
        high = [sb(f"high{q}", [P, 2, DB], f32r) for q in range(2)]
        low = [sb(f"low{q}", [P, 2, DB], f32r) for q in range(2)]
        z_t = [sb(f"z_t{q}", [P, DB]) for q in range(2)]
        y_rows = [sb(f"y_rows{q}", [P, DT, D]) for q in range(2)]
        y_t = [sb(f"y_t{q}", [P, DB]) for q in range(2)]
        u_t = [sb(f"u_t{q}", [P, DB]) for q in range(2)]
        g_t = [[sb(f"g_t{q}{v}", [P, DB]) for v in range(2)] for q in range(2)]
        g_rows_pair = [sb(f"g_rows_pair{q}", [P, 2 * DT, D]) for q in range(2)]
        g_rows = [[g_rows_pair[q][:, g * DT:(g + 1) * DT, :] for q in range(2)] for g in range(2)]
        z2_t = [sb(f"z2_t{q}", [P, DB]) for q in range(2)]
        out_rows = [sb(f"out_rows{q}", [P, DT, D]) for q in range(2)]
        stats = sb("stats", [P, 4 * DT, 6])
        mean_var = sb("mean_var", [P, 4 * DT, 2])
        rstd = sb("rstd", [P, 4 * DT])
        shift = sb("shift", [P, 4 * DT])
        ln_a = sb("ln_a", [P, 4 * DT])
        ln_b = sb("ln_b", [P, 4 * DT])

        got = [sb(f"got{q}", [SR, ST, H]) for q in range(2)]
        scaled = [sb(f"scaled{q}", [SR, ST, H]) for q in range(2)]
        state = [sb(f"state{q}", [P, 2, SB]) for q in range(2)]
        res = [u_t[q][:, 0:SB] for q in range(2)]
        agg = [h_t[q][:, :, 0:SB] for q in range(2)]
        state_hi = [high[q][:, :, 0:SB] for q in range(2)]
        state_lo = [low[q][:, :, 0:SB] for q in range(2)]
        agg_hi, agg_lo = ([sb(f"{name}{q}", [P, 2, SB], f32r) for q in range(2)]
                          for name in ("agg_hi", "agg_lo"))
        new = [sb(f"new{q}", [P, 2, SB]) for q in range(2)]
        lin = [z_t[q][:, 0:SB] for q in range(2)]
        msg = [y_t[q][:, 0:SB] for q in range(2)]
        attr = [z2_t[q][0:3, 0:SB] for q in range(2)]
        new_rows = [g_rows_pair[q][:SR, :, :].rearrange("p (j a) f -> p j (a f)", a=2) for q in range(2)]

        mm = [[ctx.enter_context(nc.psum_tensor(f"mm{q}{i}", [P, 512], f32)) for i in range(2)]
              for q in range(2)]
        ga = [ctx.enter_context(nc.psum_tensor(f"ga{i}", [P, 512], f32)) for i in range(2)]
        tr = [ctx.enter_context(nc.psum_tensor(f"tr{i}", [P, 512], f32)) for i in range(2)]

        weights_in = sem("weights_in")
        scratch_in = sem("scratch_in")
        pads_set = sem("pads_set")
        pads_in = sem("pads_in")
        ident_zero, ident_set = sem("ident_zero"), sem("ident_set")
        chunk_in, keep_done = sem("chunk_in"), sem("keep_done")
        rank_done, rank_out = sem("rank_done"), [sem(f"rank_out{q}") for q in range(2)]
        init_set, init_out = sem("init_set"), sem("init_out")
        rows_in, rows_cast = sem("rows_in"), sem("rows_cast")
        cols_t, cols_done = sem("cols_t"), sem("cols_done")
        dve_link = sem("dve_link")
        slot_made, index_made = sem("slot_made"), sem("index_made")
        scattered, tab_got = sems("scattered"), sems("tab_got")
        staged, out_staged = sem("staged"), sem("out_staged")
        tab_read = sem("tab_read")
        coef_made = sem("coef_made")
        pe_left, act_left, dve_left = sem("pe_left"), sem("act_left"), sem("dve_left")

        x_loaded = [sems(f"x_loaded{q}") for q in range(2)]
        violations_made, violations_summed = sem("violations_made"), sem("violations_summed")
        flag_summed, flag_made = sem("flag_summed"), sem("flag_made")
        pre_in, pre_out = sems("pre_in"), sems("pre_out")
        sort_cols_in, sort_chunk_in, sort_chunk_read = sem("sort_cols_in"), sem("sort_chunk_in"), sem("sort_chunk_read")
        sort_iota, sort_link, sort_differences, sort_counted = (
            sem("sort_iota"), sem("sort_link"), sem("sort_differences"), sem("sort_counted"))
        sort_placed, sort_staged, sort_scattered = sem("sort_placed"), sem("sort_staged"), sem("sort_scattered")
        sort_rows_in, sort_cast, sort_stored = sem("sort_rows_in"), sem("sort_cast"), sem("sort_stored")
        layer_mm, h_ready = sem("layer_mm"), sem("h_ready")
        y_mm, z_ready, z_turned, ln1_done = sem("y_mm"), sem("z_ready"), sem("z_turned"), sem("ln1_done")
        y_turned, y_t_ready = sem("y_turned"), sem("y_t_ready")
        g_mm, u_ready, g_ready = sem("g_mm"), sem("u_ready"), sem("g_ready")
        g_turned, g_rows_ready = sem("g_turned"), sem("g_rows_ready")
        z2_ready, z2_turned, ln2_done = sem("z2_ready"), sem("z2_turned"), sem("ln2_done")
        ln_dense_link, ln_slot_link = sem("ln_dense_link"), sem("ln_slot_link")
        y_stored, out_stored = sems("y_stored"), sems("out_stored")
        g_stored = [sems(f"g_stored{g}") for g in range(2)]

        got_in, own_in, attr_in = sems("got_in"), sems("own_in"), sems("attr_in")
        state_in, res_in = sems("state_in"), sems("res_in")
        scale_done, turned, copied, scanned = sem("scale_done"), sem("turned"), sem("copied"), sem("scanned")
        summed = sem("summed")
        agg_zero = sem("agg_zero")
        x_high, x_split = sem("x_high"), sem("x_split")
        weights_high, weights_split, h_low = sem("weights_high"), sem("weights_split"), sem("h_low")
        state_high, agg_high, low_made = sem("state_high"), sem("agg_high"), sem("low_made")
        mm_done, lin_done, new_half, new_ready = sem("mm_done"), sem("lin_done"), sem("new_half"), sem("new_ready")
        back_turned, rows_ready, norm_made = sem("back_turned"), sem("rows_ready"), sem("norm_made")
        state_out, res_out, rows_out, out_scattered = (
            sems("state_out"), sems("res_out"), sems("rows_out"), sems("out_scattered"))

        block = ctx.enter_context(nc.Block())

        PADS = 4 + 2 + EP // CHUNK + 2

        flat = lambda t: t[:, :, :].rearrange("p j f -> p (j f)")[:, 0:CHUNK]
        sort_dst, sort_place, sort_diff, sort_less = flat(got[0]), flat(got[1]), flat(scaled[0]), flat(scaled[1])
        sort_iota_i = keep[:SR, 0:2 * CHUNK].bitcast(i32)
        edge_cols = state[0][:SR, 0, :].rearrange("p (t w) -> p t w", w=4)
        edge_rows = state[1][:SR, 0, :].rearrange("t (p w) -> t p w", w=4)

        def if_unsorted(eng):
            eng.wait_ge(flag_made, 1)
            return eng.If(eng.value_load(flag_i[0:1, 0:1]) > 0)

        def dense_blocks(k):
            if isinstance(k, int) and k == PAIRS - 1:
                return [(0, DT, DR), (1, TAIL_T, TAIL_R)]
            return [(0, DT, DR), (1, DT, DR)]

        def dense_view(table, k, q, tiles, rows):
            if tiles == DT:
                whole = table[0:(2 * PAIRS - 1) * DB, :]
                return whole.rearrange("(b j p) f -> b p j f", p=DR, j=DT)[2 * k + q]
            return table[N - tiles * rows:N, :].rearrange("(j p) f -> p j f", p=rows)

        def dense_run(eng, first, n, body):
            steps = list(range(first, first + n))

            def alone():
                k = steps.pop(0)
                body(k, k % 2, k // 2)

            while steps and (steps[0] < 2 or steps[0] % 2):
                alone()
            twos = max(0, (min(first + n, PAIRS - 2) - first - n + len(steps)) // 2)
            if twos:
                half = steps[0] // 2
                with eng.Fori(half, half + twos) as i:
                    body(2 * i, 0, i)
                    body(2 * i + 1, 1, i)
                del steps[:2 * twos]
            while steps:
                alone()

        class Step:

            def __init__(self, i, par):
                self.i, self.par = i, par

            def block(self, lag):
                par, half = (self.par - lag) % 2, self.i + (self.par - lag) // 2
                b = 2 * half + par
                if isinstance(b, int) and not 0 <= b < BLOCKS:
                    return None
                return b, par, half

        def phase_run(eng, body, more=0):
            peeled = 2 + more
            for s in range(-1, 2 * peeled):
                body(Step(s // 2, s % 2))
            with eng.Fori(peeled, BLOCKS // 2 - 1) as i:
                body(Step(i, 0))
                body(Step(i, 1))
            for s in range(BLOCKS - 2, BLOCKS + 2 + more):
                body(Step(s // 2, s % 2))

        def dma_count(per_block, phase, half):
            before = sum(per_block.get(p, 0) for p in range(phase)) * (BLOCKS // 2)
            return 16 * (before + per_block[phase] * (half + 1))

        GOT = {p: 4 for p in range(PHASES)} | {L1: 1}
        ONCE_L1_G1 = {L1: 1, G1: 1}
        STATE = {L2: 1, L3: 1, L4: 1, L5: 1, G2: 1, G3: 1}
        STATE_OUT = {L1: 1, L2: 1, L3: 1, L4: 1, G1: 1, G2: 1}
        RES = {L5: 1, G3: 1}
        ROWS_OUT = {p: 1 for p in range(G3)}
        GIN_ONCE = {G1: 1, G2: 1, G3: 1}

        def schedule(dense, phase, part):
            k = 0
            for what, upto in PARTS.items():
                dense(k, upto - k)
                k = upto
                part(what)
            dense(k, PAIRS + 1 - k)
            for p in range(PHASES):
                phase(p)

        class Turnstile:

            def __init__(self, eng, mine):
                self.eng, self.mine, self.n = eng, mine, 0

            def __call__(self):
                self.n += 1
                self.eng.drain().then_inc(self.mine, 1)
                for s in (pe_left, act_left, dve_left):
                    self.eng.wait_ge(s, self.n)

        @block.sync
        def _(sp):
            for tile, view in (
                (w1_s[:, :, :], w1.rearrange("(k p) n -> p k n", p=P)),
                (w2_s[:, :, :], w2.rearrange("(k p) n -> p k n", p=P)),
                (w3_s[:, :, :], w3.rearrange("(k p) n -> p k n", p=P)),
                (wg_s[:, :, :], wg.rearrange("l p n -> p l n")),
                (wl_s[0:2, :, :], wl.rearrange("l p n -> p l n")),
                (wl_s[2:3, :, :], bl.rearrange("(a l) n -> a l n", a=1)),
                (b1_s[:, :], b1.rearrange("(k p) -> p k", p=P)),
                (b2_s[:, :], b2.rearrange("(k p) -> p k", p=P)),
                (b3_s[:, :], b3.rearrange("(k p) -> p k", p=P)),
                (bg_s[:, :], bg.rearrange("l p -> p l")),
            ):
                with nc.allow_non_contiguous_dma(reason="a few hundred words of biases"):
                    sp.dma_start(tile, view).then_inc(weights_in, 16)
            row = lambda a: a.rearrange("(a n) -> a n", a=1)
            square = lambda a: a.rearrange("(t p) -> t p", p=SR)
            pad = EP - E

            def edges():
                sp.dma_start(row(dst_x[1:1 + E]), row(dst)).then_inc(scratch_in, 16)
                sp.dma_start(row(src_x[0:E]), row(src)).then_inc(scratch_in, 16)
                sp.dma_start(attr_x[0:2, 0:E], attr_t).then_inc(scratch_in, 16)
                sp.wait_ge(pads_set, 5)
                sp.dma_start(row(dst_x[0:1]), slot_i[0:1, 0:1]).then_inc(pads_in, 16)
                sp.dma_start(row(dst_x[1 + E:1 + EP]), dst_chunk[0:1, 0:pad]).then_inc(pads_in, 16)
                sp.dma_start(row(dst_x[1 + EP:2 + EP]), x_dst_idx[0:1, 0:1]).then_inc(pads_in, 16)
                sp.dma_start(row(src_x[E:EP]), src_idx[0:1, 0:pad]).then_inc(pads_in, 16)
                for r in range(2):
                    sp.dma_start(attr_x[r:r + 1, E:EP], ones[0:1, 0:pad]).then_inc(pads_in, 16)
                for c in range(CHUNKS):
                    sp.dma_start(attr_x[2:3, c * CHUNK:(c + 1) * CHUNK], ones[:, :]).then_inc(pads_in, 16)
                for t in h_tab:
                    sp.dma_start(t[EP:EP + P, :], zero_rows[:, :]).then_inc(pads_in, 16)
                sp.wait_ge(scratch_in, 48)
                sp.wait_ge(pads_in, 16 * PADS)
                dst_rows()
                sp.wait_ge(init_set, 1)
                sp.dma_start(node_tab.rearrange("(p c) w -> p c w", p=P),
                             node_init[:, :, :]).then_inc(init_out, 16)

            def dst_rows():
                sp.dma_start(rows_i[:, 0, :], square(dst_x[1:1 + EP])).then_inc(rows_in, 16)
                sp.dma_start(rows_i[:, 1, :], square(dst_x[2:2 + EP])).then_inc(rows_in, 16)

            def load_chunk(c):
                wait(sp, keep_done, c)
                sp.dma_start(dst_chunk[:, :],
                             row(dst_x[c * CHUNK:(c + 1) * CHUNK + 1]).to_broadcast([P, CHUNK + 1])
                             ).then_inc(chunk_in, 16)

            def put_ranks(c):
                sp.wait_ge(rank_done, c + 1)
                sp.dma_start(row(rank_x[c * CHUNK:(c + 1) * CHUNK]),
                             rank_row[:, c % 2, :]).then_inc(rank_out[c % 2], 16)

            def sort():
                column = lambda a: a.rearrange("(t p) -> p t", p=SR)
                with nc.allow_non_contiguous_dma(reason="the edges' tables by column, once"):
                    for to, of in ((rows_i[:, 0, :], dst_x[1:1 + EP]), (rows_i[:, 1, :], src_x[0:EP]),
                                   (cols_f[:, 0, :], attr_x[0]), (cols_f[:, 1, :], attr_x[1])):
                        sp.dma_start(to, column(of)).then_inc(sort_cols_in, 16)
                for c in range(CHUNKS):
                    wait(sp, sort_chunk_read, c)
                    at = 1 + c * CHUNK
                    sp.dma_start(dst_chunk[:, 0:CHUNK],
                                 row(dst_x[at:at + CHUNK]).to_broadcast([P, CHUNK])
                                 ).then_inc(sort_chunk_in, 16)
                sp.wait_ge(sort_scattered, 16 * COLS)
                sp.dma_start(edge_rows, sorted_x.rearrange("(t p) w -> t p w", p=SR)).then_inc(sort_rows_in, 16)
                sp.wait_ge(sort_cast, 1)
                for to, of in ((dst_x[1:1 + EP], rows_i[:, 0, :]), (src_x[0:EP], rows_i[:, 1, :]),
                               (attr_x[0], cols_f[:, 0, :]), (attr_x[1], cols_f[:, 1, :])):
                    sp.dma_start(square(to), of).then_inc(sort_stored, 16)
                sp.wait_ge(sort_stored, 64)

            def part(what):
                if what == "check":
                    edges()
                if what == "sort":
                    with if_unsorted(sp):
                        sort()
                if what.startswith("runs"):
                    c = int(what[4:])
                    if c == 0:
                        load_chunk(0)
                    if c + 1 < CHUNKS:
                        load_chunk(c + 1)
                    put_ranks(c)
                if what == "rows":
                    dst_rows()
                    sp.dma_start(rows_i[:, 2, :], square(src_x[0:EP])).then_inc(rows_in, 16)
                    for q in range(2):
                        sp.wait_ge(rank_out[q], 16 * CHUNKS // 2)
                    sp.dma_start(rows_f[:, 3, :], square(rank_x[0:EP])).then_inc(rows_in, 16)

            def load_x(k, v):
                for q, tiles, rows in dense_blocks(k):
                    wait(sp, z_ready, 2 * k + q - 3)
                    if tiles == DT:
                        of = x_turned[:, 0:(2 * PAIRS - 1) * DB].rearrange("f (b c) -> b f c", c=DB)[2 * k + q]
                    else:
                        of = x_turned[:, N - tiles * rows:N]
                    sp.dma_start(x_t[q][v][:, 0:tiles * rows], of).then_inc(x_loaded[q][v], 16)

            def dense(first, n):
                def body(k, v, half):
                    if isinstance(k, int) and k == 0:
                        load_x(0, 0)
                        load_x(1, 1)
                        return
                    if not isinstance(k, int) or k < PAIRS - 1:
                        load_x(k + 1, 1 - v)
                    p = k - 1
                    for q, tiles, rows in dense_blocks(p):
                        sp.wait_ge(ln1_done, 2 * p + q + 1)
                        sp.dma_start(dense_view(g_tab[0], p, q, tiles, rows),
                                     y_rows[q][:rows, :tiles, :]).then_inc(y_stored[q], 16)
                    for g in range(2):
                        for q, tiles, rows in dense_blocks(p):
                            sp.wait_ge(g_rows_ready, 4 * p + 2 * g + q + 1)
                            sp.dma_start(dense_view(g_tab[1 + g], p, q, tiles, rows),
                                         g_rows[g][q][:rows, :tiles, :]).then_inc(g_stored[g][q], 16)
                    for q, tiles, rows in dense_blocks(p):
                        sp.wait_ge(ln2_done, 2 * p + q + 1)
                        sp.dma_start(dense_view(out, p, q, tiles, rows),
                                     out_rows[q][:rows, :tiles, :]).then_inc(out_stored[q], 16)
                dense_run(sp, first, n, body)

            def phase(ph):
                n0 = ph * BLOCKS

                def rows_of(b, table, base, width):
                    whole = table[base:base + EP, :].rearrange("(b j p) f -> b p j f", j=ST, p=SR)
                    return whole[b]

                def body(s):
                    if at := s.block(-1):
                        b, q, half = at
                        n = n0 + b
                        if ph == G1 and isinstance(b, int) and b < 2:
                            for r in range(2):
                                sp.wait_ge(rows_out[r], dma_count(ROWS_OUT, L5, BLOCKS // 2 - 1))
                        if ph in GIN:
                            wait(sp, turned, n - 1)
                            sp.dma_start(attr[q][:, :], attr_x[:, :].rearrange(
                                "r (b c) -> b r c", c=SB)[b]).then_inc(attr_in[q], 16)
                        if ph == G1:
                            sp.dma_start(scaled[q][:, :, 0:D],
                                         rows_of(b, g_tab[0], N, D)).then_inc(own_in[q], 16)
                        if ph in STATE:
                            if isinstance(b, int) and b < 2:
                                prev = max(p for p in STATE_OUT if p < ph)
                                sp.wait_ge(state_out[q], dma_count(STATE_OUT, prev, BLOCKS // 2 - 1))
                            wait(sp, mm_done, n - 1)
                            parts = 1 if ph in GIN else 2
                            sp.dma_start(state[q][:, 0:parts, :],
                                         state_x[b, :, 0:parts, :]).then_inc(state_in[q], 16)
                        if ph in RES:
                            if isinstance(b, int) and b < 2:
                                sp.wait_ge(res_out[q], dma_count(ONCE_L1_G1, L1 if ph == L5 else G1,
                                                                 BLOCKS // 2 - 1))
                            wait(sp, new_ready, n - 1)
                            sp.dma_start(res[q][:, :], res_x[ph == G3, b]).then_inc(res_in[q], 16)
                    if at := s.block(2):
                        b, q, half = at
                        if ph in ONCE_L1_G1:
                            sp.wait_ge(copied, ((ph == G1) * BLOCKS) + b + 1)
                            sp.dma_start(res_x[ph == G1, b], res[q][:, :]).then_inc(res_out[q], 16)
                        if ph in STATE_OUT:
                            parts = 1 if ph in GIN else 2
                            sp.wait_ge(new_ready, n0 + b + 1)
                            sp.dma_start(state_x[b, :, 0:parts, :],
                                         new[q][:, 0:parts, :]).then_inc(state_out[q], 16)
                    if at := s.block(3):
                        b, q, half = at
                        if ph in ROWS_OUT:
                            sp.wait_ge(rows_ready, n0 + b + 1)
                            if ph in HIDDEN:
                                to = rows_of(b, h_tab[ph % 2], 0, H)
                                sp.dma_start(to, new_rows[q][:, :, :]).then_inc(rows_out[q], 16)
                            else:
                                to = rows_of(b, g_tab[ph - L5], N, D)
                                sp.dma_start(to, new_rows[q][:, :, 0:D]).then_inc(rows_out[q], 16)
                phase_run(sp, body, more=1)

            schedule(dense, phase, part)
            for q in range(2):
                sp.wait_ge(out_scattered[q], 16 * 4 * BLOCKS // 2)
                sp.wait_ge(out_stored[q], 16 * PAIRS)

        @block.gpsimd
        def _(pool):
            pool.memset(ident[:, :], 0.0).then_inc(ident_zero, 1)
            pool.wait_ge(ident_zero, 1)
            pool.affine_select(out=ident[:, :], in_=ident[:, :], compare_op=ALU.not_equal, fill=1.0,
                               base=0, pattern=[[-1, P]], channel_multiplier=1).then_inc(ident_set, 1)
            pool.memset(slot_i[:, :], -1).then_inc(pads_set, 1)
            pool.memset(dst_chunk[:, :], PAD_NODE).then_inc(pads_set, 1)
            pool.memset(src_idx[:, :], 0).then_inc(pads_set, 1)
            pool.memset(x_dst_idx[:, :], PAD_NODE + 1).then_inc(pads_set, 1)
            pool.memset(zero_rows[:, :], 0.0)
            pool.memset(carrier[:, :], 0.0)
            pool.memset(ones[:, :], 1.0).then_inc(pads_set, 1)
            pool.iota(init_i[:, :], pattern=[[0, 1]], base=ZERO_ROW, channel_multiplier=1
                      ).then_inc(slot_made, 1)
            pool.wait_ge(pads_in, 16 * PADS)
            pool.iota(slot_i[:, :], pattern=[[SR, COLS]], base=0, channel_multiplier=1
                      ).then_inc(slot_made, 1)

            def gather(to, table, index, done):
                pool.indirect_dma_start(out=to, out_offset=None, in_=table,
                                        in_offset=bass.IndirectOffsetOnAxis(ap=index, axis=0)
                                        ).then_inc(done, 16)

            def scatter(table, index, of, done):
                pool.indirect_dma_start(out=table, in_=of, in_offset=None,
                                        out_offset=bass.IndirectOffsetOnAxis(ap=index, axis=0)
                                        ).then_inc(done, 16)

            def settled(done, count):
                pool.wait_ge(done, count)
                if not isinstance(count, int):
                    pool.tensor_tensor(out=carrier[:, :], in0=carrier[:, :], in1=carrier[:, :], op=ALU.add)

            def sort():
                pool.iota(sort_iota_i, pattern=[[1, CHUNK]], base=0, channel_multiplier=0
                          ).then_inc(sort_iota, 1)
                pool.wait_ge(sort_placed, 1)
                rows = tab_now[0][:, :, :].rearrange("p (j a) w -> p j (a w)", a=2)

                def put(b):
                    wait(pool, sort_scattered, 16 * ST * b)
                    pool.tensor_copy(idx_now[0][:, 0:ST], dst_idx[:, bass.ds(ST * b, ST)])
                    pool.tensor_copy(rows, edge_cols[:, bass.ds(ST * b, ST), :]).then_inc(sort_staged, 1)
                    settled(sort_staged, b + 1)
                    for j in range(ST):
                        scatter(sorted_x, idx_now[0][:, j:j + 1], rows[:, j, :], sort_scattered)
                put(0)
                with pool.Fori(1, BLOCKS) as b:
                    put(b)
                pool.wait_ge(sort_scattered, 16 * COLS)

            def part(what):
                if what == "sort":
                    with if_unsorted(pool):
                        sort()
                if what == "columns":
                    pool.wait_ge(index_made, 1)
                    pool.wait_ge(init_out, 16)
                    def put(i):
                        for q in range(2):
                            b = 2 * i + q
                            wait(pool, scattered[q], 16 * ST * i)
                            pool.tensor_copy(idx_now[q][:, 0:ST], scatter_idx[:, bass.ds(ST * b, ST)])
                            pool.tensor_copy(tab_now[q][:, 0:ST, :], scatter_val[:, bass.ds(ST * b, ST), :]
                                             ).then_inc(staged, 1)
                            pool.wait_ge(init_out, 16)
                            settled(staged, b + 1)
                            for j in range(ST):
                                scatter(node_tab, idx_now[q][:, j:j + 1], tab_now[q][:, j, :], scattered[q])
                    put(0)
                    with pool.Fori(1, BLOCKS // 2) as i:
                        put(i)
                    for q in range(2):
                        pool.wait_ge(scattered[q], 16 * ST * BLOCKS // 2)

                    def read(q, b):
                        pool.tensor_copy(of_dst[:, bass.ds(ST * b, ST), :], tab_now[q][:, 0:ST, :])
                        return pool.tensor_copy(of_src[:, bass.ds(ST * b, ST), :], tab_now[q][:, ST:2 * ST, :])

                    def get(i):
                        for q in range(2):
                            b = 2 * i + q
                            if not isinstance(i, int):
                                pool.wait_ge(tab_got[q], 16 * 2 * ST * i)
                                read(q, b - 2)
                            pool.tensor_copy(idx_now[q][:, 0:ST], dst_idx[:, bass.ds(ST * b, ST)])
                            pool.tensor_copy(idx_now[q][:, ST:2 * ST], src_idx[:, bass.ds(ST * b, ST)]
                                             ).then_inc(staged, 1)
                            pool.wait_ge(scattered[q], 16 * ST * BLOCKS // 2)
                            settled(staged, BLOCKS + b + 1)
                            for j in range(2 * ST):
                                gather(tab_now[q][:, j, :], node_tab, idx_now[q][:, j:j + 1], tab_got[q])
                    get(0)
                    with pool.Fori(1, BLOCKS // 2) as i:
                        get(i)
                    for q in range(2):
                        pool.wait_ge(tab_got[q], 16 * 2 * ST * BLOCKS // 2)
                        read(q, BLOCKS - 2 + q).then_inc(tab_read, 1)

                    def ends(i):
                        for q in range(2):
                            b = 2 * i + q
                            wait(pool, pre_out[q], 16 * i)
                            pool.tensor_copy(idx_now[q][:, 0:ST], src_idx[:, bass.ds(ST * b, ST)])
                            pool.tensor_copy(idx_now[q][:, ST:2 * ST], x_dst_idx[:, bass.ds(ST * b, ST)]
                                             ).then_inc(staged, 1)
                            settled(staged, 2 * BLOCKS + b + 1)
                            for j in range(2 * ST):
                                gather(got[q][:, j % ST, j // ST * D:(j // ST + 1) * D], x,
                                       idx_now[q][:, j:j + 1], pre_in[q])
                        for q in range(2):
                            b = 2 * i + q
                            pool.wait_ge(pre_in[q], 16 * 2 * ST * (i + 1))
                            pool.dma_start(own_x.rearrange("(b j p) f -> b p j f", j=ST, p=SR)[b],
                                           got[q][:, :, :]).then_inc(pre_out[q], 16)
                    ends(0)
                    with pool.Fori(1, BLOCKS // 2) as i:
                        ends(i)

            def phase(ph):
                n0 = ph * BLOCKS
                if ph == L1:
                    def load(s):
                        if at := s.block(-1):
                            b, q, half = at
                            if isinstance(b, int) and b < 2:
                                for r in range(2):
                                    pool.wait_ge(pre_out[r], 16 * BLOCKS // 2)
                            wait(pool, scale_done, b - 1)
                            pool.dma_start(got[q][:, :, :],
                                           own_x.rearrange("(b j p) f -> b p j f", j=ST, p=SR)[b]
                                           ).then_inc(got_in[q], 16)
                    phase_run(pool, load)
                    return
                table = h_tab[(ph - 1) % 2] if ph <= L5 else g_tab[ph - G1]
                index = h_idx if ph <= L5 else g_idx
                width = D if ph in GIN else H
                if ph == L2:
                    pool.wait_ge(coef_made, 1)
                for q in range(2):
                    pool.wait_ge(rows_out[q], dma_count(ROWS_OUT, ph - 1, BLOCKS // 2 - 1))
                if ph in GIN:
                    for q in range(2):
                        pool.wait_ge((y_stored, g_stored[0], g_stored[1])[ph - G1][q], 16 * PAIRS)
                if ph == G3:
                    for q in range(2):
                        pool.wait_ge(out_stored[q], 16 * PAIRS)

                def body(s):
                    if at := s.block(-1):
                        b, q, half = at
                        if ph in GIN:
                            wait(pool, turned, n0 + b - 1)
                            if ph == G1 and isinstance(b, int) and b < 2:
                                pool.wait_ge(scale_done, G1 * BLOCKS)
                        else:
                            wait(pool, scale_done, n0 + b - 1)
                        pool.tensor_copy(idx_now[q][:, 0:ST], index[:, bass.ds(ST * b, ST)]).then_inc(staged, 1)
                        settled(staged, 2 * BLOCKS + n0 + b + 1)
                        for j in range(ST):
                            gather(got[q][:, j, 0:width], table, idx_now[q][:, j:j + 1], got_in[q])
                    if ph == G3 and (at := s.block(3)):
                        b, q, half = at
                        pool.wait_ge(rows_ready, n0 + b + 1)
                        wait(pool, out_scattered[q], 16 * ST * half)
                        pool.tensor_copy(out_idx[q][:, :], scatter_idx[:, bass.ds(ST * b, ST)]).then_inc(out_staged, 1)
                        pool.wait_ge(out_stored[q], 16 * PAIRS)
                        settled(out_staged, b + 1)
                        for j in range(ST):
                            scatter(out, out_idx[q][:, j:j + 1], new_rows[q][:, j, 0:D], out_scattered[q])
                phase_run(pool, body, more=ph == G3)

            schedule(lambda k, n: None, phase, part)

        @block.tensor
        def _(pe):
            leave = Turnstile(pe, pe_left)
            pe.wait_ge(ident_set, 1)
            pe.wait_ge(weights_in, 160)
            pe.wait_ge(weights_split, 2)

            def part(what):
                k = PARTS.get(what) - 1
                if what == "flag":
                    pe.wait_ge(violations_made, 1)
                    pe.wait_ge(h_ready, 8 * k + 7)
                    pe.matmul(mm[0][1][0:1, 0:COLS], column_of_ones[:SR, :], violations[:, :],
                              start=True, stop=True).then_inc(violations_summed, 1)
                    pe.wait_ge(flag_made, 1)
                if what == "columns":
                    pe.wait_ge(rows_cast, 1)
                    pe.wait_ge(h_ready, 8 * k + 7)
                    for i in range(4):
                        last = pe.transpose(mm[0][1][:SR, i * COLS:(i + 1) * COLS], rows_f[:, i, :],
                                            ident[:SR, :SR])
                    last.then_inc(cols_t, 1)
                    pe.wait_ge(cols_done, 1)

            def turn(to, of, tiles, rows):
                for j in range(tiles):
                    last = pe.transpose(to[:, j * rows:(j + 1) * rows], of[:rows, j, :], ident[:rows, :rows])
                return last

            def turn_back(to, of, tiles, rows):
                for j in range(tiles):
                    last = pe.transpose(to[:rows, j * D:(j + 1) * D], of[:, j * rows:(j + 1) * rows], ident[:, :])
                return last

            def product(to, weights, moving, cols, begin=True, end=True):
                for i, (w, m) in enumerate(zip(weights, moving)):
                    last = pe.matmul(to[:, 0:cols], w, m, start=begin and i == 0,
                                     stop=end and i == len(weights) - 1)
                return last

            def dense(first, n):
                def body(k, v, half):
                    run = not isinstance(k, int) or k < PAIRS
                    fol = not isinstance(k, int) or k > 0
                    mine = dense_blocks(k) if run else []
                    p = k - 1
                    prev = dense_blocks(p) if fol else []

                    def layer(l):
                        for q, tiles, rows in mine:
                            c = tiles * rows
                            if l == 0:
                                pe.wait_ge(x_split, 2 * k + q + 1)
                                weights = lambda f: [w1_hi[:, f], w1_lo[:, f], w1_hi[:, f]]
                                moving = [x_hi[q][:, 0:c], x_hi[q][:, 0:c], x_lo[q][:, 0:c]]
                            else:
                                pe.wait_ge(h_ready, 8 * k + 2 * (l - 1) + q + 1)
                                w = w2_s if l < 4 else w3_s
                                weights = lambda f: [w[:, i, f] for i in range(2)]
                                moving = [h_t[q][:, i, 0:c] for i in range(2)]
                            for i in range(2 if l < 4 else 1):
                                last = product(mm[q][i], weights(slice(i * P, (i + 1) * P)), moving, c)
                            last.then_inc(layer_mm if l < 4 else y_mm, 1)

                    def split_high(l):
                        for q, tiles, rows in mine:
                            c = tiles * rows
                            pe.wait_ge(h_ready, 8 * k + 2 * (l - 1) + q + 1)
                            for i in range(2):
                                f = slice(i * P, (i + 1) * P)
                                product(mm[q][i], [w[:, r, f] for r in range(2) for w in (w2_hi, w2_lo)],
                                        [high[q][:, r, 0:c] for r in range(2) for _ in range(2)], c, end=False)

                    def split_low(l):
                        for q, tiles, rows in mine:
                            c = tiles * rows
                            pe.wait_ge(h_low, 4 * k + 2 * (l - 2) + q + 1)
                            for i in range(2):
                                last = product(mm[q][i], [w2_hi[:, r, i * P:(i + 1) * P] for r in range(2)],
                                               [low[q][:, r, 0:c] for r in range(2)], c, begin=False)
                            last.then_inc(layer_mm, 1)

                    layer(0)
                    layer(1)
                    for q, tiles, rows in prev:
                        pe.wait_ge(ln1_done, 2 * p + q + 1)
                        turn(ga[q], y_rows[q], tiles, rows).then_inc(y_turned, 1)

                    def gin(g):
                        for q, tiles, rows in prev:
                            c = tiles * rows
                            if g == 0:
                                pe.wait_ge(y_t_ready, 2 * p + q + 1)
                                moving = y_t[q][:, 0:c]
                            else:
                                pe.wait_ge(g_ready, 6 * p + 2 * (g - 1) + q + 1)
                                moving = g_t[q][(g - 1) % 2][:, 0:c]
                            product(ga[q], [wg_s[:, g, :]], [moving], c).then_inc(g_mm, 1)

                    def gin_rows(g):
                        for q, tiles, rows in prev:
                            pe.wait_ge(g_ready, 6 * p + 2 * g + q + 1)
                            if g == 0:
                                wait(pe, ln2_done, 2 * p - 1 + q)
                            else:
                                pe.wait_ge(g_rows_ready, 4 * p + 2 * (g - 1) + q + 1)
                            turn_back(tr[q], g_t[q][g % 2], tiles, rows).then_inc(g_turned, 1)

                    split_high(2)
                    gin(0)
                    split_low(2)
                    gin(1)
                    gin_rows(0)
                    split_high(3)
                    split_low(3)
                    gin(2)
                    gin_rows(1)
                    layer(4)
                    for q, tiles, rows in prev:
                        pe.wait_ge(z2_ready, 2 * p + q + 1)
                        pe.wait_ge(g_rows_ready, 4 * p + 2 + q + 1)
                        turn_back(tr[q], z2_t[q], tiles, rows).then_inc(z2_turned, 1)
                    for q, tiles, rows in mine:
                        pe.wait_ge(z_ready, 2 * k + q + 1)
                        wait(pe, u_ready, 6 * k - 1 + q)
                        turn_back(ga[q], z_t[q], tiles, rows).then_inc(z_turned, 1)
                dense_run(pe, first, n, body)

            def phase(ph):
                n0 = ph * BLOCKS

                def body(s):
                    if at := s.block(0):
                        b, q, half = at
                        n = n0 + b
                        wait(pe, scanned, n)
                        if ph in GIN:
                            pe.wait_ge(attr_in[q], dma_count(GIN_ONCE, ph, half))
                            pe.wait_ge(got_in[q], dma_count(GOT, ph, half))
                            if ph == G1:
                                pe.wait_ge(own_in[q], 16 * (half + 1))
                                wait(pe, copied, BLOCKS + b)
                                turn(ga[1], scaled[q][:, :, 0:D], ST, SR)
                            pe.matmul(ga[0][:, 0:SB], wl_s[:, ph - G1, :], attr[q][:, :], start=True, stop=False)
                            for j in range(ST):
                                last = pe.matmul(ga[0][:, j * SR:(j + 1) * SR], got[q][:, j, 0:D],
                                                 ident[:SR, :SR], start=False, stop=j == ST - 1)
                        else:
                            pe.wait_ge(scale_done, n + 1)
                            if ph == L1:
                                wait(pe, copied, b)
                            for i in range(2):
                                last = turn(ga[i], scaled[q][:, :, i * D:(i + 1) * D], ST, SR)
                        last.then_inc(turned, 1)
                    if at := s.block(1):
                        b, q, half = at
                        n = n0 + b
                        wait(pe, new_ready, n - 1)
                        if ph in GIN:
                            pe.wait_ge(summed, n - G1 * BLOCKS + 1)
                            last = product(mm[q][0], [wg_s[:, ph - G1, :]], [agg[q][:, 1, :]], SB)
                        elif ph in SPLIT:
                            pe.wait_ge(low_made, 2 * (n - L2 * BLOCKS + 1))
                            for i in range(2):
                                weights, moving = [], []
                                for high, low, at in ((state_hi[q], state_lo[q], 0), (agg_hi[q], agg_lo[q], 2)):
                                    for r in range(2):
                                        w_high, w_low = (w[:, at + r, i * P:(i + 1) * P] for w in (w2_hi, w2_lo))
                                        weights += [w_high, w_low, w_high]
                                        moving += [high[:, r, :], high[:, r, :], low[:, r, :]]
                                last = product(mm[q][i], weights, moving, SB)
                        else:
                            pe.wait_ge(scanned, n + 1)
                            if ph == L1:
                                pe.wait_ge(copied, b + 1)
                                moving, w, k = [res[q][:, :], agg[q][:, 0, :]], w1_s, 2
                            else:
                                pe.wait_ge(state_in[q], dma_count(STATE, ph, half))
                                moving = [state[q][:, 0, :], state[q][:, 1, :], agg[q][:, 0, :], agg[q][:, 1, :]]
                                w, k = (w3_s if ph == L5 else w2_s), 4
                            for i in range(1 if ph == L5 else 2):
                                last = product(mm[q][i], [w[:, r, i * P:(i + 1) * P] for r in range(k)], moving, SB)
                        last.then_inc(mm_done, 1)
                    if at := s.block(2):
                        b, q, half = at
                        n = n0 + b
                        pe.wait_ge(new_ready, n + 1)
                        wait(pe, rows_ready, n - 1 if ph == L5 else n)
                        if ph in HIDDEN:
                            turn_back(tr[0], new[q][:, 0, :], ST, SR)
                            last = turn_back(tr[1], new[q][:, 1, :], ST, SR)
                        else:
                            last = turn_back(tr[q if ph == L5 else 0], new[q][:, ph == G3, :], ST, SR)
                        last.then_inc(back_turned, 1)
                leave()
                phase_run(pe, body)

            schedule(dense, phase, part)

        @block.scalar
        def _(act):
            leave = Turnstile(act, act_left)
            act.wait_ge(weights_in, 160)

            def part(what):
                if what == "flag":
                    act.wait_ge(violations_summed, 1)
                    act.activation(flag_row[:, :], mm[0][1][0:1, 0:COLS], ACT.Copy,
                                   accum_out=flag_f[:, :]).then_inc(flag_summed, 1)
                    act.wait_ge(flag_summed, 1)
                    act.activation(flag_i[:, :], flag_f[:, :], ACT.Copy).then_inc(flag_made, 1)
                if what == "columns":
                    act.wait_ge(cols_t, 1)
                    act.activation(cols_f[:, :, :].rearrange("p a b -> p (a b)"), mm[0][1][:SR, 0:4 * COLS],
                                   ACT.Copy).then_inc(cols_done, 1)

            def dense(first, n):
                def body(k, v, half):
                    run = not isinstance(k, int) or k < PAIRS
                    fol = not isinstance(k, int) or k > 0
                    mine = dense_blocks(k) if run else []
                    p = k - 1
                    prev = dense_blocks(p) if fol else []

                    def tanh(l):
                        for q, tiles, rows in mine:
                            c = tiles * rows
                            act.wait_ge(layer_mm, 8 * k + 2 * l + q + 1)
                            for to in (h_t[q], high[q]) if l in (1, 2) else (h_t[q],):
                                for i in range(2):
                                    last = act.activation(to[:, i, 0:c], mm[q][i][:, 0:c], ACT.Tanh,
                                                          bias=(b2_s if l else b1_s)[:, i:i + 1])
                            last.then_inc(h_ready, 1)

                    def linear(g):
                        for q, tiles, rows in prev:
                            c = tiles * rows
                            act.wait_ge(g_mm, 6 * p + 2 * g + q + 1)
                            act.activation(u_t[q][:, 0:c], ga[q][:, 0:c], ACT.Identity,
                                           bias=bg_s[:, g:g + 1]).then_inc(u_ready, 1)

                    def rows_copy(g):
                        for q, tiles, rows in prev:
                            act.wait_ge(g_turned, 4 * p + 2 * g + q + 1)
                            wait(act, g_stored[g][q], 16 * p)
                            act.activation(g_rows[g][q][:rows, :tiles, :].rearrange("p j f -> p (j f)"),
                                           tr[q][:rows, 0:tiles * D], ACT.Copy).then_inc(g_rows_ready, 1)

                    tanh(0)
                    tanh(1)
                    for q, tiles, rows in prev:
                        act.wait_ge(y_turned, 2 * p + q + 1)
                        act.activation(y_t[q][:, 0:tiles * rows], ga[q][:, 0:tiles * rows],
                                       ACT.Copy).then_inc(y_t_ready, 1)
                    linear(0)
                    tanh(2)
                    linear(1)
                    rows_copy(0)
                    tanh(3)
                    linear(2)
                    rows_copy(1)
                dense_run(act, first, n, body)

            def phase(ph):
                n0 = ph * BLOCKS

                def body(s):
                    if ph in (L1, G1) and (at := s.block(0)):
                        b, q, half = at
                        act.wait_ge(turned, n0 + b + 1)
                        wait(act, res_out[q], dma_count(ONCE_L1_G1, ph, half - 1))
                        wait(act, mm_done, n0 + b - 1)
                        if ph == G1:
                            wait(act, summed, b - 1)
                        act.activation(res[q][:, :], ga[1][:, 0:SB], ACT.Copy).then_inc(copied, 1)
                    if ph in SPLIT and (at := s.block(0)):
                        b, q, half = at
                        n = n0 + b
                        act.wait_ge(state_in[q], dma_count(STATE, ph, half))
                        wait(act, mm_done, n - 1)
                        act.activation(state_hi[q], state[q][:, :, :], ACT.Copy).then_inc(state_high, 1)
                        act.wait_ge(scanned, n + 1)
                        act.activation(agg_hi[q][:, :, :], agg[q][:, :, :], ACT.Copy).then_inc(agg_high, 1)
                    if ph not in GIN and (at := s.block(-1)):
                        b, q, half = at
                        n = n0 + b
                        act.wait_ge(got_in[q], dma_count(GOT, ph, half))
                        wait(act, turned, n - 1)
                        for j in range(ST):
                            w = D if ph == L1 else H
                            last = act.activation(scaled[q][:, j, 0:w], got[q][:, j, 0:w], ACT.Copy,
                                                  scale=coef[:, bass.ds(ST * b + j, 1)])
                        if ph == L1:
                            last = act.activation(scaled[q][:, :, D:2 * D], got[q][:, :, D:2 * D], ACT.Copy)
                        last.then_inc(scale_done, 1)
                    if ph == L5 and (at := s.block(3)):
                        b, q, half = at
                        act.wait_ge(norm_made, b + 1)
                        act.wait_ge(rows_out[q], dma_count(ROWS_OUT, ph, half - 1))
                        for j in range(ST):
                            c = q * DT + j
                            last = act.activation(new_rows[q][:, j, 0:D], tr[q][:SR, j * D:(j + 1) * D], ACT.Identity,
                                                  bias=shift[:SR, c:c + 1], scale=rstd[:SR, c:c + 1])
                        last.then_inc(rows_ready, 1)
                    if ph in GIN and (at := s.block(0)):
                        b, q, half = at
                        act.wait_ge(turned, n0 + b + 1)
                        wait(act, scanned, n0 + b - 1)
                        act.activation(msg[q][:, :], ga[0][:, 0:SB], ACT.Relu).then_inc(scale_done, 1)
                    if at := s.block(1):
                        b, q, half = at
                        n = n0 + b
                        if ph in HIDDEN:
                            act.wait_ge(mm_done, n + 1)
                            wait(act, back_turned, n - 1)
                            if not (ph == L1 and isinstance(b, int) and b < 2):
                                count = (dma_count(STATE_OUT, ph, half - 1))
                                act.wait_ge(state_out[q], count)
                            for i in range(2):
                                last = act.activation(new[q][:, i, :], mm[q][i][:, 0:SB], ACT.Tanh,
                                                      bias=(b1_s if ph == L1 else b2_s)[:, i:i + 1])
                            last.then_inc(new_ready, 1)
                        elif ph in GIN:
                            act.wait_ge(mm_done, n + 1)
                            wait(act, new_ready, n - 1)
                            act.activation(lin[q][:, :], mm[q][0][:, 0:SB], ACT.Identity,
                                           bias=bg_s[:, ph - G1:ph - G1 + 1]).then_inc(lin_done, 1)
                if ph == L1:
                    act.wait_ge(coef_made, 1)
                leave()
                phase_run(act, body, more=ph == L5)

            schedule(dense, phase, part)

        @block.vector
        def _(dve):
            leave = Turnstile(dve, dve_left)
            links = [0]

            def link(instruction):
                links[0] += 1
                instruction.then_inc(dve_link, 1)
                dve.wait_ge(dve_link, links[0])

            def rsqrt(y, v, a, b, done):
                done(dve.tensor_scalar(a.bitcast(i32), v.bitcast(i32), 1, None, ALU.logical_shift_right))
                done(dve.tensor_scalar(y.bitcast(i32), a.bitcast(i32), -1.0, MAGIC, ALU.mult, ALU.add))
                for _ in range(NEWTON):
                    done(dve.scalar_tensor_tensor(out=a, in0=y, scalar=-0.5, in1=y, op0=ALU.mult, op1=ALU.mult))
                    done(dve.tensor_tensor(out=b, in0=a, in1=v, op=ALU.mult))
                    done(dve.scalar_tensor_tensor(out=y, in0=b, scalar=1.5, in1=y, op0=ALU.add, op1=ALU.mult))

            def layer_norm(blocks, link_sem, index):
                count = [index * LN_LINKS]

                def done(instruction):
                    count[0] = count[0] + 1
                    instruction.then_inc(link_sem, 1)
                    dve.wait_ge(link_sem, count[0])

                for place, tiles, rows, bank, _, arrived, _, _ in blocks:
                    arrived()
                    for j in range(tiles):
                        last = dve.bn_stats(stats[:rows, place * DT + j, :], bank[:rows, j * D:(j + 1) * D])
                done(last)
                dve.memset(ln_b[:, :], 0.0)
                for place, tiles, rows, *_ in blocks:
                    for j in range(tiles):
                        last = dve.bn_aggr(mean_var[:rows, place * DT + j, :], stats[:rows, place * DT + j, :])
                done(last)
                at = slice(min(place * DT for place, *_ in blocks),
                           max(place * DT + tiles for place, tiles, *_ in blocks))
                r = max(rows for _, _, rows, *_ in blocks)
                done(dve.tensor_scalar(rs_a[:r, at], mean_var[:r, at, 1], EPS, None, ALU.add))
                rsqrt(rstd[:r, at], rs_a[:r, at], ln_a[:r, at], ln_b[:r, at], done)
                if blocks[0][4] is None:
                    dve.scalar_tensor_tensor(out=shift[:r, at], in0=mean_var[:r, at, 0], scalar=-1.0,
                                             in1=rstd[:r, at], op0=ALU.mult, op1=ALU.mult
                                             ).then_inc(blocks[0][7], 1)
                    return
                for place, tiles, rows, bank, to, _, free, done_sem in blocks:
                    free()
                    for j in range(tiles):
                        c = place * DT + j
                        last = dve.tensor_scalar(to[:rows, j, 0:D], bank[:rows, j * D:(j + 1) * D],
                                                 mean_var[:rows, c, 0:1], rstd[:rows, c:c + 1],
                                                 ALU.subtract, ALU.mult)
                    last.then_inc(done_sem, 1)

            dve.memset(stats[:, :, :], 1.0)
            dve.memset(mean_var[:, :, :], 1.0)
            dve.memset(column_of_ones[:, :], 1.0)
            dve.wait_ge(weights_in, 160)
            for i, (w, w_hi, w_lo) in enumerate(((w1_s[:, 0, :], w1_hi[:, :], w1_lo[:, :]),
                                                 (w2_s[:, :, :], w2_hi[:, :, :], w2_lo[:, :, :]))):
                dve.tensor_copy(w_hi, w).then_inc(weights_high, 1)
                dve.wait_ge(weights_high, i + 1)
                dve.tensor_tensor(out=w_lo, in0=w, in1=w_hi.bitcast(f32), op=ALU.subtract
                                  ).then_inc(weights_split, 1)

            def runs(c):
                dve.wait_ge(chunk_in, 16 * (c + 1))
                at = slice(c * CHUNK, (c + 1) * CHUNK)
                dve.tensor_tensor(out=keep[:, at], in0=dst_chunk[:, 1:CHUNK + 1], in1=dst_chunk[:, 0:CHUNK],
                                  op=ALU.is_equal).then_inc(keep_done, 1)
                dve.wait_ge(keep_done, c + 1)
                if c >= 2:
                    dve.wait_ge(rank_out[c % 2], 16 * (c // 2))
                if c:
                    dve.wait_ge(rank_done, c)
                before = rank_row[:, (c - 1) % 2, CHUNK - 1:CHUNK] if c else 0.0
                dve.tensor_tensor_scan(rank_row[:, c % 2, :], keep[0:1, at], ones[:, :], before,
                                       ALU.mult, ALU.add).then_inc(rank_done, 1)

            def sort():
                links = [0]

                def link(instruction):
                    links[0] += 1
                    instruction.then_inc(sort_link, 1)
                    dve.wait_ge(sort_link, links[0])

                own_dst, own_place, bound, less = (tmp[:, i, :] for i in range(4))
                places = rs_a[:SR, :]
                dve.wait_ge(sort_cols_in, 64)
                dve.tensor_copy(own_dst, rows_i[:, 0, :])
                for i, of in enumerate((rows_i[:, 0, :], rows_i[:, 1, :], cols_f[:, 0, :], cols_f[:, 1, :])):
                    dve.tensor_copy(edge_cols[:, :, i], of)
                link(dve.tensor_copy(slot_f[:, :], slot_i[:, :]))
                dve.tensor_scalar(own_place, slot_f[:, :], PLACE, None, ALU.mult)
                dve.wait_ge(sort_iota, 1)
                link(dve.tensor_copy(sort_diff, sort_iota_i))
                link(dve.tensor_scalar(sort_place, sort_diff, PLACE, None, ALU.mult))
                for c in range(CHUNKS):
                    dve.wait_ge(sort_chunk_in, 16 * (c + 1))
                    dve.tensor_copy(sort_dst, dst_chunk[:SR, 0:CHUNK]).then_inc(sort_chunk_read, 1)
                    link(dve.tensor_scalar(bound, own_place, -PLACE * CHUNK * c, None, ALU.add))
                    dve.wait_ge(sort_chunk_read, c + 1)

                    def count(t):
                        wait(dve, sort_counted, t + c * COLS)
                        dve.scalar_tensor_tensor(out=sort_diff, in0=sort_dst, scalar=own_dst[:, bass.ds(t, 1)],
                                                 in1=sort_place, op0=ALU.subtract, op1=ALU.add
                                                 ).then_inc(sort_differences, 1)
                        dve.wait_ge(sort_differences, t + (c * COLS + 1))
                        dve.tensor_scalar(sort_less, sort_diff, bound[:, bass.ds(t, 1)], None, ALU.is_lt, ALU.add,
                                          accum_out=less[:, bass.ds(t, 1)]).then_inc(sort_counted, 1)
                    count(0)
                    with dve.Fori(1, COLS) as t:
                        count(t)
                    dve.wait_ge(sort_counted, (c + 1) * COLS)
                    if c:
                        link(dve.tensor_tensor(out=places, in0=places, in1=less, op=ALU.add))
                    else:
                        link(dve.tensor_copy(places, less))
                dve.tensor_copy(dst_idx[:, :], places).then_inc(sort_placed, 1)
                dve.wait_ge(sort_rows_in, 16)
                for i, to in enumerate((rows_i[:, 0, :], rows_i[:, 1, :], cols_f[:, 0, :], cols_f[:, 1, :])):
                    last = dve.tensor_copy(to, edge_rows[:, :, i])
                last.then_inc(sort_cast, 1)

            dst_c, next_c, src_c, rank_c = (cols_f[:, i, :] for i in range(4))

            def part(what):
                if what == "check":
                    dve.wait_ge(slot_made, 2)
                    link(dve.tensor_copy(init_f[:, :], init_i[:, :]))
                    dve.memset(node_init[:, :, 1], 0.0)
                    dve.tensor_copy(node_init[:, :, 0], init_f[:, 0:1].to_broadcast([P, INIT_COLS])
                                    ).then_inc(init_set, 1)
                    dve.wait_ge(rows_in, 32)
                    link(dve.tensor_copy(rows_f[:, 0:2, :], rows_i[:, 0:2, :]))
                    dve.tensor_tensor(out=violations[:, :], in0=rows_f[:, 0, :], in1=rows_f[:, 1, :],
                                      op=ALU.is_gt).then_inc(violations_made, 1)
                if what == "sort":
                    with if_unsorted(dve):
                        sort()
                if what.startswith("runs"):
                    runs(int(what[4:]))
                if what == "rows":
                    dve.wait_ge(rows_in, 96)
                    dve.tensor_copy(rows_f[:, 0:3, :], rows_i[:, :, :]).then_inc(rows_cast, 1)
                if what == "columns":
                    dve.wait_ge(cols_done, 1)
                    link(dve.tensor_copy(slot_f[:, :], slot_i[:, :]))
                    dve.tensor_scalar(tmp[:, 0, :], slot_f[:, :], float(N), None, ALU.add)
                    link(dve.tensor_tensor(out=tmp[:, 1, :], in0=next_c, in1=dst_c, op=ALU.not_equal))
                    link(dve.tensor_tensor(out=tmp[:, 2, :], in0=dst_c, in1=tmp[:, 0, :], op=ALU.subtract))
                    link(dve.tensor_tensor(out=tmp[:, 2, :], in0=tmp[:, 2, :], in1=tmp[:, 1, :], op=ALU.mult))
                    dve.tensor_tensor(out=scatter_idx[:, :], in0=tmp[:, 2, :], in1=tmp[:, 0, :], op=ALU.add)
                    dve.tensor_copy(scatter_val[:, :, 0], slot_f[:, :])
                    dve.tensor_copy(scatter_val[:, :, 1], rank_c)
                    dve.tensor_copy(dst_idx[:, :], dst_c)
                    dve.tensor_scalar(x_dst_idx[:, :], dst_c, float(N - 1), None, ALU.min)
                    dve.tensor_copy(src_idx[:, :], src_c).then_inc(index_made, 1)
                if what == "coefficients":
                    dve.wait_ge(tab_read, 2)
                    slot_s, deg_s, deg_d = of_src[:, :, 0], of_src[:, :, 1], of_dst[:, :, 1]
                    dve.tensor_copy(h_idx[:, :], slot_s)
                    dve.tensor_scalar(tmp[:, 1, :], deg_s, 0.0, None, ALU.is_gt)
                    link(dve.tensor_scalar(tmp[:, 0, :], deg_s, 1.0, None, ALU.max))
                    link(dve.scalar_tensor_tensor(out=tmp[:, 0, :], in0=deg_d, scalar=1.0, in1=tmp[:, 0, :],
                                                  op0=ALU.max, op1=ALU.mult))
                    rsqrt(tmp[:, 2, :], tmp[:, 0, :], rs_a[:SR, :], rs_b[:SR, :], link)
                    dve.scalar_tensor_tensor(out=coef[:, :], in0=tmp[:, 2, :], scalar=-1.0, in1=tmp[:, 1, :],
                                             op0=ALU.mult, op1=ALU.mult)
                    link(dve.scalar_tensor_tensor(out=tmp[:, 3, :], in0=slot_s, scalar=float(N), in1=src_c,
                                                  op0=ALU.add, op1=ALU.subtract))
                    link(dve.tensor_tensor(out=tmp[:, 3, :], in0=tmp[:, 3, :], in1=tmp[:, 1, :], op=ALU.mult))
                    dve.tensor_tensor(out=g_idx[:, :], in0=tmp[:, 3, :], in1=src_c, op=ALU.add).then_inc(coef_made, 1)

            def split_x(k, v, half):
                for q, tiles, rows in dense_blocks(k):
                    c = tiles * rows
                    dve.wait_ge(x_loaded[q][v], 16 * (half + 1))
                    wait(dve, layer_mm, 8 * (k - 1) + q + 1)
                    dve.tensor_copy(x_hi[q][:, 0:c], x_t[q][v][:, 0:c]).then_inc(x_high, 1)
                    dve.wait_ge(x_high, 2 * k + q + 1)
                    dve.tensor_tensor(out=x_lo[q][:, 0:c], in0=x_t[q][v][:, 0:c],
                                      in1=x_hi[q][:, 0:c].bitcast(f32), op=ALU.subtract).then_inc(x_split, 1)

            def dense(first, n):
                def body(k, v, half):
                    run = not isinstance(k, int) or k < PAIRS
                    fol = not isinstance(k, int) or k > 0
                    mine = dense_blocks(k) if run else []
                    p = k - 1
                    prev = dense_blocks(p) if fol else []
                    if isinstance(k, int) and k == 0:
                        split_x(0, 0, 0)
                    for g in range(3):
                        if g == 1 and (not isinstance(k, int) or k + 1 < PAIRS):
                            split_x(k + 1, 1 - v, half + v)
                        for q, tiles, rows in mine if g < 2 else []:
                            c = tiles * rows
                            dve.wait_ge(h_ready, 8 * k + 2 * (g + 1) + q + 1)
                            dve.tensor_tensor(out=low[q][:, :, 0:c], in0=h_t[q][:, :, 0:c],
                                              in1=high[q][:, :, 0:c].bitcast(f32), op=ALU.subtract
                                              ).then_inc(h_low, 1)
                        for q, tiles, rows in prev:
                            c = tiles * rows
                            dve.wait_ge(u_ready, 6 * p + 2 * g + q + 1)
                            dve.scalar_tensor_tensor(out=g_t[q][g % 2][:, 0:c], in0=u_t[q][:, 0:c], scalar=SLOPE,
                                                     in1=u_t[q][:, 0:c], op0=ALU.mult, op1=ALU.max).then_inc(g_ready, 1)
                            if g == 2:
                                dve.wait_ge(g_ready, 6 * p + 2 * g + q + 1)
                                dve.tensor_tensor(out=z2_t[q][:, 0:c], in0=g_t[q][0][:, 0:c], in1=y_t[q][:, 0:c],
                                                  op=ALU.add).then_inc(z2_ready, 1)
                    for q, tiles, rows in mine:
                        c = tiles * rows
                        dve.wait_ge(y_mm, 2 * k + q + 1)
                        dve.scalar_tensor_tensor(out=z_t[q][:, 0:c], in0=mm[q][0][:, 0:c], scalar=b3_s[:, 0:1],
                                                 in1=x_t[q][v][:, 0:c], op0=ALU.add, op1=ALU.add).then_inc(z_ready, 1)
                    layer_norm(
                        [(q, t, r, ga[q], y_rows[q], lambda q=q: dve.wait_ge(z_turned, 2 * k + q + 1),
                          lambda q=q: wait(dve, y_stored[q], 16 * k), ln1_done) for q, t, r in mine]
                        + [(2 + q, t, r, tr[q], out_rows[q], lambda q=q: dve.wait_ge(z2_turned, 2 * p + q + 1),
                            lambda q=q: wait(dve, out_stored[q], 16 * p), ln2_done) for q, t, r in prev],
                        ln_dense_link, k)
                dense_run(dve, first, n, body)

            def phase(ph):
                n0 = ph * BLOCKS

                def body(s):
                    if at := s.block(0):
                        b, q, half = at
                        n = n0 + b
                        if ph in GIN:
                            dve.wait_ge(scale_done, n + 1)
                        else:
                            dve.wait_ge(turned, n + 1)
                        wait(dve, mm_done, n - 1)
                        wait(dve, scanned, n)
                        for i in range(2 if L1 < ph <= L5 else 1):
                            last = dve.tensor_tensor_scan(
                                agg[q][:, i, :], keep[:, bass.ds(SB * b, SB)],
                                msg[q][:, :] if ph in GIN else ga[i][:, 0:SB],
                                agg[1 - q][:, i, SB - 1:SB], ALU.mult, ALU.add)
                        last.then_inc(scanned, 1)
                        if ph in SPLIT:
                            m = n - L2 * BLOCKS
                            dve.wait_ge(state_high, m + 1)
                            dve.tensor_tensor(out=state_lo[q], in0=state[q][:, :, :], in1=state_hi[q].bitcast(f32),
                                              op=ALU.subtract).then_inc(low_made, 1)
                            dve.wait_ge(agg_high, m + 1)
                            dve.tensor_tensor(out=agg_lo[q][:, :, :], in0=agg[q][:, :, :],
                                              in1=agg_hi[q][:, :, :].bitcast(f32), op=ALU.subtract
                                              ).then_inc(low_made, 1)
                        if ph in GIN:
                            dve.wait_ge(scanned, n + 1)
                            if ph == G1:
                                dve.wait_ge(copied, BLOCKS + b + 1)
                            else:
                                dve.wait_ge(state_in[q], dma_count(STATE, ph, half))
                            own = res[q][:, :] if ph == G1 else state[q][:, 0, :]
                            dve.tensor_tensor(out=agg[q][:, 1, :], in0=agg[q][:, 0, :], in1=own,
                                              op=ALU.add).then_inc(summed, 1)
                    if at := s.block(1):
                        b, q, half = at
                        n = n0 + b
                        if ph == L5:
                            dve.wait_ge(mm_done, n + 1)
                            dve.wait_ge(res_in[q], dma_count(RES, ph, half))
                            wait(dve, back_turned, n - 1)
                            if isinstance(b, int) and b < 2:
                                dve.wait_ge(state_out[q], dma_count(STATE_OUT, L4, BLOCKS // 2 - 1))
                            dve.scalar_tensor_tensor(out=new[q][:, 0, :], in0=mm[q][0][:, 0:SB], scalar=b3_s[:, 0:1],
                                                     in1=res[q][:, :], op0=ALU.add, op1=ALU.add).then_inc(new_ready, 1)
                        elif ph in GIN:
                            dve.wait_ge(lin_done, n - G1 * BLOCKS + 1)
                            wait(dve, back_turned, n - 1)
                            if ph in STATE_OUT:
                                count = dma_count(STATE_OUT, ph, half - 1)
                            else:
                                count = dma_count(STATE_OUT, G2, BLOCKS // 2 - 1)
                            if ph in STATE_OUT or (isinstance(b, int) and b < 2):
                                dve.wait_ge(state_out[q], count)
                            last = dve.scalar_tensor_tensor(out=new[q][:, 0, :], in0=lin[q][:, :], scalar=SLOPE,
                                                            in1=lin[q][:, :], op0=ALU.mult, op1=ALU.max)
                            if ph == G3:
                                last.then_inc(new_half, 1)
                                dve.wait_ge(new_half, b + 1)
                                dve.wait_ge(res_in[q], dma_count(RES, ph, half))
                                last = dve.tensor_tensor(out=new[q][:, 1, :], in0=new[q][:, 0, :],
                                                         in1=res[q][:, :], op=ALU.add)
                            last.then_inc(new_ready, 1)
                    if at := s.block(2):
                        b, q, half = at
                        n = n0 + b
                        def free():
                            if ph == G3:
                                if isinstance(b, int) and b < 2:
                                    dve.wait_ge(rows_out[q], dma_count(ROWS_OUT, G2, BLOCKS // 2 - 1))
                                else:
                                    dve.wait_ge(out_scattered[q], 16 * ST * half)
                            else:
                                wait(dve, rows_out[q], dma_count(ROWS_OUT, ph, half - 1))
                                if ph == L1 and isinstance(b, int) and b < 2:
                                    for g in range(2):
                                        dve.wait_ge(g_stored[g][q], 16 * PAIRS)
                        if ph == L5:
                            wait(dve, rows_ready, n - 1)
                            layer_norm([(q, ST, SR, tr[q], None, lambda: dve.wait_ge(back_turned, n + 1),
                                         None, norm_made)], ln_slot_link, b)
                        elif ph == G3:
                            layer_norm([(0, ST, SR, tr[0], new_rows[q], lambda: dve.wait_ge(back_turned, n + 1),
                                         free, rows_ready)], ln_slot_link, b + BLOCKS)
                        else:
                            dve.wait_ge(back_turned, n + 1)
                            free()
                            for i in range(2 if ph in HIDDEN else 1):
                                last = dve.tensor_copy(
                                    new_rows[q][:, :, i * D:(i + 1) * D],
                                    tr[i][:SR, 0:ST * D].rearrange("p (j f) -> p j f", f=D))
                            last.then_inc(rows_ready, 1)
                leave()
                if ph == L1:
                    for t in agg:
                        last = dve.memset(t[:, :, :], 0.0)
                    last.then_inc(agg_zero, 1)
                    dve.wait_ge(agg_zero, 1)
                phase_run(dve, body)

            schedule(dense, phase, part)


def kernel(x, src, dst, edge_attr_2, L0_gnn_W1, L0_gnn_b1, L0_gnn_W2, L0_gnn_b2, L0_gnn_W3, L0_gnn_b3,
           L1_gnn_Wl, L1_gnn_bl, L1_gnn_W, L1_gnn_b):
    import numpy as np
    import concourse.bacc as bacc
    from concourse import mybir as mb
    from concourse.bass_utils import run_bass_kernel_spmd

    nc = bacc.Bacc("TRN2", target_bir_lowering=False, num_devices=1)
    given = {
        "x": x, "x_turned": np.asarray(x).T, "src": src, "dst": dst, "attr_t": np.asarray(edge_attr_2).T,
        "w1": L0_gnn_W1, "b1": L0_gnn_b1, "w2": L0_gnn_W2, "b2": L0_gnn_b2, "w3": L0_gnn_W3, "b3": L0_gnn_b3,
        "wl": L1_gnn_Wl, "bl": L1_gnn_bl, "wg": L1_gnn_W, "bg": L1_gnn_b,
    }
    arrays, args = {}, []
    for name, a in given.items():
        a = np.ascontiguousarray(a)
        arrays[f"in_{name}"] = a
        args.append(nc.dram_tensor(f"in_{name}", a.shape, mb.dt.from_np(a.dtype), kind="ExternalInput").ap())
    args.append(nc.dram_tensor("out_x", (TAB_ROWS, D), mb.dt.float32, kind="ExternalOutput").ap())
    gnn_kernel(nc, *args)
    r = run_bass_kernel_spmd(nc, [arrays], core_ids=[0])
    return r.results[0]["out_x"][:N]
```
